# Optimizing a Trainium2 kernel written in Bass

```python
import numpy as np
import jax
import jax.numpy as jnp

def _softmax(x, axis=-1):
    return jax.nn.softmax(x, axis=axis)

def _gelu(x):
    return jax.nn.gelu(x, approximate=True)

def _silu(x):
    return jax.nn.silu(x)

def _sigmoid(x):
    return jax.nn.sigmoid(x)

def _layernorm(x, axis=-1, eps=1e-05):
    m = jnp.mean(x, axis=axis, keepdims=True)
    v = jnp.var(x, axis=axis, keepdims=True)
    return (x - m) / jnp.sqrt(v + eps)

def _scatter_add(tgt, idx, src, axis=0):
    return tgt.at[idx].add(src)

def _segment_sum(src, seg, n):
    return jax.ops.segment_sum(src, seg, n)
kernel_name = 'mk_seq_preln_d2_jaxref_r8_6e454f'

def setup_inputs(seed: int=0):
    np.random.seed(seed)
    _w = jnp.asarray

    def _L0_attn_setup():
        import jax, jax.numpy as jnp
        import numpy as np
        D_MODEL = 128
        NUM_HEADS = 16
        HEAD_DIM = D_MODEL // NUM_HEADS
        D_FF = 512
        EPS = 1e-05

        def layer_norm(x, gamma, beta):
            mu = jnp.mean(x, axis=-1, keepdims=True)
            var = jnp.mean((x - mu) ** 2, axis=-1, keepdims=True)
            return (x - mu) * jax.lax.rsqrt(var + EPS) * gamma + beta

        def apply_rope(t):
            S, d = (t.shape[-2], t.shape[-1])
            inv_freq = 1.0 / 10000.0 ** (jnp.arange(0, d, 2, dtype=jnp.float32) / d)
            angles = jnp.arange(S, dtype=jnp.float32)[:, None] * inv_freq[None, :]
            sin, cos = (jnp.sin(angles), jnp.cos(angles))
            tp = t.reshape(*t.shape[:-1], d // 2, 2)
            t0, t1 = (tp[..., 0], tp[..., 1])
            rot = jnp.stack([t0 * cos - t1 * sin, t0 * sin + t1 * cos], axis=-1)
            return rot.reshape(t.shape)
        key = jax.random.key(seed)
        ks = jax.random.split(key, 18)
        s = 0.02
        d, f = (D_MODEL, D_FF)
        return {'x': jax.random.normal(ks[0], (2, 256, d), dtype=jnp.float32), 'Wq': jax.random.normal(ks[1], (d, d), dtype=jnp.float32) * s, 'bq': jnp.zeros((d,), jnp.float32), 'Wk': jax.random.normal(ks[2], (d, d), dtype=jnp.float32) * s, 'bk': jnp.zeros((d,), jnp.float32), 'Wv': jax.random.normal(ks[3], (d, d), dtype=jnp.float32) * s, 'bv': jnp.zeros((d,), jnp.float32), 'Wo': jax.random.normal(ks[4], (d, d), dtype=jnp.float32) * s, 'bo': jnp.zeros((d,), jnp.float32), 'W1': jax.random.normal(ks[5], (d, f), dtype=jnp.float32) * s, 'b1': jnp.zeros((f,), jnp.float32), 'W2': jax.random.normal(ks[6], (f, d), dtype=jnp.float32) * s, 'b2': jnp.zeros((d,), jnp.float32), 'g1': jnp.ones((d,), jnp.float32), 'beta1': jnp.zeros((d,), jnp.float32), 'g2': jnp.ones((d,), jnp.float32), 'beta2': jnp.zeros((d,), jnp.float32)}
    _L0_attn_in = _L0_attn_setup()

    def _L0_ffn_setup():
        import jax, jax.numpy as jnp
        import numpy as np
        D_MODEL = 128
        D_HIDDEN = 512
        NUM_BANKS = 16
        NUM_SELECTED = 2
        key = jax.random.key(seed)
        ks = jax.random.split(key, 7)
        s = 0.02
        return {'tensor': jax.random.normal(ks[0], (4, 128, D_MODEL), dtype=jnp.float32), 'Wr': jax.random.normal(ks[1], (D_MODEL, NUM_BANKS), dtype=jnp.float32) * s, 'br': jnp.zeros((NUM_BANKS,), dtype=jnp.float32), 'W1': jax.random.normal(ks[2], (NUM_BANKS, D_MODEL, D_HIDDEN), dtype=jnp.float32) * s, 'b1': jnp.zeros((NUM_BANKS, D_HIDDEN), dtype=jnp.float32), 'W2': jax.random.normal(ks[3], (NUM_BANKS, D_HIDDEN, D_MODEL), dtype=jnp.float32) * s, 'b2': jnp.zeros((NUM_BANKS, D_MODEL), dtype=jnp.float32)}
    _L0_ffn_in = _L0_ffn_setup()

    def _L1_attn_setup():
        import jax, jax.numpy as jnp
        import numpy as np
        _J6 = jnp.array([[0, 0, 0, 0, 0, 1], [0, 0, 0, 0, -1, 0], [0, 0, 0, 1, 0, 0], [0, 0, 1, 0, 0, 0], [0, -1, 0, 0, 0, 0], [1, 0, 0, 0, 0, 0]], dtype=jnp.float32)
        _PI = jnp.array([0, 0, 0, 1, 1, 2])
        _PJ = jnp.array([1, 2, 3, 2, 3, 3])

        def exterior(p1, p2):
            L = p1[..., _PI] * p2[..., _PJ] - p1[..., _PJ] * p2[..., _PI]
            n = jnp.clip(jnp.linalg.norm(L, axis=-1, keepdims=True), 1e-12)
            return L / n
        key = jax.random.key(seed)
        ks = jax.random.split(key, 8)
        B, T, D, H = (2, 256, 128, 16)
        pd = 4
        s = 0.02
        return {'x': jax.random.normal(ks[0], (B, T, D), jnp.float32), 'w_qkv': jax.random.normal(ks[1], (3 * D, D), jnp.float32) * s, 'b_qkv': jnp.zeros((3 * D,), jnp.float32), 'w1_write': jax.random.normal(ks[2], (pd * H, D), jnp.float32) * s, 'w2_write': jax.random.normal(ks[3], (pd * H, D), jnp.float32) * s, 'w1_read': jax.random.normal(ks[4], (pd * H, D), jnp.float32) * s, 'w2_read': jax.random.normal(ks[5], (pd * H, D), jnp.float32) * s, 'w_out': jax.random.normal(ks[6], (D, D), jnp.float32) * s, 'b_out': jnp.zeros((D,), jnp.float32), 'decay_logits': jnp.full((H,), 4.6, jnp.float32), 'bias_scale': jnp.full((H,), 0.1, jnp.float32)}
    _L1_attn_in = _L1_attn_setup()

    def _L1_ffn_setup():
        import jax, jax.numpy as jnp
        import numpy as np
        TOP_K = 2
        key = jax.random.key(seed)
        ks = jax.random.split(key, 6)
        B, T, H, E, F = (2, 256, 128, 8, 512)
        s = 0.02
        return {'hidden_states': jax.random.normal(ks[0], (B, T, H), dtype=jnp.float32), 'router_w': jax.random.normal(ks[1], (E, H), dtype=jnp.float32) * s, 'w1': jax.random.normal(ks[2], (E, F, H), dtype=jnp.float32) * s, 'b1': jax.random.normal(ks[3], (E, F), dtype=jnp.float32) * s, 'w2': jax.random.normal(ks[4], (E, H, F), dtype=jnp.float32) * s, 'b2': jax.random.normal(ks[5], (E, H), dtype=jnp.float32) * s}
    _L1_ffn_in = _L1_ffn_setup()
    _d = {'L0_attn_x': _L0_attn_in['x'], 'L0_attn_Wq': _L0_attn_in['Wq'], 'L0_attn_bq': _L0_attn_in['bq'], 'L0_attn_Wk': _L0_attn_in['Wk'], 'L0_attn_bk': _L0_attn_in['bk'], 'L0_attn_Wv': _L0_attn_in['Wv'], 'L0_attn_bv': _L0_attn_in['bv'], 'L0_attn_Wo': _L0_attn_in['Wo'], 'L0_attn_bo': _L0_attn_in['bo'], 'L0_attn_W1': _L0_attn_in['W1'], 'L0_attn_b1': _L0_attn_in['b1'], 'L0_attn_W2': _L0_attn_in['W2'], 'L0_attn_b2': _L0_attn_in['b2'], 'L0_attn_g1': _L0_attn_in['g1'], 'L0_attn_beta1': _L0_attn_in['beta1'], 'L0_attn_g2': _L0_attn_in['g2'], 'L0_attn_beta2': _L0_attn_in['beta2'], 'L0_ffn_Wr': _L0_ffn_in['Wr'], 'L0_ffn_br': _L0_ffn_in['br'], 'L0_ffn_W1': _L0_ffn_in['W1'], 'L0_ffn_b1': _L0_ffn_in['b1'], 'L0_ffn_W2': _L0_ffn_in['W2'], 'L0_ffn_b2': _L0_ffn_in['b2'], 'L1_attn_w_qkv': _L1_attn_in['w_qkv'], 'L1_attn_b_qkv': _L1_attn_in['b_qkv'], 'L1_attn_w1_write': _L1_attn_in['w1_write'], 'L1_attn_w2_write': _L1_attn_in['w2_write'], 'L1_attn_w1_read': _L1_attn_in['w1_read'], 'L1_attn_w2_read': _L1_attn_in['w2_read'], 'L1_attn_w_out': _L1_attn_in['w_out'], 'L1_attn_b_out': _L1_attn_in['b_out'], 'L1_attn_decay_logits': _L1_attn_in['decay_logits'], 'L1_attn_bias_scale': _L1_attn_in['bias_scale'], 'L1_ffn_router_w': _L1_ffn_in['router_w'], 'L1_ffn_w1': _L1_ffn_in['w1'], 'L1_ffn_b1': _L1_ffn_in['b1'], 'L1_ffn_w2': _L1_ffn_in['w2'], 'L1_ffn_b2': _L1_ffn_in['b2']}
    _x0 = _d['L0_attn_x']
    _d['L0_attn_x'] = jax.random.normal(jax.random.fold_in(jax.random.key(seed), 1), (8, 512, 128), dtype=_x0.dtype)
    del _x0
    return _d

def reference(L0_attn_x, L0_attn_Wq, L0_attn_bq, L0_attn_Wk, L0_attn_bk, L0_attn_Wv, L0_attn_bv, L0_attn_Wo, L0_attn_bo, L0_attn_W1, L0_attn_b1, L0_attn_W2, L0_attn_b2, L0_attn_g1, L0_attn_beta1, L0_attn_g2, L0_attn_beta2, L0_ffn_Wr, L0_ffn_br, L0_ffn_W1, L0_ffn_b1, L0_ffn_W2, L0_ffn_b2, L1_attn_w_qkv, L1_attn_b_qkv, L1_attn_w1_write, L1_attn_w2_write, L1_attn_w1_read, L1_attn_w2_read, L1_attn_w_out, L1_attn_b_out, L1_attn_decay_logits, L1_attn_bias_scale, L1_ffn_router_w, L1_ffn_w1, L1_ffn_b1, L1_ffn_w2, L1_ffn_b2):

    def _L0_attn_ref(x, Wq, bq, Wk, bk, Wv, bv, Wo, bo, W1, b1, W2, b2, g1, beta1, g2, beta2):
        import jax, jax.numpy as jnp
        import numpy as np
        D_MODEL = 128
        NUM_HEADS = 16
        HEAD_DIM = D_MODEL // NUM_HEADS
        D_FF = 512
        EPS = 1e-05

        def layer_norm(x, gamma, beta):
            mu = jnp.mean(x, axis=-1, keepdims=True)
            var = jnp.mean((x - mu) ** 2, axis=-1, keepdims=True)
            return (x - mu) * jax.lax.rsqrt(var + EPS) * gamma + beta

        def apply_rope(t):
            S, d = (t.shape[-2], t.shape[-1])
            inv_freq = 1.0 / 10000.0 ** (jnp.arange(0, d, 2, dtype=jnp.float32) / d)
            angles = jnp.arange(S, dtype=jnp.float32)[:, None] * inv_freq[None, :]
            sin, cos = (jnp.sin(angles), jnp.cos(angles))
            tp = t.reshape(*t.shape[:-1], d // 2, 2)
            t0, t1 = (tp[..., 0], tp[..., 1])
            rot = jnp.stack([t0 * cos - t1 * sin, t0 * sin + t1 * cos], axis=-1)
            return rot.reshape(t.shape)
        B, S, d = x.shape
        H, hd = (NUM_HEADS, HEAD_DIM)
        x_norm = layer_norm(x, g1, beta1)
        q = (x_norm @ Wq + bq).reshape(B, S, H, hd).transpose(0, 2, 1, 3)
        k = (x_norm @ Wk + bk).reshape(B, S, H, hd).transpose(0, 2, 1, 3)
        v = (x_norm @ Wv + bv).reshape(B, S, H, hd).transpose(0, 2, 1, 3)
        q = apply_rope(q)
        k = apply_rope(k)
        q = q * (1.0 / jnp.sqrt(jnp.float32(hd)))
        scores = jnp.einsum('bhqd,bhkd->bhqk', q, k)
        attn = jax.nn.softmax(scores, axis=-1)
        out = jnp.einsum('bhqk,bhkd->bhqd', attn, v)
        out = out.transpose(0, 2, 1, 3).reshape(B, S, d)
        attn_out = out @ Wo + bo
        x = x + attn_out
        x_norm2 = layer_norm(x, g2, beta2)
        ffn = jax.nn.relu(x_norm2 @ W1 + b1) @ W2 + b2
        return x + ffn

    def _L0_ffn_ref(tensor, Wr, br, W1, b1, W2, b2):
        import jax, jax.numpy as jnp
        import numpy as np
        D_MODEL = 128
        D_HIDDEN = 512
        NUM_BANKS = 16
        NUM_SELECTED = 2
        logits = jnp.einsum('bsd,de->bse', tensor, Wr) + br
        probs = jax.nn.softmax(logits, axis=-1)
        topv, topi = jax.lax.top_k(probs, NUM_SELECTED)
        gate = jnp.sum(jax.nn.one_hot(topi, NUM_BANKS, dtype=tensor.dtype) * topv[..., None], axis=-2)
        h = jax.nn.relu(jnp.einsum('bsd,edh->bseh', tensor, W1) + b1)
        y = jnp.einsum('bseh,ehm->bsem', h, W2) + b2
        out = jnp.einsum('bse,bsem->bsm', gate, y)
        return out

    def _L1_attn_ref(x, w_qkv, b_qkv, w1_write, w2_write, w1_read, w2_read, w_out, b_out, decay_logits, bias_scale):
        import jax, jax.numpy as jnp
        import numpy as np
        _J6 = jnp.array([[0, 0, 0, 0, 0, 1], [0, 0, 0, 0, -1, 0], [0, 0, 0, 1, 0, 0], [0, 0, 1, 0, 0, 0], [0, -1, 0, 0, 0, 0], [1, 0, 0, 0, 0, 0]], dtype=jnp.float32)
        _PI = jnp.array([0, 0, 0, 1, 1, 2])
        _PJ = jnp.array([1, 2, 3, 2, 3, 3])

        def exterior(p1, p2):
            L = p1[..., _PI] * p2[..., _PJ] - p1[..., _PJ] * p2[..., _PI]
            n = jnp.clip(jnp.linalg.norm(L, axis=-1, keepdims=True), 1e-12)
            return L / n
        B, T, D = x.shape
        H = decay_logits.shape[0]
        dh = D // H
        pd = w1_write.shape[0] // H
        scale = dh ** (-0.5)
        qkv = (x @ w_qkv.T + b_qkv).reshape(B, T, 3, H, dh)
        qkv = jnp.transpose(qkv, (2, 0, 3, 1, 4))
        q, k, v = (qkv[0], qkv[1], qkv[2])
        std_logits = jnp.einsum('bhqd,bhkd->bhqk', q, k) * scale
        x_prev = jnp.concatenate([jnp.zeros((B, 1, D), x.dtype), x[:, :-1]], axis=1)
        w1 = (x_prev @ w1_write.T).reshape(B, T, H, pd)
        w2 = (x @ w2_write.T).reshape(B, T, H, pd)
        write_lines = exterior(w1, w2)
        r1 = (x @ w1_read.T).reshape(B, T, H, pd)
        r2 = (x @ w2_read.T).reshape(B, T, H, pd)
        read_lines = exterior(r1, r2)
        J_write = jnp.einsum('bthi,ij->bthj', write_lines, _J6)
        incidence = jnp.einsum('bqhp,bkhp->bhqk', read_lines, J_write)
        decays = jax.nn.sigmoid(decay_logits)
        pos = jnp.arange(T, dtype=x.dtype)
        diffs = pos[:, None] - pos[None, :]
        past = diffs > 0
        diffs_pos = jnp.where(past, diffs, 0.0)
        weights = decays[:, None, None] ** diffs_pos[None] * past[None].astype(x.dtype)
        bias = incidence * weights[None] * bias_scale[None, :, None, None]
        logits = std_logits + bias
        causal_mask = diffs < 0
        logits = jnp.where(causal_mask[None, None], -jnp.inf, logits)
        attn = jax.nn.softmax(logits, axis=-1)
        out = jnp.einsum('bhqk,bhkd->bqhd', attn, v).reshape(B, T, D)
        return out @ w_out.T + b_out

    def _L1_ffn_ref(hidden_states, router_w, w1, b1, w2, b2):
        import jax, jax.numpy as jnp
        import numpy as np
        TOP_K = 2
        x = hidden_states
        router_logits = jnp.einsum('bth,eh->bte', x, router_w)
        topk_values, topk_indices = jax.lax.top_k(router_logits, TOP_K)
        topk_weights = jax.nn.softmax(topk_values.astype(jnp.float32), axis=-1).astype(x.dtype)
        h1 = jnp.einsum('bth,efh->btef', x, w1) + b1
        h1 = jax.nn.gelu(h1, approximate=False)
        expert_outputs = jnp.einsum('btef,ehf->bteh', h1, w2) + b2
        gather_idx = topk_indices[..., None]
        topk_expert_outputs = jnp.take_along_axis(expert_outputs, gather_idx, axis=2)
        mixed_output = jnp.sum(topk_expert_outputs * topk_weights[..., None], axis=2)
        return mixed_output
    x = L0_attn_x
    x = x + _L0_attn_ref(_layernorm(x, axis=-1), L0_attn_Wq, L0_attn_bq, L0_attn_Wk, L0_attn_bk, L0_attn_Wv, L0_attn_bv, L0_attn_Wo, L0_attn_bo, L0_attn_W1, L0_attn_b1, L0_attn_W2, L0_attn_b2, L0_attn_g1, L0_attn_beta1, L0_attn_g2, L0_attn_beta2)
    x = x + _L0_ffn_ref(_layernorm(x, axis=-1), L0_ffn_Wr, L0_ffn_br, L0_ffn_W1, L0_ffn_b1, L0_ffn_W2, L0_ffn_b2)
    x = x + _L1_attn_ref(_layernorm(x, axis=-1), L1_attn_w_qkv, L1_attn_b_qkv, L1_attn_w1_write, L1_attn_w2_write, L1_attn_w1_read, L1_attn_w2_read, L1_attn_w_out, L1_attn_b_out, L1_attn_decay_logits, L1_attn_bias_scale)
    x = x + _L1_ffn_ref(_layernorm(x, axis=-1), L1_ffn_router_w, L1_ffn_w1, L1_ffn_b1, L1_ffn_w2, L1_ffn_b2)
    return x

_drawn_inputs = setup_inputs


def setup_inputs(seed=0):
    import zlib

    import numpy as np

    out = dict(_drawn_inputs(seed))
    spreads = {'L0_attn_bq': (0.0, 0.8),
     'L0_attn_bk': (0.0, 0.8),
     'L0_attn_bv': (0.0, 0.729),
     'L0_attn_bo': (0.0, 0.1),
     'L0_attn_b1': (0.0, 0.517),
     'L0_attn_b2': (0.0, 0.1),
     'L0_attn_g1': (1.0, 0.6),
     'L0_attn_beta1': (0.0, 0.8),
     'L0_attn_g2': (1.0, 0.6),
     'L0_attn_beta2': (0.0, 0.8),
     'L0_ffn_br': (0.0, 0.8),
     'L0_ffn_b1': (0.0, 0.8),
     'L0_ffn_b2': (0.0, 0.8),
     'L1_attn_b_qkv': (0.0, 0.731),
     'L1_attn_b_out': (0.0, 0.375),
     'L1_attn_decay_logits': (4.599999904632568, 0.6),
     'L1_attn_bias_scale': (0.10000000149011612, 0.6)}
    factors = {'L0_attn_Wq': 8.0,
     'L0_attn_Wk': 8.0,
     'L0_attn_Wv': 8.0,
     'L0_attn_Wo': 5.591,
     'L0_ffn_Wr': 7.529,
     'L0_ffn_W1': 8.0,
     'L0_ffn_W2': 8.0,
     'L1_attn_w_qkv': 8.0,
     'L1_attn_w1_write': 64.0,
     'L1_attn_w2_write': 64.0,
     'L1_attn_w1_read': 64.0,
     'L1_attn_w2_read': 64.0,
     'L1_attn_w_out': 4.554,
     'L1_ffn_router_w': 3.199,
     'L1_ffn_w1': 3.039,
     'L1_ffn_b1': 23.017,
     'L1_ffn_w2': 2.984,
     'L1_ffn_b2': 7.796}
    for name, (base, spread) in spreads.items():
        noise = np.random.default_rng([zlib.crc32(name.encode()), seed]).standard_normal(out[name].shape)
        drawn = base * np.exp(spread * noise) if base else spread * noise
        out[name] = jnp.asarray(drawn.astype(out[name].dtype))
    for name, factor in factors.items():
        out[name] = (out[name] * factor).astype(out[name].dtype)
    return out
```

```python
from contextlib import ExitStack

import numpy as np

import concourse.bass as bass
from concourse import mybir

F32 = mybir.dt.float32
BF16 = mybir.dt.bfloat16
ALU = mybir.AluOpType
ACT = mybir.ActivationFunctionType
AX_X = mybir.AxisListType.X

P = 128
D = 128
B, S = 8, 512
T = S // P
H = 16
HD = D // H
QUAD = 4
F = 512
FC = F // P
E0, E1 = 16, 8
EPS = 1e-5
PARTS = 3
PAIRS = PARTS * PARTS
STACK = PAIRS * HD
KR0 = 96


def sem(signal):
    return signal[0]


def per_turn(signal):
    return signal[1]


def turn(signal, i, n):
    return signal[0], i * signal[1] + (n + 1)


def prime(pool, signals):
    for s in signals:
        pool.sem_inc(sem(s), 1)


def widen(ap, n):
    k = len(ap.shape)
    return ap.unsqueeze(k).to_broadcast(list(ap.shape) + [n])


def build(nc, ins, out, phases="ABCD"):
    ctx = ExitStack()
    with ctx:
        def sb(name, shape, dt=F32):
            return ctx.enter_context(nc.sbuf_tensor(name, shape, dt))

        def dram(name, shape, dt):
            return nc.dram_tensor(name, shape, dt).ap()

        X = sb("X", [P, B * T, D])
        ident = sb("ident", [P, P])
        half = sb("half", [P, T])
        eps = sb("eps", [P, T])
        pad = sb("pad", [P, 1])
        XN = sb("XN", [P, T, D])
        YN = sb("YN", [P, T, D])
        YT = sb("YT", [P, S])
        stat = sb("stat", [P, T, 6])
        mv = sb("mv", [P, T, 2])
        ve = sb("ve", [P, T])
        rstd = sb("rstd", [P, T])
        common = dict(X=X, ident=ident, half=half, eps=eps, pad=pad, XN=XN, YN=YN, YT=YT, stat=stat, mv=mv, ve=ve, rstd=rstd)

        load_inputs(nc, ins, common)
        if "A" in phases:
            layer0_attention(nc, ins, common)
        if "B" in phases:
            experts(nc, ins, common, "L0", E0)
        if "C" in phases:
            layer1_attention(nc, ins, common)
        if "D" in phases:
            experts(nc, ins, common, "L1", E1)

        with nc.semaphore("stored") as stored, nc.Block() as block:
            @block.sync
            def _(sp):
                sp.dma_start(out.rearrange("(n p) d -> p n d", p=P), X[:, :, :]).then_inc(stored, 16)
                sp.wait_ge(stored, 16)


def load_inputs(nc, ins, c):
    with nc.semaphore("loaded") as loaded, nc.semaphore("made") as made, nc.Block() as block:
        @block.sync
        def _(sp):
            sp.dma_start(c["X"][:, :, :], ins["x"].rearrange("(n p) d -> p n d", p=P)).then_inc(loaded, 16)
            sp.wait_ge(loaded, 16)

        @block.gpsimd
        def _(pool):
            pool.memset(c["ident"][:, :], 0.0).then_inc(made, 1)
            pool.memset(c["half"][:, :], -0.5)
            pool.memset(c["eps"][:, :], EPS)
            pool.wait_ge(made, 1)
            pool.affine_select(out=c["ident"][:, :], in_=c["ident"][:, :], compare_op=ALU.not_equal, fill=1.0,
                               base=0, pattern=[[-1, P]], channel_multiplier=1)


def spread(rows):
    return rows[:, :].unsqueeze(1).to_broadcast([rows.shape[0], H, S])


def norm_signals(sig, per):
    return {"stats": sig("norm_stats", T * per), "mean": sig("norm_mean", T * per),
            "eps_added": sig("norm_eps_added", per), "rstd": sig("norm_rstd", per), "out": sig("norm_out", T * per)}


def norm_measure(dve, c, norm, i, j, src):
    if j > 0:
        dve.wait_ge(*turn(norm["out"], i, j * T))
    for t in range(T):
        dve.bn_stats(c["stat"][:, t, :], src(t)).then_inc(sem(norm["stats"]), 1)
    dve.wait_ge(*turn(norm["stats"], i, (j + 1) * T))
    dve.memset(c["pad"][:, :], 0.0)
    for t in range(T):
        dve.bn_aggr(c["mv"][:, t, :], c["stat"][:, t, :]).then_inc(sem(norm["mean"]), 1)


def norm_root(pool, c, norm, i, j):
    pool.wait_ge(*turn(norm["mean"], i, (j + 1) * T))
    pool.tensor_tensor(c["ve"][:, :], c["mv"][:, :, 1], c["eps"][:, :], ALU.add).then_inc(sem(norm["eps_added"]), 1)
    pool.wait_ge(*turn(norm["eps_added"], i, j + 1))
    pool.tensor_tensor(c["rstd"][:, :], c["ve"][:, :], c["half"][:, :], ALU.pow).then_inc(sem(norm["rstd"]), 1)


def norm_scale(dve, c, norm, i, j, dst, src):
    dve.wait_ge(*turn(norm["rstd"], i, j + 1))
    for t in range(T):
        dve.tensor_scalar(dst(t), src(t), c["mv"][:, t, 0:1], c["rstd"][:, t:t + 1],
                          ALU.subtract, ALU.mult).then_inc(sem(norm["out"]), 1)


def norm_wait(eng, norm, i, j):
    eng.wait_ge(*turn(norm["out"], i, (j + 1) * T))


def layer0_attention(nc, ins, c):
    with ExitStack() as ctx:
        def sb(name, shape, dt=F32):
            return ctx.enter_context(nc.sbuf_tensor(name, shape, dt))

        signals = []

        def sig(name, per=1):
            signals.append((ctx.enter_context(nc.semaphore(f"a_{name}")), per))
            return signals[-1]

        def flag(name):
            return ctx.enter_context(nc.semaphore(f"a_{name}"))

        X, XN, YN, YT, ident = c["X"], c["XN"], c["YN"], c["YT"], c["ident"]
        W = sb("a_W", [P, 6, D])
        W1 = sb("a_W1", [P, F])
        W2 = sb("a_W2", [P, FC, D])
        cols = sb("a_cols", [P, 8])
        b1c = sb("a_b1c", [P, FC])
        bv = sb("a_bv", [P, 2, D])
        bo = sb("a_bo", [P, T, D])
        b2 = sb("a_b2", [P, T, D])
        rope = sb("a_rope", [P, 4, S])
        rot = sb("a_rot", [P, 2, 2, S])
        part = sb("a_part", [P, 2, PARTS, S], BF16)
        QS = sb("a_QS", [P, H, S], BF16)
        KS = sb("a_KS", [P, H, S], BF16)
        zero = sb("a_zero", [2, S], BF16)
        one = sb("a_one", [2, S], BF16)
        V = sb("a_V", [P, T, H, 32])
        M = sb("a_M", [P, T, H])
        mh = sb("a_mh", [H, S], BF16)
        ml = sb("a_ml", [H, S], BF16)
        PT = sb("a_PT", [P, 8, 2, S])
        pvs = sb("a_pvs", [P, S])
        rec = sb("a_rec", [P, T, QUAD])
        AT = sb("a_AT", [P, T, D])
        ATT = sb("a_ATT", [P, S])
        XB = sb("a_XB", [P, T, D])
        XA = sb("a_XA", [P, T, D])
        hT = sb("a_hT", [P, FC, S])
        parts_d = nc.dram_tensor("a_parts", [2, PARTS, P, S], BF16).ap()
        max_d = nc.dram_tensor("a_max", [2, H, S], BF16).ap()
        FB = [ctx.enter_context(nc.psum_tensor(f"a_F{n}", [P, S], F32)) for n in range(2)]
        ST = [ctx.enter_context(nc.psum_tensor(f"a_ST{n}", [P, 2, S], F32)) for n in range(2)]
        PV = ctx.enter_context(nc.psum_tensor("a_PV", [P, S], F32))
        TB = ctx.enter_context(nc.psum_tensor("a_TB", [P, S], F32))

        NQ = H // QUAD
        UNITS = NQ * 2 * QUAD
        MAXT = H * T
        weights = flag("weights")
        const = flag("const")
        vmade = flag("vmade")
        norm = norm_signals(sig, 3)
        filled = sig("filled", 7 + MAXT + 1)
        free = [sig("free0", (8 + MAXT) // 2), sig("free1", (8 + MAXT) // 2)]
        yT = sig("yT", 2)
        roped = sig("roped", 4)
        summed = sig("summed", 2)
        cast = sig("cast", 4)
        rest = sig("rest", 4)
        vdone = sig("vdone", 2)
        stored = sig("stored", 16 * 2 * PARTS)
        stacked = sig("stacked", 16 * (2 * PAIRS + 1))
        maxed = sig("maxed", MAXT)
        mparts = sig("mparts", 2)
        mstored = sig("mstored", 32)
        mstacked = sig("mstacked", 16)
        scored = sig("scored", UNITS)
        exped = sig("exped", UNITS)
        pv = sig("pv", UNITS // QUAD)
        pvcopied = sig("pvcopied", NQ)
        pvturned = sig("pvturned", NQ)
        inv = sig("inv", NQ)
        attn = sig("attn", NQ)
        turned = sig("turned", 2)
        attT = sig("attT")
        projected = sig("projected")
        biased = sig("biased", 2)
        resid = sig("resid", 1)
        hidden = sig("hidden", FC)
        relu_a = sig("relu_a", 2)
        relu_v = sig("relu_v", 2)
        ffn = sig("ffn")
        tail = sig("tail", 2)

        block = ctx.enter_context(nc.Block())

        @block.sync
        def _(sp):
            for n, name in enumerate(["Wq", "Wqs", "Wk", "Wks", "Wv", "Wo"]):
                sp.dma_start(W[:, n, :], ins[name]).then_inc(weights, 16)
            sp.dma_start(W1[:, :], ins["aW1"]).then_inc(weights, 16)
            sp.dma_start(W2[:, :, :], ins["aW2"].rearrange("(c p) d -> p c d", p=P)).then_inc(weights, 16)
            sp.dma_start(cols[:, :], ins["acols"]).then_inc(weights, 16)
            sp.dma_start(b1c[:, :], ins["ab1"]).then_inc(weights, 16)
            sp.dma_start(rope[:, :, :], ins["rope"].rearrange("c p s -> p c s")).then_inc(weights, 16)
            for t in range(T):
                if t < 2:
                    sp.dma_start(bv[:, t, :], ins["bv"].partition_broadcast(P)).then_inc(weights, 16)
                sp.dma_start(bo[:, t, :], ins["bo"].partition_broadcast(P)).then_inc(weights, 16)
                sp.dma_start(b2[:, t, :], ins["ab2"].partition_broadcast(P)).then_inc(weights, 16)
            sp.wait_ge(const, 4)
            sp.dma_start(KS[STACK:STACK + 2, :, :], spread(one)).then_inc(weights, 16)
            sp.wait_ge(weights, 16 * 22)
            with sp.Fori(0, B) as i:
                sp.wait_ge(*turn(scored, i, 0))
                sp.dma_start(QS[STACK:STACK + 2, :, :], spread(zero)).then_inc(sem(stacked), 16)
                for z in range(2):
                    for n in range(PARTS):
                        if n < 2:
                            sp.wait_ge(*turn(cast, i, 2 * z + n + 1))
                        else:
                            sp.wait_ge(*turn(rest, i, 2 * z + 2))
                        sp.dma_start(parts_d[z, n, :, :], part[:, z, n, :]).then_inc(sem(stored), 16)
                for z, stack in enumerate((QS, KS)):
                    sp.wait_ge(*turn(stored, i, 16 * 2 * PARTS))
                    for a in range(PARTS):
                        for b in range(PARTS):
                            row = (PARTS * a + b) * HD
                            sp.dma_start(stack[row:row + HD, :, :],
                                         parts_d[z, b if z else a].rearrange("(h d) s -> d h s", d=HD)
                                         ).then_inc(sem(stacked), 16)
                sp.wait_ge(*turn(mparts, i, 2))
                sp.dma_start(max_d[0], mh[:, :]).then_inc(sem(mstored), 16)
                sp.dma_start(max_d[1], ml[:, :]).then_inc(sem(mstored), 16)
                sp.wait_ge(*turn(mstored, i, 32))
                sp.dma_start(QS[STACK:STACK + 2, :, :], max_d).then_inc(sem(mstacked), 16)
            sp.wait_ge(*turn(mstacked, B, 0))

        @block.gpsimd
        def _(pool):
            prime(pool, signals)
            pool.memset(zero[:, :], 0.0).then_inc(const, 1)
            pool.memset(one[:, :], 1.0).then_inc(const, 1)
            pool.wait_ge(weights, 16 * 22)
            with pool.Fori(0, B) as i:
                norm_root(pool, c, norm, i, 0)
                norm_root(pool, c, norm, i, 1)
                norm_wait(pool, norm, i, 0)
                pool.wait_ge(*turn(tail, i, 0))
                pool.tensor_tensor(XB[:, :, :], XN[:, :, :], bo[:, :, :], ALU.add).then_inc(sem(biased), 1)
                for z in range(2):
                    pool.wait_ge(*turn(roped, i, 2 * z + 2))
                    pool.tensor_tensor(rot[:, z, 0, :], rot[:, z, 0, :], rot[:, z, 1, :], ALU.add
                                       ).then_inc(sem(summed), 1)
                    pool.wait_ge(*turn(cast, i, 2 * z + 1))
                    pool.tensor_tensor(rot[:, z, 1, :], rot[:, z, 0, :], part[:, z, 0, :], ALU.subtract
                                       ).then_inc(sem(rest), 1)
                    pool.wait_ge(*turn(cast, i, 2 * z + 2))
                    pool.tensor_tensor(part[:, z, 2, :], rot[:, z, 1, :], part[:, z, 1, :], ALU.subtract
                                       ).then_inc(sem(rest), 1)
                norm_root(pool, c, norm, i, 2)
                pool.wait_ge(*turn(resid, i, 1))
                pool.tensor_tensor(XB[:, :, :], XA[:, :, :], b2[:, :, :], ALU.add).then_inc(sem(biased), 1)

        @block.scalar
        def _(act):
            act.wait_ge(weights, 16 * 22)
            with act.Fori(0, B) as i:
                act.wait_ge(*turn(filled, i, 1))
                act.activation(YT[:, :], FB[0][:, :], ACT.Identity, scale=cols[:, 4:5], bias=cols[:, 5:6]
                               ).then_inc(sem(yT), 1)
                for z in range(2):
                    act.wait_ge(*turn(summed, i, z + 1))
                    act.wait_ge(*turn(stored, i, 0))
                    act.activation(part[:, z, 0, :], rot[:, z, 0, :], ACT.Copy).then_inc(sem(cast), 1)
                    act.wait_ge(*turn(rest, i, 2 * z + 1))
                    act.activation(part[:, z, 1, :], rot[:, z, 1, :], ACT.Copy).then_inc(sem(cast), 1)
                act.wait_ge(*turn(filled, i, 8 + MAXT))
                act.wait_ge(*turn(mstored, i, 0))
                act.activation(mh[:, :], FB[1][0:H, :], ACT.Copy, scale=-1.0).then_inc(sem(mparts), 1)
                for u in range(UNITS):
                    act.wait_ge(*turn(scored, i, u + 1))
                    if u >= 8:
                        act.wait_ge(*turn(pv, i, u // QUAD - 1))
                    else:
                        act.wait_ge(*turn(pv, i, 0))
                    act.activation(PT[:, u % 8, :, :], ST[u % 2][:, :, :], ACT.Exp).then_inc(sem(exped), 1)
                act.wait_ge(*turn(turned, i, 1))
                act.activation(ATT[:, :], ST[0][:, 0, :], ACT.Copy).then_inc(sem(attT), 1)
                act.wait_ge(*turn(turned, i, 2))
                act.activation(YT[:, :], ST[1][:, 0, :], ACT.Identity, scale=cols[:, 6:7], bias=cols[:, 7:8]
                               ).then_inc(sem(yT), 1)
                for f in range(0, FC, 2):
                    act.wait_ge(*turn(hidden, i, f + 1))
                    act.activation(hT[:, f, :], ST[f // 2][:, 0 if f == 0 else 1, :], ACT.Relu,
                                   bias=b1c[:, f:f + 1]).then_inc(sem(relu_a), 1)

        @block.vector
        def _(dve):
            dve.memset(QS[64:96, :, :], 0.0).then_inc(const, 1)
            dve.memset(KS[64:96, :, :], 0.0).then_inc(const, 1)
            dve.memset(V[:, :, :, :], 0.0).then_inc(vmade, 1)
            dve.wait_ge(vmade, 1)
            dve.memset(V[:, :, :, HD:HD + 1], 1.0).then_inc(vmade, 1)
            dve.wait_ge(weights, 16 * 22)
            dve.wait_ge(vmade, 2)
            with dve.Fori(0, B) as i:
                def x_tile(t):
                    return X[:, bass.ds(i * T + t, 1), :].rearrange("p a d -> p (a d)")

                norm_measure(dve, c, norm, i, 0, x_tile)
                norm_scale(dve, c, norm, i, 0, lambda t: XN[:, t, :], x_tile)
                norm_wait(dve, norm, i, 0)
                norm_measure(dve, c, norm, i, 1, lambda t: XN[:, t, :])
                norm_scale(dve, c, norm, i, 1, lambda t: YN[:, t, :], lambda t: XN[:, t, :])
                for n in range(4):
                    dve.wait_ge(*turn(filled, i, n + 2))
                    dve.wait_ge(*turn(rest, i, 0))
                    dve.scalar_tensor_tensor(rot[:, n // 2, n % 2, :], FB[(n + 1) % 2][:, :], cols[:, n:n + 1],
                                             rope[:, n, :], ALU.add, ALU.mult).then_inc(sem(roped), 1)
                for n in range(2):
                    dve.wait_ge(*turn(filled, i, 6 + n))
                    dve.wait_ge(*turn(pv, i, 0))
                    dve.tensor_tensor(V[:, 2 * n:2 * n + 2, :, 0:HD],
                                      FB[(n + 5) % 2][:, 0:2 * D].rearrange("p (t h d) -> p t h d", t=2, d=HD),
                                      bv[:, :, :].rearrange("p t (h d) -> p t h d", d=HD), ALU.add
                                      ).then_inc(sem(vdone), 1)
                for n in range(MAXT):
                    h, t = n // T, n % T
                    dve.wait_ge(*turn(filled, i, 8 + n))
                    dve.tensor_reduce(M[:, t, h:h + 1], FB[(n + 7) % 2][:, :], AX_X, ALU.max).then_inc(sem(maxed), 1)
                dve.wait_ge(*turn(mparts, i, 1))
                dve.scalar_tensor_tensor(ml[:, :], FB[1][0:H, :], -1.0, mh[:, :], ALU.mult, ALU.subtract
                                         ).then_inc(sem(mparts), 1)
                for g in range(NQ):
                    dve.wait_ge(*turn(pv, i, 2 * g + 2))
                    dve.wait_ge(*turn(pvturned, i, g))
                    dve.tensor_copy(pvs[:, :], PV[:, :]).then_inc(sem(pvcopied), 1)
                    dve.wait_ge(*turn(pvturned, i, g + 1))
                    heads = TB[:, :].rearrange("p (t j e) -> p t j e", t=T, e=32)
                    dve.wait_ge(*turn(attn, i, g))
                    dve.reciprocal(rec[:, :, :], heads[:, :, :, HD]).then_inc(sem(inv), 1)
                    dve.wait_ge(*turn(inv, i, g + 1))
                    dve.tensor_tensor(AT[:, :, 32 * g:32 * g + 32].rearrange("p t (j e) -> p t j e", e=HD),
                                      heads[:, :, :, 0:HD], widen(rec[:, :, :], HD), ALU.mult).then_inc(sem(attn), 1)
                dve.wait_ge(*turn(projected, i, 1))
                dve.wait_ge(*turn(biased, i, 1))
                dve.tensor_tensor(XA[:, :, :], ST[0][:, 1, :].rearrange("p (t d) -> p t d", d=D), XB[:, :, :], ALU.add
                                  ).then_inc(sem(resid), 1)
                dve.wait_ge(*turn(resid, i, 1))
                norm_measure(dve, c, norm, i, 2, lambda t: XA[:, t, :])
                norm_scale(dve, c, norm, i, 2, lambda t: YN[:, t, :], lambda t: XA[:, t, :])
                for f in range(1, FC, 2):
                    dve.wait_ge(*turn(hidden, i, f + 1))
                    dve.tensor_scalar(hT[:, f, :], ST[f // 2][:, 1 if f == 1 else 0, :], b1c[:, f:f + 1], 0.0,
                                      ALU.add, ALU.max).then_inc(sem(relu_v), 1)
                dve.wait_ge(*turn(ffn, i, 1))
                dve.wait_ge(*turn(biased, i, 2))
                dve.tensor_tensor(XA[:, :, :], TB[:, :].rearrange("p (t d) -> p t d", d=D), XB[:, :, :], ALU.add
                                  ).then_inc(sem(tail), 1)
                dve.wait_ge(*turn(tail, i, 1))
                xb = X[:, bass.ds(i * T, T), :]
                dve.tensor_tensor(xb, xb, XA[:, :, :], ALU.add).then_inc(sem(tail), 1)
                dve.wait_ge(*turn(tail, i, 2))

        @block.tensor
        def _(pe):
            pe.wait_ge(weights, 16 * 22)
            pe.wait_ge(vmade, 2)
            with pe.Fori(0, B) as i:
                norm_wait(pe, norm, i, 1)
                pe.wait_ge(*turn(maxed, i, 0))
                for t in range(T):
                    last = pe.transpose(FB[0][:, t * P:(t + 1) * P], YN[:, t, :], ident[:, :])
                last.then_inc(sem(filled), 1)
                pe.wait_ge(*turn(yT, i, 1))
                pe.wait_ge(*turn(mparts, i, 0))
                for n in range(4):
                    if n >= 2:
                        pe.wait_ge(*turn(roped, i, n - 1))
                    pe.matmul(FB[(n + 1) % 2][:, :], W[:, n, :], YT[:, :], start=True, stop=True
                              ).then_inc(sem(filled), 1)
                for n in range(2):
                    pe.wait_ge(*turn(roped, i, n + 3))
                    for t in range(2 * n, 2 * n + 2):
                        last = pe.matmul(FB[(n + 5) % 2][:, (t % 2) * D:(t % 2 + 1) * D], YT[:, t * P:(t + 1) * P],
                                         W[:, 4, :], start=True, stop=True)
                    last.then_inc(sem(filled), 1)
                pe.wait_ge(*turn(stacked, i, per_turn(stacked)))
                for n in range(MAXT):
                    h, t = n // T, n % T
                    if n < 2:
                        pe.wait_ge(*turn(vdone, i, n + 1))
                    else:
                        pe.wait_ge(*turn(maxed, i, n - 1))
                    pe.matmul(FB[(n + 7) % 2][:, :], QS[0:KR0, h, t * P:(t + 1) * P], KS[0:KR0, h, :],
                              start=True, stop=True).then_inc(sem(filled), 1)
                pe.wait_ge(*turn(maxed, i, MAXT))
                for t in range(T):
                    last = pe.transpose(FB[1][0:H, t * P:(t + 1) * P], M[:, t, :], ident[:, :])
                last.then_inc(sem(filled), 1)

                def values(w):
                    pe.wait_ge(*turn(exped, i, QUAD * w + QUAD))
                    if w % 2 == 0:
                        pe.wait_ge(*turn(pvcopied, i, w // 2))
                    for kk in range(2):
                        for j in range(QUAD):
                            kt = 2 * (w % 2) + kk
                            last = pe.matmul(PV[32 * j:32 * j + 32, :], V[:, kt, QUAD * (w // 2) + j, :],
                                             PT[:, (QUAD * w + j) % 8, kk, :], start=(kt == 0), stop=(kt == T - 1))
                    last.then_inc(sem(pv), 1)

                def turn_values(g):
                    pe.wait_ge(*turn(pvcopied, i, g + 1))
                    pe.wait_ge(*turn(attn, i, g))
                    if g == 0:
                        pe.wait_ge(*turn(tail, i, 0))
                    for t in range(T):
                        last = pe.transpose(TB[:, t * P:(t + 1) * P], pvs[:, t * P:(t + 1) * P], ident[:, :])
                    last.then_inc(sem(pvturned), 1)

                pe.wait_ge(*turn(mstacked, i, 16))
                pe.wait_ge(*turn(relu_a, i, 0))
                pe.wait_ge(*turn(relu_v, i, 0))
                for w in range(NQ * 2):
                    for j in range(QUAD):
                        u = QUAD * w + j
                        h = QUAD * (w // 2) + j
                        if u >= 2:
                            pe.wait_ge(*turn(exped, i, u - 1))
                        for kk in range(2):
                            kt = 2 * (w % 2) + kk
                            last = pe.matmul(ST[u % 2][:, kk, :], KS[0:KR0, h, kt * P:(kt + 1) * P], QS[0:KR0, h, :],
                                             start=True, stop=True)
                        last.then_inc(sem(scored), 1)
                        if j == 1 and w >= 1:
                            values(w - 1)
                        if j == 3 and w >= 2 and w % 2 == 0:
                            turn_values(w // 2 - 1)
                values(NQ * 2 - 1)
                turn_values(NQ - 1)
                pe.wait_ge(*turn(attn, i, NQ))
                pe.wait_ge(*turn(exped, i, UNITS))
                for t in range(T):
                    last = pe.transpose(ST[0][:, 0, t * P:(t + 1) * P], AT[:, t, :], ident[:, :])
                last.then_inc(sem(turned), 1)
                pe.wait_ge(*turn(attT, i, 1))
                for t in range(T):
                    last = pe.matmul(ST[0][:, 1, t * D:(t + 1) * D], ATT[:, t * P:(t + 1) * P], W[:, 5, :],
                                     start=True, stop=True)
                last.then_inc(sem(projected), 1)
                norm_wait(pe, norm, i, 2)
                for t in range(T):
                    last = pe.transpose(ST[1][:, 0, t * P:(t + 1) * P], YN[:, t, :], ident[:, :])
                last.then_inc(sem(turned), 1)
                pe.wait_ge(*turn(yT, i, 2))
                for f, bank in enumerate([(0, 0), (0, 1), (1, 1), (1, 0)]):
                    pe.matmul(ST[bank[0]][:, bank[1], :], W1[:, f * P:(f + 1) * P], YT[:, :], start=True, stop=True
                              ).then_inc(sem(hidden), 1)
                pe.wait_ge(*turn(relu_a, i, 2))
                pe.wait_ge(*turn(relu_v, i, 2))
                for t in range(T):
                    for f in range(FC):
                        last = pe.matmul(TB[:, t * D:(t + 1) * D], hT[:, f, t * P:(t + 1) * P], W2[:, f, :],
                                         start=(f == 0), stop=(f == FC - 1))
                last.then_inc(sem(ffn), 1)


PAST = 6
LINES = H * PAST
QC = S + S // 2 + P
IR = STACK
KR1 = 128
MR = KR1 - 2
NEG = -1.0e30


def layer1_attention(nc, ins, c):
    with ExitStack() as ctx:
        def sb(name, shape, dt=F32):
            return ctx.enter_context(nc.sbuf_tensor(f"c_{name}", shape, dt))

        signals = []

        def sig(name, per=1):
            signals.append((ctx.enter_context(nc.semaphore(f"c_{name}")), per))
            return signals[-1]

        def flag(name):
            return ctx.enter_context(nc.semaphore(f"c_{name}"))

        X, XN, ident = c["X"], c["XN"], c["ident"]
        WQ = sb("WQ", [P, 3 * D])
        WO = sb("WO", [P, D])
        WR = sb("WR", [P, 4 * LINES])
        WW = sb("WW", [P, 2, 2 * LINES])
        cols = sb("cols", [P, 2])
        bv = sb("bv", [P, 2, D])
        bo = sb("bo", [P, T, D])
        XT = sb("XT", [P, S + 1])
        dec = sb("dec", [P, 4, H])
        bias = sb("bias", [P, H])
        ramp = sb("ramp", [P, P + 4])
        table = sb("table", [P, H, P])
        expo = sb("expo", [P, 4, H])
        DQ = sb("DQ", [P, 4, H])
        mask = sb("mask", [P, P], BF16)
        identb = sb("identb", [P, P], BF16)
        only = sb("only", [P, P], BF16)
        zero = sb("zero", [2, S], BF16)
        one = sb("one", [2, S], BF16)
        part = sb("part", [P, 2, PARTS, S], BF16)
        rn = sb("rn", [P, 3, T * H])
        lpart = sb("lpart", [LINES, PARTS, S], BF16)
        QS = sb("QS", [P, H, QC], BF16)
        KS = sb("KS", [P, H, S], BF16)
        QI = sb("QI", [PAIRS * PAST, H, S], BF16)
        KI = sb("KI", [PAIRS * PAST, H, S], BF16)
        V = sb("V", [P, T, H, 32])
        inc = sb("inc", [P, 2, S])
        SD = sb("SD", [P, 2, QUAD, T, P])
        MD = sb("MD", [P, T, H])
        M = sb("M", [P, T, H])
        mh = sb("mh", [QUAD, 2, S], BF16)
        ml = sb("ml", [QUAD, 2, S], BF16)
        PT = sb("PT", [P, 7, 2, S])
        room = SD[:, :, :, :, :].rearrange("p a j t k -> p (a j t k)")

        def carve(flat, at, shape):
            n = int(np.prod(shape))
            names = "abc"[:len(shape)]
            dims = dict(zip(names, shape))
            return flat[:, at:at + n].rearrange(f"p ({' '.join(names)}) -> p {' '.join(names)}", **dims), at + n

        LP, at = carve(room, 0, [T, 4 * LINES])
        prod, at = carve(room, at, [2, T, LINES])
        line, at = carve(room, at, [2, T, LINES])
        LQ, at = carve(room, at, [6, LINES])
        LK, at = carve(room, at, [T, LINES])
        room = PT[:, :, :, :].rearrange("p u k s -> p (u k s)")
        qk, at = carve(room, 0, [2, S])
        rem, at = carve(room, at, [2, S])
        lrem = room[0:LINES, at:at + S]
        pvs = sb("pvs", [P, S])
        rec = sb("rec", [P, T, QUAD])
        AT = sb("AT", [P, T, D])
        ATT = sb("ATT", [P, S])
        XB = sb("XB", [P, T, D])
        qk_d = nc.dram_tensor("c_parts", [2, PARTS, P, QC], BF16).ap()
        line_d = nc.dram_tensor("c_lines", [4, PARTS, LINES, QC - P], BF16).ap()
        max_d = nc.dram_tensor("c_max", [2, H, QC], BF16).ap()
        FB = [ctx.enter_context(nc.psum_tensor(f"c_F{n}", [P, S], F32)) for n in range(4)]
        ST = ctx.enter_context(nc.psum_tensor("c_ST", [P, 2, S], F32))
        PV = ctx.enter_context(nc.psum_tensor("c_PV", [P, S], F32))
        TB = ctx.enter_context(nc.psum_tensor("c_TB", [P, S], F32))

        NQ = H // QUAD
        UQ = QUAD + 1
        NPREP = 18
        prep_uses = [len([u for u in range(NPREP) if u % 4 == n]) for n in range(4)]
        SPANS = [(0, 0, S), (S, 2 * P, S), (S + 2 * P, 3 * P, S)]

        weights, made, table_made = flag("weights"), flag("made"), flag("table_made")
        made2 = flag("made2")
        minus_half = sb("minus_half", [P, T * H])
        norm = norm_signals(sig, 1)
        filled = sig("filled", NPREP + 4 * H)
        free = [sig(f"free{n}", prep_uses[n] + H) for n in range(4)]
        xT = sig("xT")
        projected = sig("projected", 2)
        cast, rest = sig("cast", 4), sig("rest", 4)
        vdone = sig("vdone", 2)
        points = sig("points", 8)
        product = sig("product", 4)
        crossed = sig("crossed", 2)
        squared = sig("squared", 2)
        summed = sig("summed", 4)
        normed = sig("normed", 2)
        unit = sig("unit", 2)
        scaled = sig("scaled", 1)
        decayed = sig("decayed", 4)
        lcast, lrest, lthird = sig("lcast", 10), sig("lrest", 5), sig("lthird", 5)
        lstored = sig("lstored", 16 * 5 * PARTS)
        stored = sig("stored", 16 * (3 * PARTS + PARTS))
        stacked = sig("stacked", 16 * (6 * PAIRS + 3))
        inc_copied = sig("inc_copied", H)
        inc_decayed = sig("inc_decayed", H)
        diag = sig("diag", H)
        maxed = sig("maxed", 4 * H)
        mjoined = sig("mjoined", NQ)
        mturned = sig("mturned", NQ)
        mparts = sig("mparts", 2 * NQ)
        mstored = sig("mstored", 16 * 6 * NQ)
        mstacked = sig("mstacked", 16 * NQ)
        scored = sig("scored", UQ * NQ)
        exped = sig("exped", UQ * NQ)
        pv, pvcopied, pvturned, inv, attn = sig("pv", NQ), sig("pvcopied", NQ), sig("pvturned", NQ), sig("inv", NQ), sig("attn", NQ)
        turned, attT, wo, biased, tail = sig("turned"), sig("attT"), sig("wo"), sig("biased"), sig("tail", 1)
        NW = 10 + 4 + 2

        def view(dst):
            return dst.rearrange("p (h e) -> p h e", e=PAST)

        block = ctx.enter_context(nc.Block())

        @block.sync
        def _(sp):
            sp.dma_start(WQ[:, :], ins["c_qkv"]).then_inc(weights, 16)
            sp.dma_start(WO[:, :], ins["c_wo"]).then_inc(weights, 16)
            sp.dma_start(WR[:, :], ins["c_read"]).then_inc(weights, 16)
            sp.dma_start(WW[:, 0, :], ins["c_write1"]).then_inc(weights, 16)
            sp.dma_start(WW[:, 1, :], ins["c_write2"]).then_inc(weights, 16)
            sp.dma_start(cols[:, :], ins["c_cols"]).then_inc(weights, 16)
            sp.dma_start(dec[:, 0, :], ins["c_decay"].partition_broadcast(P)).then_inc(weights, 16)
            sp.dma_start(bias[:, :], ins["c_bias"].partition_broadcast(P)).then_inc(weights, 16)
            for t in range(2):
                sp.dma_start(bv[:, t, :], ins["c_bv"].partition_broadcast(P)).then_inc(weights, 16)
            for t in range(T):
                sp.dma_start(bo[:, t, :], ins["c_bo"].partition_broadcast(P)).then_inc(weights, 16)
            sp.wait_ge(made, 7)
            sp.dma_start(KS[MR:KR1, :, :], spread(one)).then_inc(weights, 16)
            sp.wait_ge(made2, 6)
            sp.dma_start(only[MR:KR1, :], one[:, 0:P]).then_inc(weights, 16)
            sp.wait_ge(weights, 16 * NW)
            with sp.Fori(0, B) as i:
                sp.wait_ge(*turn(scored, i, 0))
                for n, (at, q0, q1) in enumerate(SPANS):
                    sp.dma_start(QS[MR:KR1, :, at:at + q1 - q0], spread(zero)[:, :, 0:q1 - q0]).then_inc(sem(stacked), 16)
                for z in range(2):
                    for n in range(PARTS):
                        if n < 2:
                            sp.wait_ge(*turn(cast, i, 2 * z + n + 1))
                        else:
                            sp.wait_ge(*turn(rest, i, 2 * z + 2))
                        for at, q0, q1 in SPANS[0:1 if z else 3]:
                            sp.dma_start(qk_d[z, n, :, at:at + q1 - q0], part[:, z, n, q0:q1]).then_inc(sem(stored), 16)
                for n, (kind, at, width) in enumerate([(2, 0, S), (3, 0, S), (1, 0, S), (0, 0, S), (0, S, 2 * P)]):
                    sp.wait_ge(*turn(lthird, i, n + 1))
                    for a in range(PARTS):
                        sp.dma_start(line_d[kind, a, :, at:at + width], lpart[:, a, 0:width]).then_inc(sem(lstored), 16)
                sp.wait_ge(*turn(stored, i, per_turn(stored)))
                sp.wait_ge(*turn(lstored, i, per_turn(lstored)))
                for a in range(PARTS):
                    for b in range(PARTS):
                        row, lrow = (PARTS * a + b) * HD, (PARTS * a + b) * PAST
                        for dst, src in (
                            (QS[row:row + HD, :, :], qk_d[0, a].rearrange("(h d) s -> d h s", d=HD)),
                            (KS[row:row + HD, :, :], qk_d[1, b, :, 0:S].rearrange("(h d) s -> d h s", d=HD)),
                            (QS[IR + lrow:IR + lrow + PAST, :, P:QC], line_d[0, a].rearrange("(h d) s -> d h s", d=PAST)),
                            (KS[IR + lrow:IR + lrow + PAST, :, :], line_d[1, b, :, 0:S].rearrange("(h d) s -> d h s", d=PAST)),
                            (QI[lrow:lrow + PAST, :, :], line_d[2, a, :, 0:S].rearrange("(h d) s -> d h s", d=PAST)),
                            (KI[lrow:lrow + PAST, :, :], line_d[3, b, :, 0:S].rearrange("(h d) s -> d h s", d=PAST)),
                        ):
                            sp.dma_start(dst, src).then_inc(sem(stacked), 16)
                for g in range(NQ):
                    hs = slice(QUAD * g, QUAD * g + QUAD)
                    sp.wait_ge(*turn(mparts, i, 2 * g + 2))
                    for n, m in enumerate((mh, ml)):
                        for at, q0, q1 in SPANS:
                            sp.dma_start(max_d[n, hs, at:at + q1 - q0], m[:, g % 2, q0:q1]).then_inc(sem(mstored), 16)
                    sp.wait_ge(*turn(mstored, i, 96 * (g + 1)))
                    sp.dma_start(QS[MR:KR1, hs, :], max_d[:, hs, :]).then_inc(sem(mstacked), 16)
            sp.wait_ge(*turn(mstacked, B, 0))

        @block.gpsimd
        def _(pool):
            prime(pool, signals)
            pool.memset(identb[:, :], 0.0).then_inc(made, 1)
            pool.memset(mask[:, :], 0.0).then_inc(made, 1)
            pool.iota(ramp[:, 0:P], pattern=[[-1, P]], base=0, channel_multiplier=1,
                      allow_small_or_imprecise_dtypes=True).then_inc(made, 1)
            pool.iota(ramp[:, P:P + 3], pattern=[[P, 3]], base=0, channel_multiplier=1,
                      allow_small_or_imprecise_dtypes=True).then_inc(made, 1)
            pool.iota(ramp[:, P + 3:P + 4], pattern=[[1, 1]], base=P, channel_multiplier=-1,
                      allow_small_or_imprecise_dtypes=True).then_inc(made, 1)
            pool.memset(zero[:, :], 0.0).then_inc(made, 1)
            pool.memset(one[:, :], 1.0).then_inc(made, 1)
            pool.wait_ge(made, 7)
            pool.affine_select(out=identb[:, :], in_=identb[:, :], compare_op=ALU.not_equal, fill=1.0,
                               base=0, pattern=[[-1, P]], channel_multiplier=1).then_inc(made, 1)
            pool.affine_select(out=mask[:, :], in_=mask[:, :], compare_op=ALU.is_ge, fill=NEG,
                               base=0, pattern=[[-1, P]], channel_multiplier=1).then_inc(made, 1)
            pool.wait_ge(table_made, 6 + H)
            pool.affine_select(out=table[:, :, :], in_=table[:, :, :], compare_op=ALU.is_gt, fill=0.0,
                               base=0, pattern=[[0, H], [-1, P]], channel_multiplier=1).then_inc(made, 1)
            pool.wait_ge(weights, 16 * NW)
            with pool.Fori(0, B) as i:
                norm_root(pool, c, norm, i, 0)
                pool.wait_ge(*turn(stored, i, 0))
                pool.wait_ge(*turn(filled, i, 0))
                pool.wait_ge(*turn(tail, i, 0))
                for z in range(2):
                    pool.wait_ge(*turn(cast, i, 2 * z + 1))
                    pool.tensor_tensor(rem[:, z, :], qk[:, z, :], part[:, z, 0, :], ALU.subtract).then_inc(sem(rest), 1)
                    pool.wait_ge(*turn(cast, i, 2 * z + 2))
                    pool.tensor_tensor(part[:, z, 2, :], rem[:, z, :], part[:, z, 1, :], ALU.subtract).then_inc(sem(rest), 1)
                for z in range(2):
                    pool.wait_ge(*turn(points, i, 4 * z + 4))
                    if z:
                        pool.wait_ge(*turn(squared, i, 1))
                        pool.wait_ge(*turn(summed, i, 2))
                    ab, cd = ((0, 1), (2, 3)) if z == 0 else ((0, 2), (1, 3))
                    for n, (a, b) in enumerate((ab, cd)):
                        pool.tensor_tensor(prod[:, n, :, :], LP[:, :, a * LINES:(a + 1) * LINES],
                                           LP[:, :, b * LINES:(b + 1) * LINES], ALU.mult).then_inc(sem(product), 1)
                    pool.wait_ge(*turn(product, i, 2 * z + 2))
                    pool.tensor_tensor(line[:, z, :, :], prod[:, 0, :, :], prod[:, 1, :, :], ALU.subtract
                                       ).then_inc(sem(crossed), 1)
                    pool.wait_ge(*turn(crossed, i, z + 1))
                    pool.tensor_tensor(prod[:, 0, :, :], line[:, z, :, :], line[:, z, :, :], ALU.mult
                                       ).then_inc(sem(squared), 1)
                    pool.wait_ge(*turn(summed, i, 2 * z + 2))
                    pool.tensor_tensor(rn[:, 2, :], rn[:, 1, :], minus_half[:, :], ALU.pow).then_inc(sem(normed), 1)
                    pool.wait_ge(*turn(normed, i, z + 1))
                    v = line[:, z, :, :].rearrange("p t (h e) -> p (t h) e", e=PAST)
                    pool.tensor_tensor(v, v, widen(rn[:, 2, :], PAST), ALU.mult).then_inc(sem(unit), 1)
                    pool.wait_ge(*turn(unit, i, z + 1))
                for n in range(5):
                    width = S if n < 4 else 2 * P
                    pool.wait_ge(*turn(lcast, i, 2 * n + 2))
                    pool.tensor_tensor(lpart[:, 2, 0:width], lrem[:, 0:width], lpart[:, 1, 0:width], ALU.subtract
                                       ).then_inc(sem(lthird), 1)
                for h in range(H):
                    pool.wait_ge(*turn(inc_copied, i, h + 1))
                    tab = table[:, h, :].unsqueeze(1).to_broadcast([P, T, P])
                    v = inc[:, h % 2, :].rearrange("p (t k) -> p t k", k=P)
                    pool.tensor_tensor(v, v, tab, ALU.mult).then_inc(sem(inc_decayed), 1)

        @block.scalar
        def _(act):
            act.wait_ge(weights, 16 * NW)
            act.wait_ge(table_made, 1)
            act.activation(dec[:, 2, :], dec[:, 1, :], ACT.Exp, scale=-1.0).then_inc(table_made, 1)
            act.wait_ge(table_made, 2)
            act.activation(dec[:, 2, :], dec[:, 2, :], ACT.Ln, bias=1.0).then_inc(table_made, 1)
            act.wait_ge(table_made, 6)
            for h in range(H):
                act.activation(table[:, h, :], ramp[:, 0:P], ACT.Exp, scale=dec[:, 3, h:h + 1]).then_inc(table_made, 1)
            act.activation(DQ[:, :, :], expo[:, :, :], ACT.Exp).then_inc(table_made, 1)
            with act.Fori(0, B) as i:
                act.wait_ge(*turn(filled, i, 1))
                act.activation(XT[:, 1:S + 1], FB[0][:, :], ACT.Copy).then_inc(sem(xT), 1)
                act.sem_inc(sem(free[0]), 1)
                act.wait_ge(*turn(stored, i, 0))
                for z in range(2):
                    act.wait_ge(*turn(projected, i, z + 1))
                    act.activation(part[:, z, 0, :], qk[:, z, :], ACT.Copy).then_inc(sem(cast), 1)
                    act.wait_ge(*turn(rest, i, 2 * z + 1))
                    act.activation(part[:, z, 1, :], rem[:, z, :], ACT.Copy).then_inc(sem(cast), 1)
                for z in range(2):
                    if z:
                        act.wait_ge(*turn(product, i, 2))
                    for t in range(T):
                        u = 5 + 4 * z + t
                        act.wait_ge(*turn(filled, i, u + 1))
                        act.activation(LP[:, t, :], FB[u % 4][:, 0:4 * LINES], ACT.Copy).then_inc(sem(points), 1)
                        act.wait_ge(*turn(points, i, 4 * z + t + 1))
                        act.sem_inc(sem(free[u % 4]), 1)
                for n in range(5):
                    u = 13 + n
                    width = S if n < 4 else 2 * P
                    act.wait_ge(*turn(filled, i, u + 1))
                    if n:
                        act.wait_ge(*turn(lstored, i, 48 * n))
                    else:
                        act.wait_ge(*turn(lstored, i, 0))
                    act.activation(lpart[:, 0, 0:width], FB[u % 4][0:LINES, 0:width], ACT.Copy).then_inc(sem(lcast), 1)
                    act.wait_ge(*turn(lrest, i, n + 1))
                    act.activation(lpart[:, 1, 0:width], lrem[:, 0:width], ACT.Copy).then_inc(sem(lcast), 1)

                def incidence(h):
                    act.wait_ge(*turn(filled, i, NPREP + 4 * h + 1))
                    if h >= 2:
                        act.wait_ge(*turn(diag, i, h - 1))
                    act.activation(inc[:, h % 2, :], FB[(0) % 4][:, :], ACT.Copy).then_inc(sem(inc_copied), 1)
                    act.wait_ge(*turn(inc_copied, i, h + 1))
                    act.sem_inc(sem(free[0]), 1)

                def minus_max(g):
                    act.wait_ge(*turn(mturned, i, g + 1))
                    act.wait_ge(*turn(mstored, i, 96 * (g - 1) if g >= 2 else 0))
                    act.activation(mh[:, g % 2, :], TB[0:QUAD, :], ACT.Copy, scale=-1.0).then_inc(sem(mparts), 1)

                def exp(g, j):
                    u = UQ * g + j
                    act.wait_ge(*turn(scored, i, u + 1))
                    act.wait_ge(*turn(pv, i, (u - 7) // UQ + 1 if u >= 7 else 0))
                    act.activation(PT[:, u % 7, :, :], ST[:, :, :], ACT.Exp).then_inc(sem(exped), 1)

                for g in range(-1, NQ):
                    for j in range(QUAD):
                        if g + 1 < NQ:
                            incidence(QUAD * (g + 1) + j)
                        if g >= 0:
                            exp(g, j)
                    if g >= 0:
                        exp(g, QUAD)
                    if g + 1 < NQ:
                        minus_max(g + 1)
                act.wait_ge(*turn(turned, i, 1))
                act.activation(ATT[:, :], ST[:, 0, :], ACT.Copy).then_inc(sem(attT), 1)

        @block.vector
        def _(dve):
            dve.memset(V[:, :, :, :], 0.0).then_inc(made2, 1)
            dve.memset(QS[:, :, 0:P], 0.0).then_inc(made2, 1)
            dve.memset(XT[:, 0:1], 0.0).then_inc(made2, 1)
            dve.memset(minus_half[:, :], -0.5).then_inc(made2, 1)
            dve.memset(only[:, :], 0.0).then_inc(made2, 1)
            dve.wait_ge(made2, 5)
            dve.memset(V[:, :, :, HD:HD + 1], 1.0).then_inc(made2, 1)
            dve.wait_ge(made2, 6)
            dve.wait_ge(weights, 16 * NW)
            dve.tensor_scalar(dec[:, 1, :], dec[:, 0, :], -44.0, None, ALU.max).then_inc(table_made, 1)
            dve.wait_ge(table_made, 3)
            dve.tensor_scalar(dec[:, 3, :], dec[:, 2, :], -1.0, None, ALU.mult).then_inc(table_made, 1)
            dve.tensor_scalar(ramp[:, 0:P], ramp[:, 0:P], 0.0, None, ALU.max).then_inc(table_made, 1)
            dve.wait_ge(table_made, 5)
            dve.tensor_tensor(expo[:, :, :], dec[:, 3, :].unsqueeze(1).to_broadcast([P, 4, H]),
                              widen(ramp[:, P:P + 4], H), ALU.mult).then_inc(table_made, 1)
            dve.wait_ge(table_made, 7 + H)
            dve.wait_ge(made, 10)
            with dve.Fori(0, B) as i:
                def x_tile(t):
                    return X[:, bass.ds(i * T + t, 1), :].rearrange("p a d -> p (a d)")

                norm_measure(dve, c, norm, i, 0, x_tile)
                norm_scale(dve, c, norm, i, 0, lambda t: XN[:, t, :], x_tile)
                for z in range(2):
                    dve.wait_ge(*turn(filled, i, z + 2))
                    dve.wait_ge(*turn(rest, i, 0))
                    dve.tensor_scalar(qk[:, z, :], FB[1 + z][:, :], cols[:, z:z + 1], 1.0 if z else float(HD) ** -0.5,
                                      ALU.add, ALU.mult).then_inc(sem(projected), 1)
                    dve.wait_ge(*turn(projected, i, z + 1))
                    dve.sem_inc(sem(free[1 + z]), 1)
                for n in range(2):
                    dve.wait_ge(*turn(filled, i, 4 + n))
                    dve.wait_ge(*turn(pv, i, 0))
                    dve.tensor_tensor(V[:, 2 * n:2 * n + 2, :, 0:HD],
                                      FB[(n + 3) % 4][:, 0:2 * D].rearrange("p (t h d) -> p t h d", t=2, d=HD),
                                      bv[:, :, :].rearrange("p t (h d) -> p t h d", d=HD), ALU.add
                                      ).then_inc(sem(vdone), 1)
                    dve.wait_ge(*turn(vdone, i, n + 1))
                    dve.sem_inc(sem(free[(n + 3) % 4]), 1)
                for z in range(2):
                    dve.wait_ge(*turn(squared, i, z + 1))
                    dve.tensor_reduce(rn[:, 0, :], prod[:, 0, :, :].rearrange("p t (h e) -> p (t h) e", e=PAST),
                                      AX_X, ALU.add).then_inc(sem(summed), 1)
                    dve.wait_ge(*turn(summed, i, 2 * z + 1))
                    dve.tensor_scalar(rn[:, 1, :], rn[:, 0, :], 1e-24, None, ALU.max).then_inc(sem(summed), 1)
                dve.wait_ge(*turn(unit, i, 1))
                v = line[:, 0, :, :].rearrange("p t (h e) -> p t h e", e=PAST)
                dve.tensor_tensor(v, v, widen(bias[:, :], PAST).unsqueeze(1).to_broadcast([P, T, H, PAST]), ALU.mult
                                  ).then_inc(sem(scaled), 1)
                dve.wait_ge(*turn(scaled, i, 1))
                dve.wait_ge(*turn(unit, i, 2))
                at = 0
                for kt in range(T - 1):
                    n = T - 1 - kt
                    dve.tensor_tensor(LQ[:, at:at + n, :].rearrange("p t (h e) -> p t h e", e=PAST), v[:, kt + 1:T],
                                      widen(DQ[:, 0:n, :], PAST), ALU.mult).then_inc(sem(decayed), 1)
                    at += n
                dve.tensor_tensor(LK[:, :, :].rearrange("p t (h e) -> p t h e", e=PAST),
                                  line[:, 1, :, :].rearrange("p t (h e) -> p t h e", e=PAST),
                                  widen(DQ[:, 3, :], PAST).unsqueeze(1).to_broadcast([P, T, H, PAST]), ALU.mult
                                  ).then_inc(sem(decayed), 1)
                for n in range(5):
                    u = 13 + n
                    width = S if n < 4 else 2 * P
                    dve.wait_ge(*turn(lcast, i, 2 * n + 1))
                    dve.wait_ge(*turn(lthird, i, n))
                    dve.tensor_tensor(lrem[:, 0:width], FB[u % 4][0:LINES, 0:width], lpart[:, 0, 0:width], ALU.subtract
                                      ).then_inc(sem(lrest), 1)
                    dve.wait_ge(*turn(lrest, i, n + 1))
                    dve.sem_inc(sem(free[u % 4]), 1)

                def maxima(h):
                    g = h // QUAD
                    base = NPREP + 4 * h
                    dve.wait_ge(*turn(filled, i, base + 3))
                    dve.tensor_reduce(M[:, 3, h:h + 1], FB[2][:, 0:3 * P], AX_X, ALU.max).then_inc(sem(maxed), 1)
                    dve.tensor_reduce(M[:, 1, h:h + 1], FB[2][:, 3 * P:4 * P], AX_X, ALU.max).then_inc(sem(maxed), 1)
                    dve.wait_ge(*turn(filled, i, base + 4))
                    dve.tensor_reduce(M[:, 2, h:h + 1], FB[3][:, 0:2 * P], AX_X, ALU.max).then_inc(sem(maxed), 1)
                    dve.wait_ge(*turn(inc_decayed, i, h + 1))
                    if g >= 2:
                        dve.wait_ge(*turn(scored, i, UQ * (g - 1)))
                    else:
                        dve.wait_ge(*turn(scored, i, 0))
                    sd = SD[:, g % 2, h % QUAD, :, :]
                    dve.tensor_tensor(sd, FB[1][:, :].rearrange("p (t k) -> p t k", k=P),
                                      inc[:, h % 2, :].rearrange("p (t k) -> p t k", k=P), ALU.add).then_inc(sem(diag), 1)
                    dve.wait_ge(*turn(diag, i, h + 1))
                    dve.wait_ge(*turn(maxed, i, 4 * h + 3))
                    for n in (1, 2, 3):
                        dve.sem_inc(sem(free[n]), 1)
                    dve.tensor_reduce(MD[:, :, h], sd, AX_X, ALU.max).then_inc(sem(maxed), 1)

                def join(g):
                    hs = slice(QUAD * g, QUAD * g + QUAD)
                    dve.wait_ge(*turn(maxed, i, 4 * QUAD * (g + 1)))
                    dve.tensor_tensor(MD[:, 1:T, hs], MD[:, 1:T, hs], M[:, 1:T, hs], ALU.max).then_inc(sem(mjoined), 1)
                    dve.wait_ge(*turn(mparts, i, 2 * g + 1))
                    dve.scalar_tensor_tensor(ml[:, g % 2, :], TB[0:QUAD, :], -1.0, mh[:, g % 2, :], ALU.mult,
                                             ALU.subtract).then_inc(sem(mparts), 1)

                for g in range(-1, NQ):
                    if g + 1 < NQ:
                        for j in range(QUAD):
                            maxima(QUAD * (g + 1) + j)
                        join(g + 1)
                    if g >= 0:
                        dve.wait_ge(*turn(pv, i, g + 1))
                        dve.wait_ge(*turn(pvturned, i, g))
                        dve.tensor_copy(pvs[:, :], PV[:, :]).then_inc(sem(pvcopied), 1)
                        dve.wait_ge(*turn(pvturned, i, g + 1))
                        heads = TB[:, :].rearrange("p (t j e) -> p t j e", t=T, e=32)
                        dve.reciprocal(rec[:, :, :], heads[:, :, :, HD]).then_inc(sem(inv), 1)
                        dve.wait_ge(*turn(inv, i, g + 1))
                        dve.tensor_tensor(AT[:, :, 32 * g:32 * g + 32].rearrange("p t (j e) -> p t j e", e=HD),
                                          heads[:, :, :, 0:HD], widen(rec[:, :, :], HD), ALU.mult).then_inc(sem(attn), 1)
                        dve.wait_ge(*turn(attn, i, g + 1))
                xb = X[:, bass.ds(i * T, T), :]
                dve.tensor_tensor(XB[:, :, :], xb, bo[:, :, :], ALU.add).then_inc(sem(biased), 1)
                dve.wait_ge(*turn(wo, i, 1))
                dve.wait_ge(*turn(biased, i, 1))
                dve.tensor_tensor(xb, ST[:, 1, :].rearrange("p (t d) -> p t d", d=D), XB[:, :, :], ALU.add
                                  ).then_inc(sem(tail), 1)
                dve.wait_ge(*turn(tail, i, 1))

        @block.tensor
        def _(pe):
            pe.wait_ge(weights, 16 * NW)
            pe.wait_ge(made, 10)
            pe.wait_ge(made2, 6)
            with pe.Fori(0, B) as i:
                def bank(u):
                    pe.wait_ge(*turn(free[u % 4], i, u // 4))
                    return FB[u % 4]

                norm_wait(pe, norm, i, 0)
                f = bank(0)
                for t in range(T):
                    last = pe.transpose(f[:, t * P:(t + 1) * P], XN[:, t, :], ident[:, :])
                last.then_inc(sem(filled), 1)
                pe.wait_ge(*turn(xT, i, 1))
                for z in range(2):
                    pe.matmul(bank(1 + z)[:, :], WQ[:, z * D:(z + 1) * D], XT[:, 1:S + 1], start=True, stop=True
                              ).then_inc(sem(filled), 1)
                for n in range(2):
                    f = bank(3 + n)
                    for t in range(2 * n, 2 * n + 2):
                        last = pe.matmul(f[:, (t % 2) * D:(t % 2 + 1) * D], XT[:, 1 + t * P:1 + (t + 1) * P],
                                         WQ[:, 2 * D:3 * D], start=True, stop=True)
                    last.then_inc(sem(filled), 1)
                for t in range(T):
                    pe.matmul(bank(5 + t)[:, 0:4 * LINES], XT[:, 1 + t * P:1 + (t + 1) * P], WR[:, :],
                              start=True, stop=True).then_inc(sem(filled), 1)
                for t in range(T):
                    f = bank(9 + t)
                    pe.matmul(f[:, 0:2 * LINES], XT[:, t * P:(t + 1) * P], WW[:, 0, :], start=True, stop=True)
                    pe.matmul(f[:, 2 * LINES:4 * LINES], XT[:, 1 + t * P:1 + (t + 1) * P], WW[:, 1, :],
                              start=True, stop=True).then_inc(sem(filled), 1)
                for n, (src, tiles) in enumerate([(line[:, 0], range(T)), (line[:, 1], range(T)), (LK, range(T)),
                                                  (LQ, range(T)), (LQ, range(T, 6))]):
                    f = bank(13 + n)
                    if n == 0:
                        pe.wait_ge(*turn(scaled, i, 1))
                    elif n == 1:
                        pe.wait_ge(*turn(unit, i, 2))
                    else:
                        pe.wait_ge(*turn(decayed, i, 4))
                    for k, t in enumerate(tiles):
                        last = pe.transpose(f[0:LINES, k * P:(k + 1) * P], src[:, t, :], ident[:, :])
                    last.then_inc(sem(filled), 1)

                def logits(h):
                    def head_bank(n):
                        pe.wait_ge(*turn(free[n], i, prep_uses[n] + h))
                        return FB[n]

                    if h == 0:
                        pe.wait_ge(*turn(stacked, i, per_turn(stacked)))
                    f = head_bank(0)
                    for t in range(T):
                        ts = slice(t * P, (t + 1) * P)
                        last = pe.matmul(f[:, ts], QI[:, h, ts], KI[:, h, ts], start=True, stop=True)
                    last.then_inc(sem(filled), 1)
                    f = head_bank(1)
                    for t in range(T):
                        ts = slice(t * P, (t + 1) * P)
                        pe.matmul(f[:, ts], QS[0:STACK, h, ts], KS[0:STACK, h, ts], start=True, stop=False)
                        last = pe.matmul(f[:, ts], identb[:, :], mask[:, :], start=False, stop=True)
                    last.then_inc(sem(filled), 1)
                    f = head_bank(2)
                    for kt in range(3):
                        at = [3 * P, S + P, S + 2 * P][kt]
                        pe.matmul(f[:, kt * P:(kt + 1) * P], QS[0:KR1, h, at:at + P], KS[0:KR1, h, kt * P:(kt + 1) * P],
                                  start=True, stop=True)
                    pe.matmul(f[:, 3 * P:4 * P], QS[0:KR1, h, P:2 * P], KS[0:KR1, h, 0:P], start=True, stop=True
                              ).then_inc(sem(filled), 1)
                    f = head_bank(3)
                    pe.matmul(f[:, 0:P], QS[0:KR1, h, 2 * P:3 * P], KS[0:KR1, h, 0:P], start=True, stop=True)
                    pe.matmul(f[:, P:2 * P], QS[0:KR1, h, S:S + P], KS[0:KR1, h, P:2 * P], start=True, stop=True
                              ).then_inc(sem(filled), 1)

                def turn_max(g):
                    pe.wait_ge(*turn(mjoined, i, g + 1))
                    pe.wait_ge(*turn(attn, i, g - 1 if g >= 1 else 0))
                    for t in range(T):
                        last = pe.transpose(TB[0:QUAD, t * P:(t + 1) * P], MD[:, t, QUAD * g:QUAD * g + QUAD],
                                            ident[:, :])
                    last.then_inc(sem(mturned), 1)

                def diagonal(out, g, j, t):
                    pe.matmul(out, only[:, :], QS[0:KR1, QUAD * g + j, t * P:(t + 1) * P], start=True, stop=False)
                    return pe.matmul(out, SD[:, g % 2, j, t, :], ident[:, :], start=False, stop=True)

                def scores(g, j):
                    h = QUAD * g + j
                    if j == 0:
                        pe.wait_ge(*turn(mstacked, i, 16 * (g + 1)))
                    u = UQ * g + j
                    pe.wait_ge(*turn(exped, i, u))
                    if u == 0:
                        pe.wait_ge(*turn(tail, i, 0))
                    if j < QUAD:
                        diagonal(ST[:, 0, 0:P], g, j, 0)
                        pe.matmul(ST[:, 0, P:S], KS[0:KR1, h, 0:P], QS[0:KR1, h, P:S], start=True, stop=True)
                        diagonal(ST[:, 1, 0:P], g, j, 1)
                        pe.matmul(ST[:, 1, P:3 * P], KS[0:KR1, h, P:2 * P], QS[0:KR1, h, S:S + 2 * P],
                                  start=True, stop=True)
                        diagonal(ST[:, 1, 3 * P:4 * P], g, j, 3).then_inc(sem(scored), 1)
                    else:
                        for k in range(QUAD):
                            h = QUAD * g + k
                            at = (k % 2) * 2 * P
                            diagonal(ST[:, k // 2, at:at + P], g, k, 2)
                            last = pe.matmul(ST[:, k // 2, at + P:at + 2 * P], KS[0:KR1, h, 2 * P:3 * P],
                                             QS[0:KR1, h, S + 2 * P:QC], start=True, stop=True)
                        last.then_inc(sem(scored), 1)

                def values(g):
                    pe.wait_ge(*turn(exped, i, UQ * (g + 1)))
                    pe.wait_ge(*turn(pvcopied, i, g))
                    def buf(j):
                        return PT[:, (UQ * g + j) % 7, :, :]
                    for kt in range(T):
                        for j in range(QUAD):
                            if kt == 0:
                                src = buf(j)[:, 0, :]
                            elif kt == 1:
                                src = buf(j)[:, 1, 0:3 * P]
                            elif kt == 2:
                                src = buf(QUAD)[:, j // 2, (j % 2) * 2 * P:(j % 2 + 1) * 2 * P]
                            else:
                                src = buf(j)[:, 1, 3 * P:4 * P]
                            last = pe.matmul(PV[32 * j:32 * j + 32, kt * P:S], V[:, kt, QUAD * g + j, :], src,
                                             start=(kt == 0), stop=(kt == T - 1), skip_group_check=True)
                    last.then_inc(sem(pv), 1)

                def turn_values(g):
                    pe.wait_ge(*turn(pvcopied, i, g + 1))
                    pe.wait_ge(*turn(mparts, i, 2 * min(g + 2, NQ)))
                    pe.wait_ge(*turn(attn, i, g))
                    for t in range(T):
                        last = pe.transpose(TB[:, t * P:(t + 1) * P], pvs[:, t * P:(t + 1) * P], ident[:, :])
                    last.then_inc(sem(pvturned), 1)

                for g in range(-1, NQ):
                    for j in range(QUAD):
                        if g + 1 < NQ:
                            logits(QUAD * (g + 1) + j)
                        if g >= 0:
                            scores(g, j)
                    if g >= 0:
                        scores(g, QUAD)
                    if g + 1 < NQ:
                        turn_max(g + 1)
                    if g >= 0:
                        values(g)
                        turn_values(g)
                pe.wait_ge(*turn(attn, i, NQ))
                for t in range(T):
                    last = pe.transpose(ST[:, 0, t * P:(t + 1) * P], AT[:, t, :], ident[:, :])
                last.then_inc(sem(turned), 1)
                pe.wait_ge(*turn(attT, i, 1))
                for t in range(T):
                    last = pe.matmul(ST[:, 1, t * D:(t + 1) * D], ATT[:, t * P:(t + 1) * P], WO[:, :],
                                     start=True, stop=True)
                last.then_inc(sem(wo), 1)


def experts(nc, ins, c, tag, E):
    first = tag == "L0"
    func = ACT.Relu if first else ACT.Gelu
    with ExitStack() as ctx:
        def sb(name, shape, dt=F32):
            return ctx.enter_context(nc.sbuf_tensor(f"{tag}_{name}", shape, dt))

        signals = []

        def sig(name, per=1):
            signals.append((ctx.enter_context(nc.semaphore(f"{tag}_{name}")), per))
            return signals[-1]

        def flag(name):
            return ctx.enter_context(nc.semaphore(f"{tag}_{name}"))

        X, XN, XT, ident = c["X"], c["XN"], c["YT"], c["ident"]
        W1 = sb("W1", [P, E, F])
        W2 = sb("W2", [P, E, FC, D])
        b1 = sb("b1", [P, E, FC])
        b2 = sb("b2", [E, D])
        wr = sb("wr", [P, E])
        br = sb("br", [P, T, E])
        desc = sb("desc", [P, T, E])
        sc = sb("sc", [P, 12, T, E])
        red = sb("red", [P, 8, T])
        gT = sb("gT", [E, S])
        acc = sb("acc", [P, T, D])
        hT = sb("hT", [P, 2, FC, S])
        MB = [ctx.enter_context(nc.psum_tensor(f"{tag}_M{n}", [P, S], F32)) for n in range(2)]
        HB = [ctx.enter_context(nc.psum_tensor(f"{tag}_H{n}", [P, S], F32)) for n in range(FC)]
        YB = [ctx.enter_context(nc.psum_tensor(f"{tag}_Y{n}", [P, S], F32)) for n in range(2)]

        LOADS = 4 + 1 + 2 * 4 + T
        loads = flag("loads")
        made = flag("made")
        norm = norm_signals(sig, 1)
        turned, xT, logits = sig("turned"), sig("xT"), sig("logits")
        STEPS = 19
        route = sig("route", STEPS)
        exps = sig("exps")
        gturned, gcopied, b2out = sig("gturned"), sig("gcopied"), sig("b2out")
        hidden = sig("hidden", E * FC)
        act_a, act_v = sig("act_a", E * FC), sig("act_v", E * FC)
        y = sig("y", E)
        added = sig("added", E * T + 1)
        done = sig("done")

        def gate(dve, i, e):
            dve.wait_ge(*turn(y, i, e + 1))
            dve.wait_ge(*turn(added, i, 1 + e * T))
            for t in range(T):
                dve.scalar_tensor_tensor(acc[:, t, :], YB[e % 2][:, t * D:(t + 1) * D], sc[:, 10, t, e:e + 1],
                                         acc[:, t, :], ALU.mult, ALU.add).then_inc(sem(added), 1)

        def second(pe, i, e):
            pe.wait_ge(*turn(act_a, i, (e + 1) * FC))
            if first:
                pe.wait_ge(*turn(act_v, i, (e + 1) * FC))
            pe.wait_ge(*turn(added, i, 1 + (e - 1) * T if e >= 2 else 0))
            for t in range(T):
                for f in range(FC):
                    last = pe.matmul(YB[e % 2][:, t * D:(t + 1) * D], hT[:, e % 2, f, t * P:(t + 1) * P],
                                     W2[:, e, f, :], start=(f == 0), stop=(f == FC - 1))
            last.then_inc(sem(y), 1)

        block = ctx.enter_context(nc.Block())

        @block.sync
        def _(sp):
            w = 0
            for n in range(4):
                es = slice(n * E // 4, (n + 1) * E // 4)
                sp.dma_start(W1[:, es, :], ins[f"{tag}_w1"][:, es, :]).then_inc(loads, 16)
                sp.dma_start(W2[:, es, :, :], ins[f"{tag}_w2"][:, es, :, :]).then_inc(loads, 16)
                w += 2
            sp.dma_start(b1[:, :, :], ins[f"{tag}_b1"]).then_inc(loads, 16)
            sp.dma_start(b2[:, :], ins[f"{tag}_b2"]).then_inc(loads, 16)
            sp.dma_start(wr[:, :], ins[f"{tag}_wr"]).then_inc(loads, 16)
            w += 3
            if first:
                for t in range(T):
                    sp.dma_start(br[:, t, :], ins["L0_br"].partition_broadcast(P)).then_inc(loads, 16)
                    w += 1
            sp.wait_ge(loads, 16 * w)

        WAIT = 16 * (8 + 3 + (T if first else 0))

        @block.gpsimd
        def _(pool):
            prime(pool, signals)
            pool.iota(desc[:, :, :], pattern=[[0, T], [-1, E]], base=E, channel_multiplier=0,
                      allow_small_or_imprecise_dtypes=True).then_inc(made, 1)
            with pool.Fori(0, B) as i:
                norm_root(pool, c, norm, i, 0)

        @block.scalar
        def _(act):
            act.wait_ge(loads, WAIT)
            with act.Fori(0, B) as i:
                act.wait_ge(*turn(turned, i, 1))
                act.activation(XT[:, :], MB[0][:, :], ACT.Copy).then_inc(sem(xT), 1)
                act.wait_ge(*turn(route, i, 3))
                act.activation(sc[:, 2, :, :], sc[:, 1, :, :], ACT.Exp).then_inc(sem(exps), 1)
                for e in range(E):
                    for f in range(0, FC, 2 if first else 1):
                        act.wait_ge(*turn(hidden, i, e * FC + f + 1))
                        if e >= 2:
                            act.wait_ge(*turn(y, i, e - 1))
                        else:
                            act.wait_ge(*turn(y, i, 0))
                        act.activation(hT[:, e % 2, f, :], HB[f][:, :], func, bias=b1[:, e, f:f + 1]
                                       ).then_inc(sem(act_a), 2 if first else 1)

        @block.vector
        def _(dve):
            dve.wait_ge(loads, WAIT)
            dve.wait_ge(made, 1)
            with dve.Fori(0, B) as i:
                def x_tile(t):
                    return X[:, bass.ds(i * T + t, 1), :].rearrange("p a d -> p (a d)")

                def small(n):
                    return sc[:, n, :, :]

                def r(n):
                    return red[:, n, :]

                count = [0]

                def step(ins_):
                    count[0] += 1
                    ins_.then_inc(sem(route), 1)
                    dve.wait_ge(*turn(route, i, count[0]))

                norm_measure(dve, c, norm, i, 0, x_tile)
                dve.wait_ge(*turn(turned, i, 0))
                norm_scale(dve, c, norm, i, 0, lambda t: XN[:, t, :], x_tile)
                dve.wait_ge(*turn(logits, i, 1))
                lg = MB[1][:, 0:T * E].rearrange("p (t e) -> p t e", e=E)
                if first:
                    step(dve.tensor_tensor(small(0), lg, br[:, :, :], ALU.add))
                else:
                    step(dve.tensor_copy(small(0), lg))
                step(dve.tensor_reduce(r(0), small(0), AX_X, ALU.max))
                step(dve.tensor_tensor(small(1), small(0), widen(r(0), E), ALU.subtract))
                dve.wait_ge(*turn(exps, i, 1))
                if first:
                    step(dve.tensor_reduce(r(1), small(2), AX_X, ALU.add))
                    step(dve.reciprocal(r(2), r(1)))
                    step(dve.tensor_tensor(small(3), small(2), widen(r(2), E), ALU.mult))
                    key = small(3)
                else:
                    key = small(0)
                step(dve.tensor_reduce(r(3), key, AX_X, ALU.max))
                step(dve.tensor_tensor(small(4), key, widen(r(3), E), ALU.is_equal))
                step(dve.tensor_tensor(small(5), small(4), desc[:, :, :], ALU.mult))
                step(dve.tensor_reduce(r(4), small(5), AX_X, ALU.max))
                step(dve.tensor_tensor(small(6), desc[:, :, :], widen(r(4), E), ALU.is_equal))
                step(dve.scalar_tensor_tensor(small(7), small(6), -3.0e38, key, ALU.mult, ALU.add))
                step(dve.tensor_reduce(r(5), small(7), AX_X, ALU.max))
                step(dve.tensor_tensor(small(4), small(7), widen(r(5), E), ALU.is_equal))
                step(dve.tensor_tensor(small(5), small(4), desc[:, :, :], ALU.mult))
                step(dve.tensor_reduce(r(6), small(5), AX_X, ALU.max))
                step(dve.tensor_tensor(small(8), desc[:, :, :], widen(r(6), E), ALU.is_equal))
                step(dve.tensor_tensor(small(9), small(6), small(8), ALU.add))
                if first:
                    step(dve.tensor_tensor(small(10), small(9), small(3), ALU.mult))
                else:
                    step(dve.tensor_tensor(small(11), small(9), small(2), ALU.mult))
                    step(dve.tensor_reduce(r(1), small(11), AX_X, ALU.add))
                    step(dve.reciprocal(r(2), r(1)))
                    step(dve.tensor_tensor(small(10), small(11), widen(r(2), E), ALU.mult))
                assert count[0] == per_turn(route), count[0]
                dve.wait_ge(*turn(gturned, i, 1))
                dve.tensor_copy(gT[:, :], MB[0][0:E, :]).then_inc(sem(gcopied), 1)
                dve.wait_ge(*turn(b2out, i, 1))
                xb = X[:, bass.ds(i * T, T), :]
                dve.tensor_tensor(acc[:, :, :], MB[1][:, :].rearrange("p (t d) -> p t d", d=D), xb, ALU.add
                                  ).then_inc(sem(added), 1)
                for e in range(E):
                    if first:
                        for f in range(1, FC, 2):
                            dve.wait_ge(*turn(hidden, i, e * FC + f + 1))
                            if e >= 2:
                                dve.wait_ge(*turn(y, i, e - 1))
                            else:
                                dve.wait_ge(*turn(y, i, 0))
                            dve.tensor_scalar(hT[:, e % 2, f, :], HB[f][:, :], b1[:, e, f:f + 1], 0.0, ALU.add, ALU.max
                                              ).then_inc(sem(act_v), 2)
                    if e >= 1:
                        gate(dve, i, e - 1)
                gate(dve, i, E - 1)
                dve.wait_ge(*turn(added, i, 1 + E * T))
                dve.tensor_scalar(xb, acc[:, :, :], 1.0, None, ALU.mult).then_inc(sem(done), 1)
                dve.wait_ge(*turn(done, i, 1))

        @block.tensor
        def _(pe):
            pe.wait_ge(loads, WAIT)
            with pe.Fori(0, B) as i:
                norm_wait(pe, norm, i, 0)
                pe.wait_ge(*turn(gcopied, i, 0))
                for t in range(T):
                    last = pe.transpose(MB[0][:, t * P:(t + 1) * P], XN[:, t, :], ident[:, :])
                last.then_inc(sem(turned), 1)
                pe.wait_ge(*turn(xT, i, 1))
                pe.wait_ge(*turn(added, i, 0))
                for t in range(T):
                    last = pe.matmul(MB[1][:, t * E:(t + 1) * E], XT[:, t * P:(t + 1) * P], wr[:, :],
                                     start=True, stop=True)
                last.then_inc(sem(logits), 1)
                for e in range(E):
                    if e == 1:
                        pe.wait_ge(*turn(route, i, per_turn(route)))
                        for t in range(T):
                            last = pe.transpose(MB[0][0:E, t * P:(t + 1) * P], sc[:, 10, t, :], ident[:, :])
                        last.then_inc(sem(gturned), 1)
                        pe.wait_ge(*turn(gcopied, i, 1))
                        for t in range(T):
                            last = pe.matmul(MB[1][:, t * D:(t + 1) * D], gT[:, t * P:(t + 1) * P], b2[:, :],
                                             start=True, stop=True)
                        last.then_inc(sem(b2out), 1)
                    for f in range(FC):
                        s = act_v if first and f % 2 else act_a
                        pe.wait_ge(*turn(s, i, (e - 1) * FC + (f // 2 * 2 + 2 if first else f + 1) if e else 0))
                        pe.matmul(HB[f][:, :], W1[:, e, f * P:(f + 1) * P], XT[:, :], start=True, stop=True
                                  ).then_inc(sem(hidden), 1)
                    if e >= 1:
                        second(pe, i, e - 1)
                second(pe, i, E - 1)


_HEAD_ROWS_A = [2, 3, 1, 0, 2, 0]
_HEAD_ROWS_B = [3, 1, 2, 3, 0, 1]
_LINE_A = [0, 0, 0, 1, 1, 2]
_LINE_B = [1, 2, 3, 2, 3, 3]


def rotary():
    f = np.float32
    freq = f(1.0) / f(10000.0) ** (np.arange(0, HD, 2, dtype=f) / f(HD))
    angle = np.arange(S, dtype=f)[:, None] * freq[None, :]
    cos = np.tile(np.repeat(np.cos(angle), 2, axis=1), (1, H)).T
    sin = np.tile(np.repeat(np.sin(angle), 2, axis=1) * np.tile(f([-1, 1]), HD // 2), (1, H)).T
    scale = f(1.0) / np.sqrt(f(HD))
    return np.ascontiguousarray(np.stack([cos * scale, sin * scale, cos, sin]).astype(f))


def lay_out(v):
    swap = np.arange(D) ^ 1
    col = lambda a: np.asarray(a).reshape(-1, 1)
    g = {}
    g["x"] = np.asarray(v["L0_attn_x"]).reshape(B * S, D)
    for n in "qkvo":
        g["W" + n] = v["L0_attn_W" + n]
    for n in "qk":
        g[f"W{n}s"] = np.asarray(v["L0_attn_W" + n])[:, swap]
    bq, bk = np.asarray(v["L0_attn_bq"]), np.asarray(v["L0_attn_bk"])
    g["acols"] = np.concatenate([col(bq), col(bq[swap]), col(bk), col(bk[swap]), col(v["L0_attn_g1"]),
                                 col(v["L0_attn_beta1"]), col(v["L0_attn_g2"]), col(v["L0_attn_beta2"])], axis=1)
    g["bv"], g["bo"], g["ab2"] = v["L0_attn_bv"], v["L0_attn_bo"], v["L0_attn_b2"]
    g["aW1"], g["aW2"] = v["L0_attn_W1"], v["L0_attn_W2"]
    g["ab1"] = np.asarray(v["L0_attn_b1"]).reshape(FC, P).T
    g["rope"] = rotary()
    g["L0_w1"] = np.asarray(v["L0_ffn_W1"]).transpose(1, 0, 2)
    g["L0_w2"] = np.asarray(v["L0_ffn_W2"]).reshape(E0, FC, P, D).transpose(2, 0, 1, 3)
    g["L0_b1"] = np.asarray(v["L0_ffn_b1"]).reshape(E0, FC, P).transpose(2, 0, 1)
    g["L0_b2"], g["L0_wr"], g["L0_br"] = v["L0_ffn_b2"], v["L0_ffn_Wr"], v["L0_ffn_br"]
    g["L1_w1"] = np.asarray(v["L1_ffn_w1"]).transpose(2, 0, 1)
    g["L1_w2"] = np.asarray(v["L1_ffn_w2"]).transpose(0, 2, 1).reshape(E1, FC, P, D).transpose(2, 0, 1, 3)
    g["L1_b1"] = np.asarray(v["L1_ffn_b1"]).reshape(E1, FC, P).transpose(2, 0, 1)
    g["L1_b2"], g["L1_wr"] = v["L1_ffn_b2"], np.asarray(v["L1_ffn_router_w"]).T
    heads = np.arange(H)[:, None] * 4
    pick = lambda w, rows: np.asarray(w)[(heads + np.array(rows)[None, :]).reshape(-1), :].T
    g["c_qkv"] = np.asarray(v["L1_attn_w_qkv"]).T
    g["c_wo"] = np.asarray(v["L1_attn_w_out"]).T
    g["c_read"] = np.concatenate([pick(v["L1_attn_w1_read"], _LINE_A), pick(v["L1_attn_w2_read"], _LINE_B),
                                  pick(v["L1_attn_w1_read"], _LINE_B), pick(v["L1_attn_w2_read"], _LINE_A)], axis=1)
    g["c_write1"] = np.concatenate([pick(v["L1_attn_w1_write"], _HEAD_ROWS_A),
                                    pick(v["L1_attn_w1_write"], _HEAD_ROWS_B)], axis=1)
    g["c_write2"] = np.concatenate([pick(v["L1_attn_w2_write"], _HEAD_ROWS_B),
                                    pick(v["L1_attn_w2_write"], _HEAD_ROWS_A)], axis=1)
    bqkv = np.asarray(v["L1_attn_b_qkv"])
    g["c_cols"] = np.stack([bqkv[0:D], bqkv[D:2 * D]], axis=1)
    g["c_bv"], g["c_bo"] = bqkv[2 * D:3 * D], v["L1_attn_b_out"]
    g["c_decay"], g["c_bias"] = v["L1_attn_decay_logits"], v["L1_attn_bias_scale"]
    return {k: np.ascontiguousarray(a) for k, a in g.items()}


def kernel(**inputs):
    import numpy as _np
    import concourse.bacc as _bacc
    from concourse import mybir as _mybir
    from concourse.bass_utils import run_bass_kernel_spmd as _run

    nc = _bacc.Bacc("TRN2", target_bir_lowering=False, num_devices=1)
    laid = lay_out(inputs)
    ins = {n: nc.dram_tensor(f"in_{n}", a.shape, _mybir.dt.from_np(a.dtype), kind="ExternalInput").ap()
           for n, a in laid.items()}
    out = nc.dram_tensor("out_x", (B * S, D), F32, kind="ExternalOutput").ap()
    build(nc, ins, out)
    r = _run(nc, [{f"in_{n}": a for n, a in laid.items()}], core_ids=[0])
    return _np.asarray(r.results[0]["out_x"]).reshape(B, S, D)
```

```python
from contextlib import ExitStack

import numpy as np

import concourse.bass as bass
from concourse import mybir

F32 = mybir.dt.float32
BF16 = mybir.dt.bfloat16
I32 = mybir.dt.int32
ALU = mybir.AluOpType
ACT = mybir.ActivationFunctionType
AX_X = mybir.AxisListType.X

P = 128
D = 128
B, S = 8, 512
T = S // P
H = 16
HD = D // H
QUAD = 4
F = 512
FC = F // P
E0, E1 = 16, 8
EPS = 1e-5
PARTS = 3
PAIRS = PARTS * PARTS
STACK = PAIRS * HD
KR0 = 96


def sem(signal):
    return signal[0]


def per_turn(signal):
    return signal[1]


def turn(signal, i, n):
    return signal[0], i * signal[1] + (n + signal[2])


def over(ap, axis, n):
    shape = list(ap.shape)
    return ap.unsqueeze(axis).to_broadcast(shape[:axis] + [n] + shape[axis:])


def prime(pool, signals):
    for s in signals:
        pool.sem_inc(sem(s), s[2])


def clear(nc, semaphores):
    with nc.Block() as block:
        @block.gpsimd
        def _(pool):
            for s in semaphores:
                pool.sem_clear(s)


def widen(ap, n):
    k = len(ap.shape)
    return ap.unsqueeze(k).to_broadcast(list(ap.shape) + [n])


def build(nc, ins, out, phases="ABCD"):
    ctx = ExitStack()
    with ctx:
        def sb(name, shape, dt=F32):
            return ctx.enter_context(nc.sbuf_tensor(name, shape, dt))

        def dram(name, shape, dt):
            return nc.dram_tensor(name, shape, dt).ap()

        X = sb("X", [P, B * T, D])
        ident = sb("ident", [P, P])
        half = sb("half", [P, T])
        eps = sb("eps", [P, T])
        pad = sb("pad", [P, 1])
        XN = sb("XN", [P, T, D])
        YN = sb("YN", [P, T, D])
        YT = sb("YT", [P, S])
        stat = sb("stat", [P, T, 6])
        mv = sb("mv", [P, T, 2])
        ve = sb("ve", [P, T])
        rstd = sb("rstd", [P, T])
        common = dict(X=X, ident=ident, half=half, eps=eps, pad=pad, XN=XN, YN=YN, YT=YT, stat=stat, mv=mv, ve=ve, rstd=rstd)

        for tag in ("L0", "L1"):
            for name in ("gathered", "scattered"):
                common[f"{tag}_{name}"] = [ctx.enter_context(nc.semaphore(f"{tag}_{name}{u}")) for u in range(4)]
        for name in ("loaded", "made", "stored"):
            common[name] = ctx.enter_context(nc.semaphore(name))
        load_inputs(nc, ins, common)
        if "A" in phases:
            layer0_attention(nc, ins, common)
        if "B" in phases:
            experts(nc, ins, common, "L0", E0)
        if "C" in phases:
            layer1_attention(nc, ins, common)
        if "D" in phases:
            experts(nc, ins, common, "L1", E1)

        stored = common["stored"]
        with nc.Block() as block:
            @block.sync
            def _(sp):
                sp.dma_start(out.rearrange("(n p) d -> p n d", p=P), X[:, :, :]).then_inc(stored, 16)
                sp.wait_ge(stored, 16)


def load_inputs(nc, ins, c):
    loaded, made = c["loaded"], c["made"]
    with nc.Block() as block:
        @block.sync
        def _(sp):
            sp.dma_start(c["X"][:, :, :], ins["x"].rearrange("(n p) d -> p n d", p=P)).then_inc(loaded, 16)
            sp.wait_ge(loaded, 16)

        @block.gpsimd
        def _(pool):
            pool.memset(c["ident"][:, :], 0.0).then_inc(made, 1)
            pool.memset(c["half"][:, :], -0.5)
            pool.memset(c["eps"][:, :], EPS)
            pool.wait_ge(made, 1)
            pool.affine_select(out=c["ident"][:, :], in_=c["ident"][:, :], compare_op=ALU.not_equal, fill=1.0,
                               base=0, pattern=[[-1, P]], channel_multiplier=1)


def spread(rows):
    return rows[:, :].unsqueeze(1).to_broadcast([rows.shape[0], H, S])


def norm_signals(sig, per):
    return {"stats": sig("norm_stats", T * per), "mean": sig("norm_mean", T * per),
            "eps_added": sig("norm_eps_added", per), "rstd": sig("norm_rstd", per), "out": sig("norm_out", T * per)}


def norm_measure(dve, c, norm, i, j, src):
    if j > 0:
        dve.wait_ge(*turn(norm["out"], i, j * T))
    for t in range(T):
        dve.bn_stats(c["stat"][:, t, :], src(t)).then_inc(sem(norm["stats"]), 1)
    dve.wait_ge(*turn(norm["stats"], i, (j + 1) * T))
    dve.memset(c["pad"][:, :], 0.0)
    for t in range(T):
        dve.bn_aggr(c["mv"][:, t, :], c["stat"][:, t, :]).then_inc(sem(norm["mean"]), 1)


def norm_root(pool, c, norm, i, j):
    pool.wait_ge(*turn(norm["mean"], i, (j + 1) * T))
    pool.tensor_tensor(c["ve"][:, :], c["mv"][:, :, 1], c["eps"][:, :], ALU.add).then_inc(sem(norm["eps_added"]), 1)
    pool.wait_ge(*turn(norm["eps_added"], i, j + 1))
    pool.tensor_tensor(c["rstd"][:, :], c["ve"][:, :], c["half"][:, :], ALU.pow).then_inc(sem(norm["rstd"]), 1)


def norm_scale(dve, c, norm, i, j, dst, src):
    dve.wait_ge(*turn(norm["rstd"], i, j + 1))
    for t in range(T):
        dve.tensor_scalar(dst(t), src(t), c["mv"][:, t, 0:1], c["rstd"][:, t:t + 1],
                          ALU.subtract, ALU.mult).then_inc(sem(norm["out"]), 1)


def norm_wait(eng, norm, i, j):
    eng.wait_ge(*turn(norm["out"], i, (j + 1) * T))


def stack_left(sp, stack, row, width, parts_d, signal, head=0):
    for a in range(PARTS):
        rows = PARTS * width
        src = heads_of(parts_d[a].rearrange("(d h) s -> d (h s)", d=width), stack, head)
        sp.dma_start(stack[row + a * rows:row + (a + 1) * rows],
                     src.unsqueeze(0).to_broadcast([PARTS] + list(src.shape))).then_inc(signal, 16)


def heads_of(src, stack, head):
    _, n, columns = stack.shape
    return src[:, head * columns:(head + n) * columns]


def stack_right(sp, stack, row, width, parts_d, signal, head=0):
    src = heads_of(parts_d.rearrange("b (d h) s -> (b d) (h s)", d=width), stack, head)
    sp.dma_start(stack[row:row + PAIRS * width],
                 src.unsqueeze(0).to_broadcast([PARTS] + list(src.shape))).then_inc(signal, 16)


def layer0_attention(nc, ins, c):
    with ExitStack() as ctx:
        def sb(name, shape, dt=F32):
            return ctx.enter_context(nc.sbuf_tensor(name, shape, dt))

        signals, flags = [], []

        def sig(name, per=1, start=1):
            signals.append((ctx.enter_context(nc.semaphore(f"a_{name}")), per, start))
            return signals[-1]

        def flag(name):
            flags.append(ctx.enter_context(nc.semaphore(f"a_{name}")))
            return flags[-1]

        X, XN, YN, YT, ident = c["X"], c["XN"], c["YN"], c["YT"], c["ident"]
        W = sb("a_W", [P, 6, D])
        W1 = sb("a_W1", [P, F])
        W2 = sb("a_W2", [P, FC, D])
        cols = sb("a_cols", [P, 8])
        b1c = sb("a_b1c", [P, FC])
        bv = sb("a_bv", [P, 2, D])
        bo = sb("a_bo", [P, T, D])
        b2 = sb("a_b2", [P, T, D])
        rope = sb("a_rope", [P, 4, S])
        rot = sb("a_rot", [P, 2, 2, S])
        part = sb("a_part", [P, 2, PARTS, S], BF16)
        QS = sb("a_QS", [P, H, S], BF16)
        KS = sb("a_KS", [P, H, S], BF16)
        zero = sb("a_zero", [2, S], BF16)
        one = sb("a_one", [2, S], BF16)
        V = sb("a_V", [P, T, H, 32])
        M = sb("a_M", [P, T, H])
        mh = sb("a_mh", [QUAD, 2, S], BF16)
        ml = sb("a_ml", [QUAD, 2, S], BF16)
        PT = sb("a_PT", [P, 8, 2, S])
        pvs = sb("a_pvs", [P, S])
        rec = sb("a_rec", [P, T, QUAD])
        AT = sb("a_AT", [P, T, D])
        ATT = sb("a_ATT", [P, S])
        XB = sb("a_XB", [P, T, D])
        XA = sb("a_XA", [P, T, D])
        XC = sb("a_XC", [P, T, D])
        ZN = sb("a_ZN", [P, T, D])
        ZT = sb("a_ZT", [P, S])
        hT = sb("a_hT", [P, FC, S])
        tail_c = {name: sb(f"a_t{name}", list(c[name].shape)) for name in ("stat", "mv", "ve", "rstd", "pad")}
        tail_c["eps"], tail_c["half"] = c["eps"], c["half"]
        parts_d = nc.dram_tensor("a_parts", [2, PARTS, P, S], BF16).ap()
        FB = [ctx.enter_context(nc.psum_tensor(f"a_F{n}", [P, S], F32)) for n in range(2)]
        ST = [ctx.enter_context(nc.psum_tensor(f"a_ST{n}", [P, 2, S], F32)) for n in range(2)]
        PV = ctx.enter_context(nc.psum_tensor("a_PV", [P, S], F32))
        TB = ctx.enter_context(nc.psum_tensor("a_TB", [P, S], F32))

        NQ = H // QUAD
        UQ = 2 * QUAD
        UNITS = NQ * UQ
        weights, const, vmade = flag("weights"), flag("const"), flag("vmade")
        norm, tail_norm = norm_signals(sig, 2), norm_signals(lambda name, per: sig("t" + name, per), 1)
        turned, yT = sig("turned"), sig("yT")
        projected, roped = sig("projected", 4), sig("roped", 4)
        valued, vdone = sig("valued", 3), sig("vdone", 3)
        filled, maxed = sig("filled", H * T), sig("maxed", H * T)
        at_turned, attT = sig("at_turned"), sig("attT")
        wo, resid = sig("wo"), sig("resid")
        z_turned, zT = sig("z_turned"), sig("zT")
        hidden, relu_a, relu_v = sig("hidden", FC), sig("relu_a", FC // 2), sig("relu_v", FC // 2)
        ffn, summed_up = sig("ffn"), sig("summed_up", 1)
        summed, cast, rest = sig("summed", 2), sig("cast", 4), sig("rest", 4)
        q_stored, k_stored = sig("q_stored", 16), sig("k_stored", 16)
        stacked = [sig(f"stacked{g}", 16 * (PARTS + 2)) for g in range(NQ)]
        mturned, mparts = sig("mturned", NQ), sig("mparts", 2 * NQ)
        mstacked = sig("mstacked", 32 * NQ, 33)
        scored, exped = sig("scored", UNITS), sig("exped", UNITS, 2)
        pv, pvcopied, pvturned = sig("pv", 2 * NQ, 2), sig("pvcopied", NQ), sig("pvturned", NQ)
        inv, attn = sig("inv", NQ), sig("attn", NQ, 2)
        passed = sig("passed", NQ + 2)
        biased, biased2, added = sig("biased"), sig("biased2"), sig("added")

        V_FILLS = [(0, 2), (2, 1), (3, 1)]
        readers = {"turned": (yT, lambda n: 1), "projected": (roped, lambda n: n + 1),
                   "valued": (vdone, lambda n: n + 1), "logits": (maxed, lambda n: n + 1),
                   "at": (attT, lambda n: 1), "wo": (resid, lambda n: 1), "z": (zT, lambda n: 1),
                   "hidden": (None, None), "ffn": (summed_up, lambda n: 1)}
        EXTRA = {0: [("at", -1, 0)], 2: [("wo", -1, 0)], 5: [("turned", 1, 0)],
                 7: [("projected", 1, 0)], 8: [("projected", 1, 1)], 9: [("projected", 1, 2)],
                 10: [("projected", 1, 3)], 12: [("z", -1, 0)],
                 14: [("hidden", -1, 0)], 15: [("hidden", -1, 1)], 16: [("hidden", -1, 2)],
                 17: [("hidden", -1, 3)], 20: [("ffn", -1, 0)]}

        def extras(u, tail, prep):
            return [use for use in EXTRA.get(u, []) if (tail if use[1] < 0 else prep)]

        def table(uses, before):
            before = [(kind, batch - 1, n) for kind, batch, n in before[-2:]]
            assert len(uses) % 2 == 0
            return {use: (n % 2, (before + uses)[n]) for n, use in enumerate(uses)}

        def uses_of(tail, prep):
            uses = []
            for u in range(UNITS):
                if u < UNITS - UQ:
                    uses += [("logits", 0, QUAD * T + 2 * u), ("logits", 0, QUAD * T + 2 * u + 1)]
                elif prep:
                    uses += [("logits", 1, 2 * (u - UNITS + UQ)), ("logits", 1, 2 * (u - UNITS + UQ) + 1)]
                uses += extras(u, tail, prep)
            return uses + ([("valued", 1, n) for n in range(3)] if prep else [])

        OPENING = ([("turned", 1, 0)] + [("projected", 1, n) for n in range(4)] + [("logits", 1, n) for n in range(16)]
                   + [("valued", 1, n) for n in range(3)])
        CLOSING = [use for u in range(UNITS) for use in extras(u, True, False)]
        opening = table(OPENING, [("turned", 1, 0)] * 2)
        first_turn = table(uses_of(False, True), OPENING)
        middle = table(uses_of(True, True), uses_of(False, True))
        last_turn = table(uses_of(True, False), uses_of(True, True))
        closing = table(CLOSING, uses_of(True, False))

        def turns(eng, run):
            run(0, False, True, first_turn)
            with eng.Fori(1, B - 1) as i:
                run(i, True, True, middle)
            run(B - 1, True, False, last_turn)

        def bank(tab, use):
            return FB[tab[use][0]]

        block_weights = 16 * 22
        ctx.callback(clear, nc, [sem(s) for s in signals] + flags)
        block = ctx.enter_context(nc.Block())

        @block.sync
        def _(sp):
            for n, name in enumerate(["Wq", "Wqs", "Wk", "Wks", "Wv", "Wo"]):
                sp.dma_start(W[:, n, :], ins[name]).then_inc(weights, 16)
            sp.dma_start(W1[:, :], ins["aW1"]).then_inc(weights, 16)
            sp.dma_start(W2[:, :, :], ins["aW2"].rearrange("(c p) d -> p c d", p=P)).then_inc(weights, 16)
            sp.dma_start(cols[:, :], ins["acols"]).then_inc(weights, 16)
            sp.dma_start(b1c[:, :], ins["ab1"]).then_inc(weights, 16)
            sp.dma_start(rope[:, :, :], ins["rope"].rearrange("c p s -> p c s")).then_inc(weights, 16)
            for t in range(T):
                if t < 2:
                    sp.dma_start(bv[:, t, :], ins["bv"].partition_broadcast(P)).then_inc(weights, 16)
                sp.dma_start(bo[:, t, :], ins["bo"].partition_broadcast(P)).then_inc(weights, 16)
                sp.dma_start(b2[:, t, :], ins["ab2"].partition_broadcast(P)).then_inc(weights, 16)
            sp.wait_ge(const, 4)
            sp.dma_start(KS[STACK:STACK + 2, :, :], spread(one)).then_inc(weights, 16)
            sp.wait_ge(weights, block_weights)

            def store_parts(i):
                for g in range(NQ):
                    sp.wait_ge(*turn(stacked[g], i, 0))
                    sp.sem_inc(sem(passed), 1)
                for z, stored in enumerate((q_stored, k_stored)):
                    sp.wait_ge(*turn(rest, i, 2 * z + 2))
                    sp.dma_start(parts_d[z].rearrange("a p s -> p a s"), part[:, z, :, :]).then_inc(sem(stored), 16)
                for stored in (q_stored, k_stored):
                    sp.wait_ge(*turn(stored, i, 16))
                    sp.sem_inc(sem(passed), 1)

            def stack(i, g):
                hs = slice(QUAD * g, QUAD * g + QUAD)
                sp.wait_ge(*turn(scored, i - 1, UQ * (g + 1)) if not isinstance(i, int) or i > 0 else (const, 4))
                sp.dma_start(QS[STACK:STACK + 2, hs, :], zero[:, :].unsqueeze(1).to_broadcast([2, QUAD, S])
                             ).then_inc(sem(stacked[g]), 16)
                stack_left(sp, QS[:, hs, :], 0, HD, parts_d[0], sem(stacked[g]), QUAD * g)
                stack_right(sp, KS[:, hs, :], 0, HD, parts_d[1], sem(stacked[g]), QUAD * g)

            def stack_max(i, g):
                sp.wait_ge(*turn(mparts, i, 2 * g + 2))
                for n, m in enumerate((mh, ml)):
                    sp.dma_start(QS[STACK + n:STACK + n + 1, QUAD * g:QUAD * g + QUAD, :], m[:, g % 2, :]
                                 ).then_inc(sem(mstacked), 16)

            store_parts(0)
            for g in range(NQ):
                stack(0, g)
            stack_max(0, 0)

            def run(i, tail, prep, tab):
                stack_max(i, 1)
                if prep:
                    store_parts(i + 1)
                stack_max(i, 2)
                if prep:
                    stack(i + 1, 0)
                    stack(i + 1, 1)
                stack_max(i, 3)
                if prep:
                    stack(i + 1, 2)
                    stack_max(i + 1, 0)
                    stack(i + 1, 3)

            turns(sp, run)
            sp.wait_ge(*turn(mstacked, B, 0 - 32))

        @block.gpsimd
        def _(pool):
            prime(pool, signals)
            pool.memset(zero[:, :], 0.0).then_inc(const, 1)
            pool.memset(one[:, :], 1.0).then_inc(const, 1)
            pool.wait_ge(weights, block_weights)

            def split(i):
                for z in range(2):
                    pool.wait_ge(*turn(roped, i, 2 * z + 2))
                    pool.tensor_tensor(rot[:, z, 0, :], rot[:, z, 0, :], rot[:, z, 1, :], ALU.add
                                       ).then_inc(sem(summed), 1)
                    pool.wait_ge(*turn(cast, i, 2 * z + 1))
                    pool.tensor_tensor(rot[:, z, 1, :], rot[:, z, 0, :], part[:, z, 0, :], ALU.subtract
                                       ).then_inc(sem(rest), 1)
                    pool.wait_ge(*turn(cast, i, 2 * z + 2))
                    pool.tensor_tensor(part[:, z, 2, :], rot[:, z, 1, :], part[:, z, 1, :], ALU.subtract
                                       ).then_inc(sem(rest), 1)

            def bias_tokens(i):
                norm_wait(pool, norm, i, 0)
                pool.wait_ge(*turn(resid, i, 0))
                pool.tensor_tensor(XB[:, :, :], XN[:, :, :], bo[:, :, :], ALU.add).then_inc(sem(biased), 1)

            def bias_more(i):
                pool.wait_ge(*turn(resid, i, 1))
                pool.wait_ge(*turn(summed_up, i, 0))
                pool.tensor_tensor(XC[:, :, :], XA[:, :, :], b2[:, :, :], ALU.add).then_inc(sem(biased2), 1)

            norm_root(pool, c, norm, 0, 0)
            norm_root(pool, c, norm, 0, 1)
            split(0)

            def run(i, tail, prep, tab):
                if prep:
                    norm_root(pool, c, norm, i + 1, 0)
                bias_tokens(i)
                if tail:
                    norm_root(pool, tail_c, tail_norm, i - 1, 0)
                if prep:
                    norm_root(pool, c, norm, i + 1, 1)
                if tail:
                    bias_more(i - 1)
                if prep:
                    split(i + 1)

            turns(pool, run)
            norm_root(pool, tail_c, tail_norm, B - 1, 0)
            bias_more(B - 1)

        @block.scalar
        def _(act):
            act.wait_ge(weights, block_weights)

            def features(i, tab):
                act.wait_ge(*turn(turned, i, 1))
                act.wait_ge(*turn(vdone, i, 0))
                act.activation(YT[:, :], bank(tab, ("turned", 1, 0))[:, :], ACT.Identity, scale=cols[:, 4:5],
                               bias=cols[:, 5:6]).then_inc(sem(yT), 1)

            def split(i, z, n):
                if n == 0:
                    act.wait_ge(*turn(summed, i, z + 1))
                    act.wait_ge(*turn((q_stored, k_stored)[z], i, 0))
                    act.activation(part[:, z, 0, :], rot[:, z, 0, :], ACT.Copy).then_inc(sem(cast), 1)
                else:
                    act.wait_ge(*turn(rest, i, 2 * z + 1))
                    act.activation(part[:, z, 1, :], rot[:, z, 1, :], ACT.Copy).then_inc(sem(cast), 1)

            def minus_max(i, g):
                act.wait_ge(*turn(mturned, i, g + 1))
                act.wait_ge(*turn(mstacked, i, 32 * (g - 1)))
                act.activation(mh[:, g % 2, :], TB[0:QUAD, :], ACT.Copy, scale=-1.0).then_inc(sem(mparts), 1)

            def tail_at(i, tab):
                act.wait_ge(*turn(at_turned, i, 1))
                act.activation(ATT[:, :], bank(tab, ("at", -1, 0))[:, :], ACT.Copy).then_inc(sem(attT), 1)

            def tail_z(i, tab):
                act.wait_ge(*turn(z_turned, i, 1))
                act.activation(ZT[:, :], bank(tab, ("z", -1, 0))[:, :], ACT.Identity, scale=cols[:, 6:7],
                               bias=cols[:, 7:8]).then_inc(sem(zT), 1)

            def tail_relu(i, tab, f):
                act.wait_ge(*turn(hidden, i, f + 1))
                act.wait_ge(*turn(ffn, i, 0))
                act.activation(hT[:, f, :], bank(tab, ("hidden", -1, f))[:, :], ACT.Relu, bias=b1c[:, f:f + 1]
                               ).then_inc(sem(relu_a), 1)

            def tail_step(u, i, tab):
                if u == 0:
                    tail_at(i, tab)
                if u == 12:
                    tail_z(i, tab)
                if u in (14, 16):
                    tail_relu(i, tab, u - 14)

            def prep_step(u, i, tab):
                if u == 5:
                    features(i, tab)
                if u in (9, 10, 12, 13):
                    split(i, (u - 9) // 3, (u - 9) % 3)

            for u in range(UNITS):
                prep_step(u, 0, opening)
            minus_max(0, 0)

            def run(i, tail, prep, tab):
                for u in range(UNITS):
                    act.wait_ge(*turn(scored, i, u + 1))
                    act.wait_ge(*turn(pv, i, u // QUAD - 1))
                    act.activation(PT[:, u % 8, :, :], ST[u % 2][:, :, :], ACT.Exp).then_inc(sem(exped), 1)
                    if tail:
                        tail_step(u, i - 1, tab)
                    if prep:
                        prep_step(u, i + 1, tab)
                    if u % UQ == UQ - 1 and (prep or u < UNITS - UQ):
                        minus_max(i + (u + 1) // UNITS, (u // UQ + 1) % NQ)

            turns(act, run)
            for u in range(UNITS):
                tail_step(u, B - 1, closing)

        @block.vector
        def _(dve):
            dve.memset(QS[64:96, :, :], 0.0).then_inc(const, 1)
            dve.memset(KS[64:96, :, :], 0.0).then_inc(const, 1)
            dve.memset(V[:, :, :, :], 0.0).then_inc(vmade, 1)
            dve.wait_ge(vmade, 1)
            dve.memset(V[:, :, :, HD:HD + 1], 1.0).then_inc(vmade, 1)
            dve.wait_ge(weights, block_weights)
            dve.wait_ge(vmade, 2)

            def x_tile(i, t):
                return X[:, bass.ds(i * T + t, 1), :].rearrange("p a d -> p (a d)")

            def rotate(i, n, tab):
                dve.wait_ge(*turn(projected, i, n + 1))
                dve.wait_ge(*turn(rest, i, 0))
                dve.scalar_tensor_tensor(rot[:, n // 2, n % 2, :], bank(tab, ("projected", 1, n))[:, :], cols[:, n:n + 1],
                                         rope[:, n, :], ALU.add, ALU.mult).then_inc(sem(roped), 1)

            def prep_step(u, i, tab):
                if u == 0:
                    norm_measure(dve, c, norm, i, 0, lambda t: x_tile(i, t))
                if u == 3:
                    dve.wait_ge(*turn(biased, i, 0))
                    norm_scale(dve, c, norm, i, 0, lambda t: XN[:, t, :], lambda t: x_tile(i, t))
                    norm_wait(dve, norm, i, 0)
                    norm_measure(dve, c, norm, i, 1, lambda t: XN[:, t, :])
                if u == 4:
                    norm_scale(dve, c, norm, i, 1, lambda t: YN[:, t, :], lambda t: XN[:, t, :])
                if u in (7, 8, 9, 10):
                    rotate(i, u - 7, tab)

            def values(i, tab):
                for n, (t, count) in enumerate(V_FILLS):
                    dve.wait_ge(*turn(valued, i, n + 1))
                    dve.wait_ge(*turn(pv, i, 0))
                    dve.tensor_tensor(V[:, t:t + count, :, 0:HD],
                                      bank(tab, ("valued", 1, n))[:, 0:count * D].rearrange("p (t h d) -> p t h d",
                                                                                            t=count, d=HD),
                                      bv[:, 0:count, :].rearrange("p t (h d) -> p t h d", d=HD), ALU.add
                                      ).then_inc(sem(vdone), 1)

            def tail_step(u, i, tab):
                if u == 2:
                    dve.wait_ge(*turn(wo, i, 1))
                    dve.wait_ge(*turn(biased, i, 1))
                    dve.wait_ge(*turn(biased2, i, 0))
                    dve.tensor_tensor(XA[:, :, :], bank(tab, ("wo", -1, 0))[:, :].rearrange("p (t d) -> p t d", d=D),
                                      XB[:, :, :], ALU.add).then_inc(sem(resid), 1)
                    dve.wait_ge(*turn(resid, i, 1))
                    norm_measure(dve, tail_c, tail_norm, i, 0, lambda t: XA[:, t, :])
                if u == 11:
                    norm_scale(dve, tail_c, tail_norm, i, 0, lambda t: ZN[:, t, :], lambda t: XA[:, t, :])
                if u in (15, 17):
                    f = u - 14
                    dve.wait_ge(*turn(hidden, i, f + 1))
                    dve.wait_ge(*turn(ffn, i, 0))
                    dve.tensor_scalar(hT[:, f, :], bank(tab, ("hidden", -1, f))[:, :], b1c[:, f:f + 1], 0.0,
                                      ALU.add, ALU.max).then_inc(sem(relu_v), 1)
                if u == 20:
                    dve.wait_ge(*turn(ffn, i, 1))
                    dve.wait_ge(*turn(biased2, i, 1))
                    dve.tensor_tensor(XC[:, :, :], bank(tab, ("ffn", -1, 0))[:, :].rearrange("p (t d) -> p t d", d=D),
                                      XC[:, :, :], ALU.add).then_inc(sem(summed_up), 1)
                    dve.wait_ge(*turn(summed_up, i, 1))
                    xb = X[:, bass.ds(i * T, T), :]
                    dve.tensor_tensor(xb, xb, XC[:, :, :], ALU.add).then_inc(sem(added), 1)

            def maximum(i, n, tab, batch):
                h, t = n // T, n % T
                dve.wait_ge(*turn(filled, i, n + 1))
                dve.tensor_reduce(M[:, t, h:h + 1], bank(tab, ("logits", batch, n))[:, :], AX_X, ALU.max
                                  ).then_inc(sem(maxed), 1)

            def minus_max(i, g):
                dve.wait_ge(*turn(mparts, i, 2 * g + 1))
                dve.scalar_tensor_tensor(ml[:, g % 2, :], TB[0:QUAD, :], -1.0, mh[:, g % 2, :], ALU.mult,
                                         ALU.subtract).then_inc(sem(mparts), 1)

            for u in range(UNITS):
                prep_step(u, 0, opening)
            for n in range(QUAD * T):
                maximum(0, n, opening, 1)
            values(0, opening)
            minus_max(0, 0)

            def run(i, tail, prep, tab):
                for u in range(UNITS):
                    g = u // UQ
                    for n in (2 * u, 2 * u + 1):
                        if g < NQ - 1:
                            maximum(i, QUAD * T + n, tab, 0)
                        elif prep:
                            maximum(i + 1, n - 2 * (UNITS - UQ), tab, 1)
                    if tail:
                        tail_step(u, i - 1, tab)
                    if prep:
                        prep_step(u, i + 1, tab)
                    if u % UQ < UQ - 1:
                        continue
                    if g < NQ - 1 or prep:
                        minus_max(i + (g + 1) // NQ, (g + 1) % NQ)
                    dve.wait_ge(*turn(pv, i, 2 * g + 2))
                    dve.wait_ge(*turn(pvturned, i, g))
                    dve.tensor_copy(pvs[:, :], PV[:, :]).then_inc(sem(pvcopied), 1)
                    dve.wait_ge(*turn(pvturned, i, g + 1))
                    heads = TB[:, :].rearrange("p (t j e) -> p t j e", t=T, e=32)
                    dve.wait_ge(*turn(attn, i, g))
                    dve.reciprocal(rec[:, :, :], heads[:, :, :, HD]).then_inc(sem(inv), 1)
                    dve.wait_ge(*turn(inv, i, g + 1))
                    dve.wait_ge(*turn(at_turned, i, 0))
                    dve.tensor_tensor(AT[:, :, 32 * g:32 * g + 32].rearrange("p t (j e) -> p t j e", e=HD),
                                      heads[:, :, :, 0:HD], widen(rec[:, :, :], HD), ALU.mult).then_inc(sem(attn), 1)
                if prep:
                    values(i + 1, tab)

            turns(dve, run)
            for u in range(UNITS):
                tail_step(u, B - 1, closing)
            dve.wait_ge(*turn(added, B, 0))

        @block.tensor
        def _(pe):
            pe.wait_ge(weights, block_weights)
            pe.wait_ge(vmade, 2)

            def front(tab, use, i):
                kind, batch, n = tab[use][1]
                if kind == "hidden":
                    done = turn(relu_v if n % 2 else relu_a, i + batch, n // 2 + 1)
                else:
                    done = turn(readers[kind][0], i + batch, readers[kind][1](n))
                if tab is not opening or list(tab).index(use) >= 2:
                    pe.wait_ge(*done)
                return bank(tab, use)

            def prep_step(use, i, tab):
                kind, _, n = use
                if kind == "turned":
                    norm_wait(pe, norm, i + 1, 1)
                    f = front(tab, use, i)
                    for t in range(T):
                        last = pe.transpose(f[:, t * P:(t + 1) * P], YN[:, t, :], ident[:, :])
                    last.then_inc(sem(turned), 1)
                elif kind == "projected":
                    if n == 0:
                        pe.wait_ge(*turn(yT, i + 1, 1))
                    f = front(tab, use, i)
                    pe.matmul(f[:, :], W[:, n, :], YT[:, :], start=True, stop=True).then_inc(sem(projected), 1)

            def prep_values(i, tab):
                for n, (t0, count) in enumerate(V_FILLS):
                    f = front(tab, ("valued", 1, n), i)
                    for t in range(t0, t0 + count):
                        last = pe.matmul(f[:, (t - t0) * D:(t - t0 + 1) * D], YT[:, t * P:(t + 1) * P], W[:, 4, :],
                                         start=True, stop=True)
                    last.then_inc(sem(valued), 1)

            def tail_step(use, i, tab):
                kind, _, n = use
                b = i - 1
                if kind == "at":
                    pe.wait_ge(*turn(attn, b, NQ))
                    f = front(tab, use, i)
                    for t in range(T):
                        last = pe.transpose(f[:, t * P:(t + 1) * P], AT[:, t, :], ident[:, :])
                    last.then_inc(sem(at_turned), 1)
                elif kind == "wo":
                    pe.wait_ge(*turn(attT, b, 1))
                    f = front(tab, use, i)
                    for t in range(T):
                        last = pe.matmul(f[:, t * D:(t + 1) * D], ATT[:, t * P:(t + 1) * P], W[:, 5, :],
                                         start=True, stop=True)
                    last.then_inc(sem(wo), 1)
                elif kind == "z":
                    norm_wait(pe, tail_norm, b, 0)
                    f = front(tab, use, i)
                    for t in range(T):
                        last = pe.transpose(f[:, t * P:(t + 1) * P], ZN[:, t, :], ident[:, :])
                    last.then_inc(sem(z_turned), 1)
                elif kind == "hidden":
                    pe.wait_ge(*turn(zT, b, 1))
                    f = front(tab, use, i)
                    pe.matmul(f[:, :], W1[:, n * P:(n + 1) * P], ZT[:, :], start=True, stop=True).then_inc(sem(hidden), 1)
                else:
                    pe.wait_ge(*turn(relu_a, b, FC // 2))
                    pe.wait_ge(*turn(relu_v, b, FC // 2))
                    f = front(tab, use, i)
                    for t in range(T):
                        for k in range(FC):
                            last = pe.matmul(f[:, t * D:(t + 1) * D], hT[:, k, t * P:(t + 1) * P], W2[:, k, :],
                                             start=(k == 0), stop=(k == FC - 1))
                    last.then_inc(sem(ffn), 1)

            def logits(i, tab, batch, n):
                h, t = n // T, n % T
                if n % (QUAD * T) == 0:
                    pe.wait_ge(*turn(stacked[h // QUAD], i + batch, 16 * (PARTS + 2)))
                f = front(tab, ("logits", batch, n), i)
                pe.matmul(f[:, :], QS[0:KR0, h, t * P:(t + 1) * P], KS[0:KR0, h, :],
                          start=True, stop=True).then_inc(sem(filled), 1)

            def turn_max(i, g):
                pe.wait_ge(*turn(maxed, i, QUAD * T * (g + 1)))
                pe.wait_ge(*turn(attn, i, g - 1))
                for t in range(T):
                    last = pe.transpose(TB[0:QUAD, t * P:(t + 1) * P], M[:, t, QUAD * g:QUAD * g + QUAD], ident[:, :])
                last.then_inc(sem(mturned), 1)

            def values(i, w):
                pe.wait_ge(*turn(exped, i, QUAD * w + QUAD))
                if w == 0:
                    pe.wait_ge(*turn(vdone, i, 3))
                if w % 2 == 0:
                    pe.wait_ge(*turn(pvcopied, i, w // 2))
                for kk in range(2):
                    for j in range(QUAD):
                        kt = 2 * (w % 2) + kk
                        last = pe.matmul(PV[32 * j:32 * j + 32, :], V[:, kt, QUAD * (w // 2) + j, :],
                                         PT[:, (QUAD * w + j) % 8, kk, :], start=(kt == 0), stop=(kt == T - 1))
                last.then_inc(sem(pv), 1)

            def turn_values(i, g, more):
                pe.wait_ge(*turn(pvcopied, i, g + 1))
                pe.wait_ge(*turn(attn, i, g))
                pe.wait_ge(*turn(mparts, i, 2 * (g + 2 if more else NQ)))
                for t in range(T):
                    last = pe.transpose(TB[:, t * P:(t + 1) * P], pvs[:, t * P:(t + 1) * P], ident[:, :])
                last.then_inc(sem(pvturned), 1)

            def scores(i, u):
                w, j = u // QUAD, u % QUAD
                h = QUAD * (w // 2) + j
                if u % UQ == 0:
                    pe.wait_ge(*turn(mstacked, i, 32 * (w // 2 + 1)))
                pe.wait_ge(*turn(exped, i, u - 1))
                for kk in range(2):
                    kt = 2 * (w % 2) + kk
                    last = pe.matmul(ST[u % 2][:, kk, :], KS[0:KR0, h, kt * P:(kt + 1) * P], QS[0:KR0, h, :],
                                     start=True, stop=True)
                last.then_inc(sem(scored), 1)

            for use in OPENING[0:5]:
                prep_step(use, -1, opening)
            for n in range(QUAD * T):
                logits(-1, opening, 1, n)
            turn_max(0, 0)
            prep_values(-1, opening)

            def run(i, tail, prep, tab):
                for u in range(UNITS):
                    g = u // UQ
                    scores(i, u)
                    for n in (2 * u, 2 * u + 1):
                        if g < NQ - 1:
                            logits(i, tab, 0, QUAD * T + n)
                        elif prep:
                            logits(i, tab, 1, n - 2 * (UNITS - UQ))
                    for use in extras(u, tail, prep):
                        (tail_step if use[1] < 0 else prep_step)(use, i, tab)
                    if u % UQ == QUAD + 1:
                        values(i, 2 * g)
                    if u % UQ == UQ - 1:
                        more = prep or g < NQ - 1
                        if more:
                            turn_max(i + (g + 1) // NQ, (g + 1) % NQ)
                        values(i, 2 * g + 1)
                        turn_values(i, g, more)
                if prep:
                    prep_values(i, tab)

            turns(pe, run)
            for use in CLOSING:
                tail_step(use, B, closing)


PAST = 6
LINES = H * PAST
QC = S + S // 2 + P
IR = STACK
KR1 = 128
MR = KR1 - 2
NEG = -1.0e30


def layer1_attention(nc, ins, c):
    with ExitStack() as ctx:
        def sb(name, shape, dt=F32):
            return ctx.enter_context(nc.sbuf_tensor(f"c_{name}", shape, dt))

        signals, flags = [], []

        def sig(name, per=1, start=1):
            signals.append((ctx.enter_context(nc.semaphore(f"c_{name}")), per, start))
            return signals[-1]

        def flag(name):
            flags.append(ctx.enter_context(nc.semaphore(f"c_{name}")))
            return flags[-1]

        X, XN, ident = c["X"], c["XN"], c["ident"]
        WQ = sb("WQ", [P, 3 * D])
        WO = sb("WO", [P, D])
        WR = sb("WR", [P, 4 * LINES])
        WW = sb("WW", [P, 2, 2 * LINES])
        cols = sb("cols", [P, 2])
        bv = sb("bv", [P, D])
        bo = sb("bo", [P, D])
        XT = sb("XT", [P, S + 1])
        dec = sb("dec", [P, 4, H])
        bias = sb("bias", [P, H])
        ramp = sb("ramp", [P, P + 4])
        table_of_decays = sb("table", [P, H, P])
        expo = sb("expo", [P, 4, H])
        DQ = sb("DQ", [P, 4, H])
        mask = sb("mask", [P, P], BF16)
        identb = sb("identb", [P, P], BF16)
        only = sb("only", [P, P], BF16)
        zero = sb("zero", [2, QC], BF16)
        one = sb("one", [2, S], BF16)
        part = sb("part", [P, 2, PARTS, S], BF16)
        rn = sb("rn", [P, 3, T * H])
        qk = sb("qk", [P, 2, S])
        rem = sb("rem", [P, 2, S])
        QS = sb("QS", [P, H, QC], BF16)
        KS = sb("KS", [P, H, S], BF16)
        QI = sb("QI", [PAIRS * PAST, H, S], BF16)
        KI = sb("KI", [PAIRS * PAST, H, S], BF16)
        V = sb("V", [P, T, H, 32])
        inc = sb("inc", [P, S])
        SD = sb("SD", [P, 2, QUAD, T, P])
        MD = sb("MD", [P, T, H])
        M = sb("M", [P, T, H])
        mh = sb("mh", [QUAD, 2, S], BF16)
        ml = sb("ml", [QUAD, 2, S], BF16)
        PT = sb("PT", [P, QUAD + 1, 2, S])
        LP = sb("LP", [P, T, 4 * LINES])
        prod = sb("prod", [P, 2, T, LINES])
        line = sb("line", [P, 2, T, LINES])
        flat = LP[:, :, :].rearrange("p t n -> p (t n)")
        LQ = flat[:, 0:6 * LINES].rearrange("p (t n) -> p t n", n=LINES)
        LK = flat[:, 6 * LINES:(6 + T) * LINES].rearrange("p (t n) -> p t n", n=LINES)
        pvs = sb("pvs", [P, S])
        rec = sb("rec", [P, T, QUAD])
        AT = sb("AT", [P, T, D])
        ATT, XB = c["YT"], c["YN"]
        q_d = nc.dram_tensor("c_q", [PARTS, P, QC], BF16).ap()
        k_d = nc.dram_tensor("c_k", [PARTS, P, S], BF16).ap()
        r_d = nc.dram_tensor("c_r", [PARTS, LINES, S], BF16).ap()
        w_d = nc.dram_tensor("c_w", [PARTS, LINES, S], BF16).ap()
        rd_d = nc.dram_tensor("c_rd", [PARTS, LINES, QC], BF16).ap()
        wd_d = nc.dram_tensor("c_wd", [PARTS, LINES, S], BF16).ap()
        FB = [ctx.enter_context(nc.psum_tensor(f"c_F{n}", [P, S], F32)) for n in range(4)]
        ST = ctx.enter_context(nc.psum_tensor("c_ST", [P, 2, S], F32))
        PV = ctx.enter_context(nc.psum_tensor("c_PV", [P, S], F32))
        TB = ctx.enter_context(nc.psum_tensor("c_TB", [P, S], F32))

        NQ = H // QUAD
        UQ = QUAD + 1
        UNITS = UQ * NQ
        STACKS = 1 + 3 * PARTS + 3
        SPANS = [(0, 0, S), (S, 2 * P, S), (S + 2 * P, 3 * P, S)]

        weights, made, table_made = flag("weights"), flag("made"), flag("table_made")
        made2 = flag("made2")
        minus_half = sb("minus_half", [P, T * H])
        norm = norm_signals(sig, 1)
        turned, xT = sig("turned"), sig("xT")
        made_qk, projected = sig("made_qk", 2), sig("projected", 2)
        cast, rest = sig("cast", 4), sig("rest", 4)
        valued, vdone = sig("valued", 2), sig("vdone", 2)
        pointed, points = sig("pointed", 8), sig("points", 8)
        product, crossed, squared = sig("product", 4), sig("crossed", 2), sig("squared", 2)
        summed, normed, unit, scaled = sig("summed", 4), sig("normed", 2), sig("unit", 2), sig("scaled", 1)
        decayed = sig("decayed", 4)
        lined = sig("lined", 5)
        lcast, lrest, lthird = sig("lcast", 10), sig("lrest", 5), sig("lthird", 5)
        stored = [sig("stored0", 16 * 6), sig("stored1", 16 * 3)]
        stacked = [sig(f"stacked{g}", 16 * STACKS) for g in range(NQ)]
        passed = sig("passed", NQ + 2)
        logit, maxed = sig("logit", 4 * H), sig("maxed", 4 * H)
        inc_decayed, diag = sig("inc_decayed", H), sig("diag", H)
        mjoined, mturned, mparts = sig("mjoined", NQ), sig("mturned", NQ), sig("mparts", 2 * NQ)
        mstacked = sig("mstacked", 16 * 6 * NQ, 16 * 6 + 1)
        scored, exped = sig("scored", UQ * NQ, UQ + 1), sig("exped", UQ * NQ)
        pv, pvcopied, pvturned, inv = sig("pv", NQ), sig("pvcopied", NQ), sig("pvturned", NQ), sig("inv", NQ)
        attn = sig("attn", NQ, 2)
        at_turned, attT, wo, biased, added = sig("at_turned"), sig("attT"), sig("wo"), sig("biased"), sig("added")
        NW = 10 + 1 + 1 + 1

        readers = {"turned": (xT, lambda n: 1), "qk": (projected, lambda n: n + 1), "v": (vdone, lambda n: n + 1),
                   "points": (points, lambda n: n + 1), "line": (lrest, lambda n: n + 1),
                   "inc": (inc_decayed, lambda n: n + 1), "diag": (diag, lambda n: n + 1),
                   "past31": (maxed, lambda n: 4 * n + 2), "past2": (maxed, lambda n: 4 * n + 3),
                   "at": (attT, lambda n: 1), "wo": (added, lambda n: 1)}
        banks = {"turned": 0, "qk": 1, "v": 2, "points": 0, "line": 1, "inc": 0, "diag": 1, "past31": 2, "past2": 3,
                 "at": 2, "wo": 3}
        EXTRA = {0: [("at", -1, 0)], 1: [("wo", -1, 0), ("turned", 1, 0)], 2: [("qk", 1, 0), ("qk", 1, 1)],
                 3: [("points", 1, 0), ("points", 1, 1), ("points", 1, 2), ("points", 1, 3)],
                 4: [("points", 1, 4), ("points", 1, 5)],
                 5: [("points", 1, 6), ("points", 1, 7)],
                 9: [("line", 1, 0), ("line", 1, 1)], 10: [("line", 1, 2), ("line", 1, 3)], 11: [("line", 1, 4)]}
        CASTS = (2, 3)
        SUMS = (5, 7)
        DECAY_AT = 8
        LINE_AT = (9, 9, 10, 10, 11)
        HEAD = ("inc", "diag", "past31", "past2")

        def extras(u, tail, prep):
            return [use for use in EXTRA.get(u, []) if (tail if use[1] < 0 else prep)]

        def next_head(u, prep):
            g, j = u // UQ, u % UQ
            if j == QUAD or (g == NQ - 1 and not prep):
                return None
            return (1 if g == NQ - 1 else 0), ((g + 1) % NQ) * QUAD + j

        def table(uses, before):
            last, tab = {}, {}
            for kind, batch, n in before:
                last[banks_of(kind, n)] = (kind, batch - 1, n)
            for use in uses:
                b = banks_of(use[0], use[2])
                tab[use] = (b, last.get(b))
                last[b] = use
            return tab

        def banks_of(kind, n):
            return banks[kind] if kind in HEAD else (banks[kind] + n) % 4

        def uses_of(tail, prep):
            uses = []
            for u in range(UNITS):
                if next_head(u, prep):
                    batch, h = next_head(u, prep)
                    uses += [(kind, batch, h) for kind in HEAD]
                uses += extras(u, tail, prep)
            return uses + ([("v", 1, n) for n in range(2)] if prep else [])

        OPENING = ([use for u in range(UNITS) for use in extras(u, False, True)]
                   + [(kind, 1, h) for h in range(QUAD) for kind in HEAD] + [("v", 1, n) for n in range(2)])
        CLOSING = [use for u in range(UNITS) for use in extras(u, True, False)]
        opening = table(OPENING, [])
        first_turn = table(uses_of(False, True), OPENING)
        middle = table(uses_of(True, True), uses_of(False, True))
        last_turn = table(uses_of(True, False), uses_of(True, True))
        closing = table(CLOSING, uses_of(True, False))

        def turns(eng, run):
            run(0, False, True, first_turn)
            with eng.Fori(1, B - 1) as i:
                run(i, True, True, middle)
            run(B - 1, True, False, last_turn)

        def bank(tab, use):
            return FB[tab[use][0]]

        def view(dst):
            return dst.rearrange("p (h e) -> p h e", e=PAST)

        PIECES = [(r_d, 0, S), (w_d, 0, S), (wd_d, 0, S), (rd_d, P, S), (rd_d, P + S, 2 * P)]
        ctx.callback(clear, nc, [sem(s) for s in signals] + flags)
        block = ctx.enter_context(nc.Block())

        @block.sync
        def _(sp):
            sp.dma_start(WQ[:, :], ins["c_qkv"]).then_inc(weights, 16)
            sp.dma_start(WO[:, :], ins["c_wo"]).then_inc(weights, 16)
            sp.dma_start(WR[:, :], ins["c_read"]).then_inc(weights, 16)
            sp.dma_start(WW[:, 0, :], ins["c_write1"]).then_inc(weights, 16)
            sp.dma_start(WW[:, 1, :], ins["c_write2"]).then_inc(weights, 16)
            sp.dma_start(cols[:, :], ins["c_cols"]).then_inc(weights, 16)
            sp.dma_start(dec[:, 0, :], ins["c_decay"].partition_broadcast(P)).then_inc(weights, 16)
            sp.dma_start(bias[:, :], ins["c_bias"].partition_broadcast(P)).then_inc(weights, 16)
            sp.dma_start(bv[:, :], ins["c_bv"].partition_broadcast(P)).then_inc(weights, 16)
            sp.dma_start(bo[:, :], ins["c_bo"].partition_broadcast(P)).then_inc(weights, 16)
            sp.wait_ge(made, 7)
            sp.dma_start(KS[MR:KR1, :, :], spread(one)).then_inc(weights, 16)
            sp.wait_ge(made2, 6)
            sp.dma_start(only[MR:KR1, :], one[:, 0:P]).then_inc(weights, 16)
            sp.dma_start(rd_d[:, :, 0:P].rearrange("a p s -> p a s"), QS[0:LINES, 0:PARTS, 0:P]).then_inc(weights, 16)
            sp.wait_ge(weights, 16 * NW)

            def hold():
                sp.sem_inc(sem(passed), 1)

            def store_qk(i):
                for g in range(NQ):
                    sp.wait_ge(*turn(stacked[g], i, 0))
                    hold()
                for z, parts_d in enumerate((q_d, k_d)):
                    sp.wait_ge(*turn(rest, i, 2 * z + 2))
                    for at, q0, q1 in SPANS[0:1 if z else 3]:
                        sp.dma_start(parts_d[:, :, at:at + q1 - q0].rearrange("a p s -> p a s"), part[:, z, :, q0:q1]
                                     ).then_inc(sem(stored[z]), 16)

            def store_lines(i):
                for n, (dst, at, width) in enumerate(PIECES):
                    sp.wait_ge(*turn(lthird, i, n + 1))
                    sp.dma_start(dst[:, :, at:at + width].rearrange("a p s -> p a s"),
                                 part[0:LINES, n % 2, :, 0:width]).then_inc(sem(stored[n % 2]), 16)
                for z in range(2):
                    sp.wait_ge(*turn(stored[z], i, per_turn(stored[z])))
                    hold()

            def stack(i, g):
                hs, at, s = slice(QUAD * g, QUAD * g + QUAD), QUAD * g, sem(stacked[g])
                sp.wait_ge(*turn(scored, i - 1, UQ * (g + 1)) if not isinstance(i, int) or i > 0 else (made, 7))
                sp.dma_start(QS[MR:KR1, hs, :], zero[:, :].unsqueeze(1).to_broadcast([2, QUAD, QC])).then_inc(s, 16)
                stack_left(sp, QS[:, hs, :], 0, HD, q_d, s, at)
                stack_right(sp, KS[:, hs, :], 0, HD, k_d, s, at)
                stack_left(sp, QI[:, hs, :], 0, PAST, r_d, s, at)
                stack_right(sp, KI[:, hs, :], 0, PAST, w_d, s, at)
                stack_right(sp, KS[:, hs, :], IR, PAST, wd_d, s, at)
                stack_left(sp, QS[:, hs, :], IR, PAST, rd_d, s, at)

            def stack_max(i, g):
                sp.wait_ge(*turn(mparts, i, 2 * g + 2))
                for n, m in enumerate((mh, ml)):
                    for at, q0, q1 in SPANS:
                        sp.dma_start(QS[MR + n:MR + n + 1, QUAD * g:QUAD * g + QUAD, at:at + q1 - q0],
                                     m[:, g % 2, q0:q1]).then_inc(sem(mstacked), 16)

            store_qk(0)
            store_lines(0)
            for g in range(NQ):
                stack(0, g)
            stack_max(0, 0)

            def run(i, tail, prep, tab):
                stack_max(i, 1)
                if prep:
                    store_qk(i + 1)
                stack_max(i, 2)
                if prep:
                    store_lines(i + 1)
                    stack(i + 1, 0)
                stack_max(i, 3)
                if prep:
                    stack(i + 1, 1)
                    stack(i + 1, 2)
                    stack_max(i + 1, 0)
                    stack(i + 1, 3)

            turns(sp, run)
            sp.wait_ge(*turn(mstacked, B, -16 * 6))

        @block.gpsimd
        def _(pool):
            prime(pool, signals)
            pool.memset(identb[:, :], 0.0).then_inc(made, 1)
            pool.memset(mask[:, :], 0.0).then_inc(made, 1)
            pool.iota(ramp[:, 0:P], pattern=[[-1, P]], base=0, channel_multiplier=1,
                      allow_small_or_imprecise_dtypes=True).then_inc(made, 1)
            pool.iota(ramp[:, P:P + 3], pattern=[[P, 3]], base=0, channel_multiplier=1,
                      allow_small_or_imprecise_dtypes=True).then_inc(made, 1)
            pool.iota(ramp[:, P + 3:P + 4], pattern=[[1, 1]], base=P, channel_multiplier=-1,
                      allow_small_or_imprecise_dtypes=True).then_inc(made, 1)
            pool.memset(zero[:, :], 0.0).then_inc(made, 1)
            pool.memset(one[:, :], 1.0).then_inc(made, 1)
            pool.wait_ge(made, 7)
            pool.affine_select(out=identb[:, :], in_=identb[:, :], compare_op=ALU.not_equal, fill=1.0,
                               base=0, pattern=[[-1, P]], channel_multiplier=1).then_inc(made, 1)
            pool.affine_select(out=mask[:, :], in_=mask[:, :], compare_op=ALU.is_ge, fill=NEG,
                               base=0, pattern=[[-1, P]], channel_multiplier=1).then_inc(made, 1)
            pool.wait_ge(table_made, 6 + H)
            pool.affine_select(out=table_of_decays[:, :, :], in_=table_of_decays[:, :, :], compare_op=ALU.is_gt, fill=0.0,
                               base=0, pattern=[[0, H], [-1, P]], channel_multiplier=1).then_inc(made, 1)
            pool.wait_ge(weights, 16 * NW)

            def prep(i):
                norm_root(pool, c, norm, i, 0)
                for z in range(2):
                    pool.wait_ge(*turn(cast, i, 2 * z + 1))
                    pool.wait_ge(*turn(lcast, i, 0))
                    pool.tensor_tensor(rem[:, z, :], qk[:, z, :], part[:, z, 0, :], ALU.subtract).then_inc(sem(rest), 1)
                    pool.wait_ge(*turn(cast, i, 2 * z + 2))
                    pool.tensor_tensor(part[:, z, 2, :], rem[:, z, :], part[:, z, 1, :], ALU.subtract
                                       ).then_inc(sem(rest), 1)
                for z in range(2):
                    pool.wait_ge(*turn(points, i, 4 * z + 4))
                    if z:
                        pool.wait_ge(*turn(summed, i, 2))
                    ab, cd = ((0, 1), (2, 3)) if z == 0 else ((0, 2), (1, 3))
                    for n, (a, b) in enumerate((ab, cd)):
                        pool.tensor_tensor(prod[:, n, :, :], LP[:, :, a * LINES:(a + 1) * LINES],
                                           LP[:, :, b * LINES:(b + 1) * LINES], ALU.mult).then_inc(sem(product), 1)
                    pool.wait_ge(*turn(product, i, 2 * z + 2))
                    pool.wait_ge(*turn(lined, i, 0))
                    pool.tensor_tensor(line[:, z, :, :], prod[:, 0, :, :], prod[:, 1, :, :], ALU.subtract
                                       ).then_inc(sem(crossed), 1)
                    pool.wait_ge(*turn(crossed, i, z + 1))
                    pool.tensor_tensor(prod[:, 0, :, :], line[:, z, :, :], line[:, z, :, :], ALU.mult
                                       ).then_inc(sem(squared), 1)
                    pool.wait_ge(*turn(summed, i, 2 * z + 2))
                    pool.tensor_tensor(rn[:, 2, :], rn[:, 1, :], minus_half[:, :], ALU.pow).then_inc(sem(normed), 1)
                    pool.wait_ge(*turn(normed, i, z + 1))
                    v = line[:, z, :, :].rearrange("p t (e h) -> p t e h", e=PAST)
                    pool.tensor_tensor(v, v, over(rn[:, 2, :].rearrange("p (t h) -> p t h", t=T), 2, PAST), ALU.mult
                                       ).then_inc(sem(unit), 1)
                for n, (_, _, width) in enumerate(PIECES):
                    pool.wait_ge(*turn(lcast, i, 2 * n + 2))
                    pool.tensor_tensor(part[0:LINES, n % 2, 2, 0:width], rem[0:LINES, n % 2, 0:width],
                                       part[0:LINES, n % 2, 1, 0:width], ALU.subtract).then_inc(sem(lthird), 1)

            with pool.Fori(0, B) as i:
                prep(i)

        @block.scalar
        def _(act):
            act.wait_ge(weights, 16 * NW)
            act.wait_ge(table_made, 1)
            act.activation(dec[:, 2, :], dec[:, 1, :], ACT.Exp, scale=-1.0).then_inc(table_made, 1)
            act.wait_ge(table_made, 2)
            act.activation(dec[:, 2, :], dec[:, 2, :], ACT.Ln, bias=1.0).then_inc(table_made, 1)
            act.wait_ge(table_made, 6)
            for h in range(H):
                act.activation(table_of_decays[:, h, :], ramp[:, 0:P], ACT.Exp, scale=dec[:, 3, h:h + 1]).then_inc(table_made, 1)
            act.activation(DQ[:, :, :], expo[:, :, :], ACT.Exp).then_inc(table_made, 1)

            def prep_step(u, i, tab):
                if u == 1:
                    act.wait_ge(*turn(turned, i, 1))
                    act.wait_ge(*turn(valued, i, 0))
                    act.activation(XT[:, 1:S + 1], bank(tab, ("turned", 1, 0))[:, :], ACT.Copy).then_inc(sem(xT), 1)
                if u in CASTS:
                    z = CASTS.index(u)
                    act.wait_ge(*turn(projected, i, z + 1))
                    act.wait_ge(*turn(stored[z], i, 0))
                    act.activation(part[:, z, 0, :], qk[:, z, :], ACT.Copy).then_inc(sem(cast), 1)
                    act.wait_ge(*turn(rest, i, 2 * z + 1))
                    act.activation(part[:, z, 1, :], rem[:, z, :], ACT.Copy).then_inc(sem(cast), 1)
                for kind, batch, n in EXTRA.get(u, []):
                    if kind == "points":
                        act.wait_ge(*turn(pointed, i, n + 1))
                        act.wait_ge(*turn(lined, i, 0) if n < T else turn(product, i, 2))
                        act.activation(LP[:, n % T, :], bank(tab, ("points", 1, n))[:, 0:4 * LINES], ACT.Copy
                                       ).then_inc(sem(points), 1)
                for n, (_, _, width) in enumerate(PIECES):
                    if u == LINE_AT[n]:
                        act.wait_ge(*turn(lined, i, n + 1))
                        before = 16 * (3 + n // 2) if n % 2 == 0 else 16 * (1 + n // 2)
                        act.wait_ge(*turn(stored[n % 2], i, before))
                        act.activation(part[0:LINES, n % 2, 0, 0:width], bank(tab, ("line", 1, n))[0:LINES, 0:width],
                                       ACT.Copy).then_inc(sem(lcast), 1)
                        act.wait_ge(*turn(lrest, i, n + 1))
                        act.activation(part[0:LINES, n % 2, 1, 0:width], rem[0:LINES, n % 2, 0:width], ACT.Copy
                                       ).then_inc(sem(lcast), 1)

            def tail_step(u, i, tab):
                if u == 0:
                    act.wait_ge(*turn(at_turned, i, 1))
                    act.activation(ATT[:, :], bank(tab, ("at", -1, 0))[:, :], ACT.Copy).then_inc(sem(attT), 1)

            def minus_max(i, g):
                act.wait_ge(*turn(mturned, i, g + 1))
                act.wait_ge(*turn(mstacked, i, 96 * (g - 1)))
                act.activation(mh[:, g % 2, :], TB[0:QUAD, :], ACT.Copy, scale=-1.0).then_inc(sem(mparts), 1)

            for u in range(UNITS):
                prep_step(u, 0, opening)
            minus_max(0, 0)

            def run(i, tail, prep, tab):
                for u in range(UNITS):
                    g = u // UQ
                    act.wait_ge(*turn(scored, i, u + 1))
                    act.wait_ge(*turn(pv, i, g))
                    act.activation(PT[:, u % UQ, :, :], ST[:, :, :], ACT.Exp).then_inc(sem(exped), 1)
                    if tail:
                        tail_step(u, i - 1, tab)
                    if prep:
                        prep_step(u, i + 1, tab)
                    if u % UQ == QUAD and (prep or g < NQ - 1):
                        minus_max(i + (g + 1) // NQ, (g + 1) % NQ)

            turns(act, run)
            tail_step(0, B - 1, closing)

        @block.vector
        def _(dve):
            dve.memset(V[:, :, :, :], 0.0).then_inc(made2, 1)
            dve.memset(QS[:, :, 0:P], 0.0).then_inc(made2, 1)
            dve.memset(XT[:, 0:1], 0.0).then_inc(made2, 1)
            dve.memset(minus_half[:, :], -0.5).then_inc(made2, 1)
            dve.memset(only[:, :], 0.0).then_inc(made2, 1)
            dve.wait_ge(made2, 5)
            dve.memset(V[:, :, :, HD:HD + 1], 1.0).then_inc(made2, 1)
            dve.wait_ge(made2, 6)
            dve.wait_ge(weights, 16 * NW)
            dve.tensor_scalar(dec[:, 1, :], dec[:, 0, :], -44.0, None, ALU.max).then_inc(table_made, 1)
            dve.wait_ge(table_made, 3)
            dve.tensor_scalar(dec[:, 3, :], dec[:, 2, :], -1.0, None, ALU.mult).then_inc(table_made, 1)
            dve.tensor_scalar(ramp[:, 0:P], ramp[:, 0:P], 0.0, None, ALU.max).then_inc(table_made, 1)
            dve.wait_ge(table_made, 5)
            dve.tensor_tensor(expo[:, :, :], dec[:, 3, :].unsqueeze(1).to_broadcast([P, 4, H]),
                              widen(ramp[:, P:P + 4], H), ALU.mult).then_inc(table_made, 1)
            dve.wait_ge(table_made, 7 + H)
            dve.wait_ge(made, 10)

            def prep_step(u, i, tab):
                def x_tile(t):
                    return X[:, bass.ds(i * T + t, 1), :].rearrange("p a d -> p (a d)")

                if u == 0:
                    norm_measure(dve, c, norm, i, 0, x_tile)
                if u == 1:
                    dve.wait_ge(*turn(turned, i, 0))
                    norm_scale(dve, c, norm, i, 0, lambda t: XN[:, t, :], x_tile)
                if u == 2:
                    for z in range(2):
                        dve.wait_ge(*turn(made_qk, i, z + 1))
                        dve.wait_ge(*turn(rest, i, 0))
                        dve.tensor_scalar(qk[:, z, :], bank(tab, ("qk", 1, z))[:, :], cols[:, z:z + 1],
                                          1.0 if z else float(HD) ** -0.5, ALU.add, ALU.mult).then_inc(sem(projected), 1)
                if u in SUMS:
                    z = SUMS.index(u)
                    dve.wait_ge(*turn(squared, i, z + 1))
                    dve.tensor_reduce(rn[:, 0, :].rearrange("p (t h) -> p t h", t=T),
                                      prod[:, 0, :, :].rearrange("p t (e h) -> p t h e", e=PAST),
                                      AX_X, ALU.add).then_inc(sem(summed), 1)
                    dve.wait_ge(*turn(summed, i, 2 * z + 1))
                    dve.tensor_scalar(rn[:, 1, :], rn[:, 0, :], 1e-24, None, ALU.max).then_inc(sem(summed), 1)
                if u == DECAY_AT:
                    dve.wait_ge(*turn(unit, i, 1))
                    v = line[:, 0, :, :].rearrange("p t (e h) -> p t e h", e=PAST)
                    dve.tensor_tensor(v, v, over(over(bias[:, :], 1, PAST), 1, T), ALU.mult).then_inc(sem(scaled), 1)
                    dve.wait_ge(*turn(scaled, i, 1))
                    dve.wait_ge(*turn(unit, i, 2))
                    first = 0
                    for kt in range(T - 1):
                        n = T - 1 - kt
                        dve.tensor_tensor(LQ[:, first:first + n, :].rearrange("p t (e h) -> p t e h", e=PAST),
                                          v[:, kt + 1:T], over(DQ[:, 0:n, :], 2, PAST), ALU.mult).then_inc(sem(decayed), 1)
                        first += n
                    dve.tensor_tensor(LK[:, :, :].rearrange("p t (e h) -> p t e h", e=PAST),
                                      line[:, 1, :, :].rearrange("p t (e h) -> p t e h", e=PAST),
                                      over(over(DQ[:, 3, :], 1, PAST), 1, T), ALU.mult).then_inc(sem(decayed), 1)
                for n, (_, _, width) in enumerate(PIECES):
                    if u == LINE_AT[n]:
                        dve.wait_ge(*turn(lcast, i, 2 * n + 1))
                        dve.wait_ge(*turn(lthird, i, n - 1) if n >= 2 else turn(rest, i, 2 * n + 2))
                        dve.tensor_tensor(rem[0:LINES, n % 2, 0:width], bank(tab, ("line", 1, n))[0:LINES, 0:width],
                                          part[0:LINES, n % 2, 0, 0:width], ALU.subtract).then_inc(sem(lrest), 1)

            def values(i, tab):
                for n in range(2):
                    dve.wait_ge(*turn(valued, i, n + 1))
                    dve.wait_ge(*turn(pv, i, 0))
                    dve.tensor_tensor(V[:, 2 * n:2 * n + 2, :, 0:HD],
                                      bank(tab, ("v", 1, n))[:, 0:2 * D].rearrange("p (t h d) -> p t h d", t=2, d=HD),
                                      over(bv[:, :].rearrange("p (h d) -> p h d", d=HD), 1, 2), ALU.add
                                      ).then_inc(sem(vdone), 1)

            def tail_step(u, i, tab):
                xb = X[:, bass.ds(i * T, T), :]
                if u == 0:
                    dve.wait_ge(*turn(added, i, 0))
                    dve.tensor_tensor(XB[:, :, :], xb, over(bo[:, :], 1, T), ALU.add).then_inc(sem(biased), 1)
                if u == 1:
                    dve.wait_ge(*turn(wo, i, 1))
                    dve.wait_ge(*turn(biased, i, 1))
                    dve.tensor_tensor(xb, bank(tab, ("wo", -1, 0))[:, :].rearrange("p (t d) -> p t d", d=D),
                                      XB[:, :, :], ALU.add).then_inc(sem(added), 1)

            def maxima(i, h, tab, batch):
                g = h // QUAD
                dve.wait_ge(*turn(logit, i, 4 * h + 1))
                dve.wait_ge(*turn(diag, i, h))
                dve.tensor_tensor(inc[:, :].rearrange("p (t k) -> p t k", k=P),
                                  bank(tab, ("inc", batch, h))[:, :].rearrange("p (t k) -> p t k", k=P),
                                  over(table_h(h), 1, T), ALU.mult).then_inc(sem(inc_decayed), 1)
                f = bank(tab, ("past31", batch, h))
                dve.wait_ge(*turn(logit, i, 4 * h + 3))
                dve.tensor_reduce(M[:, 3, h:h + 1], f[:, 0:3 * P], AX_X, ALU.max).then_inc(sem(maxed), 1)
                dve.tensor_reduce(M[:, 1, h:h + 1], f[:, 3 * P:4 * P], AX_X, ALU.max).then_inc(sem(maxed), 1)
                dve.wait_ge(*turn(logit, i, 4 * h + 4))
                dve.tensor_reduce(M[:, 2, h:h + 1], bank(tab, ("past2", batch, h))[:, 0:2 * P], AX_X, ALU.max
                                  ).then_inc(sem(maxed), 1)
                dve.wait_ge(*turn(inc_decayed, i, h + 1))
                dve.wait_ge(*turn(scored, i, UQ * (g - 1)))
                sd = SD[:, g % 2, h % QUAD, :, :]
                dve.tensor_tensor(sd, bank(tab, ("diag", batch, h))[:, :].rearrange("p (t k) -> p t k", k=P),
                                  inc[:, :].rearrange("p (t k) -> p t k", k=P), ALU.add).then_inc(sem(diag), 1)
                dve.wait_ge(*turn(diag, i, h + 1))
                dve.tensor_reduce(MD[:, :, h], sd, AX_X, ALU.max).then_inc(sem(maxed), 1)

            def table_h(h):
                return table_of_decays[:, h, :]

            def join(i, g):
                hs = slice(QUAD * g, QUAD * g + QUAD)
                dve.wait_ge(*turn(maxed, i, 4 * QUAD * (g + 1)))
                dve.tensor_tensor(MD[:, 1:T, hs], MD[:, 1:T, hs], M[:, 1:T, hs], ALU.max).then_inc(sem(mjoined), 1)
                dve.wait_ge(*turn(mparts, i, 2 * g + 1))
                dve.scalar_tensor_tensor(ml[:, g % 2, :], TB[0:QUAD, :], -1.0, mh[:, g % 2, :], ALU.mult,
                                         ALU.subtract).then_inc(sem(mparts), 1)

            for u in range(UNITS):
                prep_step(u, 0, opening)
            for h in range(QUAD):
                maxima(0, h, opening, 1)
            join(0, 0)
            values(0, opening)

            def run(i, tail, prep, tab):
                for u in range(UNITS):
                    g = u // UQ
                    if next_head(u, prep):
                        batch, h = next_head(u, prep)
                        maxima(i + batch, h, tab, batch)
                    if tail:
                        tail_step(u, i - 1, tab)
                    if prep:
                        prep_step(u, i + 1, tab)
                    if u % UQ < QUAD:
                        continue
                    if prep or g < NQ - 1:
                        join(i + (g + 1) // NQ, (g + 1) % NQ)
                    dve.wait_ge(*turn(pv, i, g + 1))
                    dve.wait_ge(*turn(pvturned, i, g))
                    dve.tensor_copy(pvs[:, :], PV[:, :]).then_inc(sem(pvcopied), 1)
                    dve.wait_ge(*turn(pvturned, i, g + 1))
                    heads = TB[:, :].rearrange("p (t j e) -> p t j e", t=T, e=32)
                    dve.reciprocal(rec[:, :, :], heads[:, :, :, HD]).then_inc(sem(inv), 1)
                    dve.wait_ge(*turn(inv, i, g + 1))
                    dve.wait_ge(*turn(at_turned, i, 0))
                    dve.tensor_tensor(AT[:, :, 32 * g:32 * g + 32].rearrange("p t (j e) -> p t j e", e=HD),
                                      heads[:, :, :, 0:HD], widen(rec[:, :, :], HD), ALU.mult).then_inc(sem(attn), 1)
                if prep:
                    values(i + 1, tab)

            turns(dve, run)
            for u in range(2):
                tail_step(u, B - 1, closing)
            dve.wait_ge(*turn(added, B, 0))

        @block.tensor
        def _(pe):
            pe.wait_ge(weights, 16 * NW)
            pe.wait_ge(made, 10)
            pe.wait_ge(made2, 6)

            def front(tab, use, i):
                if tab[use][1]:
                    kind, batch, n = tab[use][1]
                    pe.wait_ge(*turn(readers[kind][0], i + batch, readers[kind][1](n)))
                return bank(tab, use)

            def prep_step(use, i, tab):
                kind, _, n = use
                b = i + 1
                if kind == "turned":
                    norm_wait(pe, norm, b, 0)
                    f = front(tab, use, i)
                    for t in range(T):
                        last = pe.transpose(f[:, t * P:(t + 1) * P], XN[:, t, :], ident[:, :])
                    last.then_inc(sem(turned), 1)
                elif kind == "qk":
                    if n == 0:
                        pe.wait_ge(*turn(xT, b, 1))
                    pe.matmul(front(tab, use, i)[:, :], WQ[:, n * D:(n + 1) * D], XT[:, 1:S + 1], start=True, stop=True
                              ).then_inc(sem(made_qk), 1)
                elif kind == "points":
                    t, f = n % T, front(tab, use, i)
                    if n < T:
                        pe.matmul(f[:, 0:4 * LINES], XT[:, 1 + t * P:1 + (t + 1) * P], WR[:, :], start=True, stop=True
                                  ).then_inc(sem(pointed), 1)
                    else:
                        pe.matmul(f[:, 0:2 * LINES], XT[:, t * P:(t + 1) * P], WW[:, 0, :], start=True, stop=True)
                        pe.matmul(f[:, 2 * LINES:4 * LINES], XT[:, 1 + t * P:1 + (t + 1) * P], WW[:, 1, :],
                                  start=True, stop=True).then_inc(sem(pointed), 1)
                else:
                    src, tiles = [(line[:, 0], range(T)), (line[:, 1], range(T)), (LK, range(T)), (LQ, range(T)),
                                  (LQ, range(T, 6))][n]
                    if n == 0:
                        pe.wait_ge(*turn(scaled, b, 1))
                    elif n == 1:
                        pe.wait_ge(*turn(unit, b, 2))
                    else:
                        pe.wait_ge(*turn(decayed, b, 4))
                    f = front(tab, use, i)
                    for k, t in enumerate(tiles):
                        last = pe.transpose(f[0:LINES, k * P:(k + 1) * P], src[:, t, :], ident[:, :])
                    last.then_inc(sem(lined), 1)

            def prep_values(i, tab):
                for n in range(2):
                    f = front(tab, ("v", 1, n), i)
                    for t in range(2 * n, 2 * n + 2):
                        last = pe.matmul(f[:, (t % 2) * D:(t % 2 + 1) * D], XT[:, 1 + t * P:1 + (t + 1) * P],
                                         WQ[:, 2 * D:3 * D], start=True, stop=True)
                    last.then_inc(sem(valued), 1)

            def tail_step(use, i, tab):
                if use[0] == "at":
                    pe.wait_ge(*turn(attn, i - 1, NQ))
                    f = front(tab, use, i)
                    for t in range(T):
                        last = pe.transpose(f[:, t * P:(t + 1) * P], AT[:, t, :], ident[:, :])
                    last.then_inc(sem(at_turned), 1)
                else:
                    pe.wait_ge(*turn(attT, i - 1, 1))
                    f = front(tab, use, i)
                    for t in range(T):
                        last = pe.matmul(f[:, t * D:(t + 1) * D], ATT[:, t * P:(t + 1) * P], WO[:, :],
                                         start=True, stop=True)
                    last.then_inc(sem(wo), 1)

            def logits(i, tab, batch, h):
                if h % QUAD == 0:
                    pe.wait_ge(*turn(stacked[h // QUAD], i + batch, 16 * STACKS))
                f = front(tab, ("inc", batch, h), i)
                for t in range(T):
                    ts = slice(t * P, (t + 1) * P)
                    last = pe.matmul(f[:, ts], QI[:, h, ts], KI[:, h, ts], start=True, stop=True)
                last.then_inc(sem(logit), 1)
                f = front(tab, ("diag", batch, h), i)
                for t in range(T):
                    ts = slice(t * P, (t + 1) * P)
                    pe.matmul(f[:, ts], QS[0:STACK, h, ts], KS[0:STACK, h, ts], start=True, stop=False)
                    last = pe.matmul(f[:, ts], identb[:, :], mask[:, :], start=False, stop=True)
                last.then_inc(sem(logit), 1)
                f = front(tab, ("past31", batch, h), i)
                for kt in range(3):
                    at = [3 * P, S + P, S + 2 * P][kt]
                    pe.matmul(f[:, kt * P:(kt + 1) * P], QS[0:KR1, h, at:at + P], KS[0:KR1, h, kt * P:(kt + 1) * P],
                              start=True, stop=True)
                pe.matmul(f[:, 3 * P:4 * P], QS[0:KR1, h, P:2 * P], KS[0:KR1, h, 0:P], start=True, stop=True
                          ).then_inc(sem(logit), 1)
                f = front(tab, ("past2", batch, h), i)
                pe.matmul(f[:, 0:P], QS[0:KR1, h, 2 * P:3 * P], KS[0:KR1, h, 0:P], start=True, stop=True)
                pe.matmul(f[:, P:2 * P], QS[0:KR1, h, S:S + P], KS[0:KR1, h, P:2 * P], start=True, stop=True
                          ).then_inc(sem(logit), 1)

            def turn_max(i, g):
                pe.wait_ge(*turn(mjoined, i, g + 1))
                pe.wait_ge(*turn(attn, i, g - 1))
                for t in range(T):
                    last = pe.transpose(TB[0:QUAD, t * P:(t + 1) * P], MD[:, t, QUAD * g:QUAD * g + QUAD],
                                        ident[:, :])
                last.then_inc(sem(mturned), 1)

            def diagonal(out, g, j, t):
                pe.matmul(out, only[:, :], QS[0:KR1, QUAD * g + j, t * P:(t + 1) * P], start=True, stop=False)
                return pe.matmul(out, SD[:, g % 2, j, t, :], ident[:, :], start=False, stop=True)

            def scores(i, g, j):
                h = QUAD * g + j
                if j == 0:
                    pe.wait_ge(*turn(mstacked, i, 96 * (g + 1)))
                u = UQ * g + j
                pe.wait_ge(*turn(exped, i, u))
                if j < QUAD:
                    diagonal(ST[:, 0, 0:P], g, j, 0)
                    pe.matmul(ST[:, 0, P:S], KS[0:KR1, h, 0:P], QS[0:KR1, h, P:S], start=True, stop=True)
                    diagonal(ST[:, 1, 0:P], g, j, 1)
                    pe.matmul(ST[:, 1, P:3 * P], KS[0:KR1, h, P:2 * P], QS[0:KR1, h, S:S + 2 * P],
                              start=True, stop=True)
                    diagonal(ST[:, 1, 3 * P:4 * P], g, j, 3).then_inc(sem(scored), 1)
                else:
                    for k in range(QUAD):
                        h = QUAD * g + k
                        at = (k % 2) * 2 * P
                        diagonal(ST[:, k // 2, at:at + P], g, k, 2)
                        last = pe.matmul(ST[:, k // 2, at + P:at + 2 * P], KS[0:KR1, h, 2 * P:3 * P],
                                         QS[0:KR1, h, S + 2 * P:QC], start=True, stop=True)
                    last.then_inc(sem(scored), 1)

            def values(i, g):
                pe.wait_ge(*turn(exped, i, UQ * (g + 1)))
                if g == 0:
                    pe.wait_ge(*turn(vdone, i, 2))
                pe.wait_ge(*turn(pvcopied, i, g))
                def buf(j):
                    return PT[:, j, :, :]
                for kt in range(T):
                    for j in range(QUAD):
                        if kt == 0:
                            src = buf(j)[:, 0, :]
                        elif kt == 1:
                            src = buf(j)[:, 1, 0:3 * P]
                        elif kt == 2:
                            src = buf(QUAD)[:, j // 2, (j % 2) * 2 * P:(j % 2 + 1) * 2 * P]
                        else:
                            src = buf(j)[:, 1, 3 * P:4 * P]
                        last = pe.matmul(PV[32 * j:32 * j + 32, kt * P:S], V[:, kt, QUAD * g + j, :], src,
                                         start=(kt == 0), stop=(kt == T - 1), skip_group_check=True)
                last.then_inc(sem(pv), 1)

            def turn_values(i, g, more):
                pe.wait_ge(*turn(pvcopied, i, g + 1))
                pe.wait_ge(*turn(mparts, i, 2 * (g + 2 if more else NQ)))
                pe.wait_ge(*turn(attn, i, g))
                for t in range(T):
                    last = pe.transpose(TB[:, t * P:(t + 1) * P], pvs[:, t * P:(t + 1) * P], ident[:, :])
                last.then_inc(sem(pvturned), 1)

            for use in OPENING:
                if use[0] in ("turned", "qk", "points", "line"):
                    prep_step(use, -1, opening)
            for h in range(QUAD):
                logits(-1, opening, 1, h)
            turn_max(0, 0)
            prep_values(-1, opening)

            def run(i, tail, prep, tab):
                for u in range(UNITS):
                    g, j = u // UQ, u % UQ
                    scores(i, g, j)
                    if next_head(u, prep):
                        logits(i, tab, *next_head(u, prep))
                    for use in extras(u, tail, prep):
                        (tail_step if use[1] < 0 else prep_step)(use, i, tab)
                    if j == QUAD:
                        more = prep or g < NQ - 1
                        if more:
                            turn_max(i + (g + 1) // NQ, (g + 1) % NQ)
                        values(i, g)
                        turn_values(i, g, more)
                if prep:
                    prep_values(i, tab)

            turns(pe, run)
            for use in CLOSING:
                tail_step(use, B, closing)


def experts(nc, ins, c, tag, E):
    first = tag == "L0"
    func = ACT.Relu if first else ACT.Gelu
    with ExitStack() as ctx:
        def sb(name, shape, dt=F32):
            return ctx.enter_context(nc.sbuf_tensor(f"{tag}_{name}", shape, dt))

        signals, flags = [], []

        def sig(name, per=1, start=1):
            signals.append((ctx.enter_context(nc.semaphore(f"{tag}_{name}")), per, start))
            return signals[-1]

        def flag(name):
            flags.append(ctx.enter_context(nc.semaphore(f"{tag}_{name}")))
            return flags[-1]

        NG = B * T
        TOK = NG * P
        CH = 2
        NT = CH * NG + E
        U = len(c[f"{tag}_gathered"])
        TURNS = NT // U
        HALF = 2
        PAIRS_OF_BATCHES = B // HALF
        HT = HALF * T
        assert NT % U == 0 and NT <= P

        X, XN, XT, ident = c["X"], [c["XN"], c["YN"]], c["YT"], c["ident"]
        W1 = sb("W1", [P, E, F + FC])
        W2 = sb("W2", [P, E, FC, D])
        b2 = sb("b2", [P, E, D])
        wr = sb("wr", [P, E])
        br = sb("br", [P, E])
        mva = sb("mva", [P, NG, 2])
        root = sb("root", [P, 2, NG])
        consts = sb("consts", [P, 2, NG])
        desc = sb("desc", [P, NG, E])
        key = sb("key", [P, NG, E])
        ex = sb("ex", [P, NG, E])
        work = sb("work", [P, NG, E])
        eq = sb("eq", [P, NG, E])
        choice = sb("choice", [P, CH, NG, E])
        both = sb("both", [P, NG, E], BF16)
        load = sb("load", [P, E], BF16)
        red = sb("red", [P, 4, NG])
        gate = sb("gate", [P, CH, NG])
        tri = sb("tri", [P, P], BF16)
        ones = sb("ones", [P, P], BF16)
        zeros = sb("zeros", [P, 2 * NT], BF16)
        steps = sb("steps", [P, E, NG])
        full = sb("full", [P, E, NG])
        count = sb("count", [P, E])
        tiles = sb("tiles", [P, 3, E])
        start = sb("start", [P, E])
        place = sb("place", [P, CH, NG])
        place_i = sb("place_i", [P, 3, CH, NG], I32)
        row = sb("row", [P, CH, NG])
        tile_of = sb("tile_of", [P, CH, NG])
        base = sb("base", [P, 2, CH, NG])
        code = sb("code", [P, 2, CH, NG])
        numbers = sb("numbers", [P, P])
        is_row = sb("is_row", [P, HALF, CH, T, P], BF16)
        is_tile = sb("is_tile", [P, HALF, CH, T, 2 * NT], BF16)
        past = sb("past", [P, NT, E])
        owner = sb("owner", [P, 2, NT])
        owner_i = sb("owner_i", [P, NT], I32)
        spare = sb("spare", [P, NT])
        dest = sb("dest", [P, 2, NT])
        dest_i = sb("dest_i", [P, 2, NT], I32)
        source = sb("source", [P, NT])
        gi = sb("gi", [P, U], I32)
        si = sb("si", [P, U], I32)
        xg = sb("xg", [P, U, D])
        xT = sb("xT", [P, 2, P])
        W1s = sb("W1s", [P, 2, F + FC])
        hT = sb("hT", [P, 2, FC, P])
        ys = sb("ys", [P, U, D])
        got = sb("got", [P, HALF, CH, T, D])
        xn_d = nc.dram_tensor(f"{tag}_xn", [TOK, D], F32).ap()
        y_d = nc.dram_tensor(f"{tag}_y", [CH * TOK + NT * P, D], F32).ap()
        PS = [ctx.enter_context(nc.psum_tensor(f"{tag}_P{n}", [P, S], F32)) for n in range(8)]

        loads, made, table_made = flag("loads"), flag("made"), flag("table_made")
        stats, mean, kept = sig("stats", T), sig("mean", T), sig("kept")
        rooted = flag("rooted")
        out = sig("out", HT)
        turned, copied = sig("turned", HALF, HALF), sig("copied", HALF)
        logits, ready, collected = sig("logits", HALF), sig("ready", HALF), sig("collected", HALF, HALF)
        xn_stored = [sig(f"xn_stored{h}", 16) for h in range(HALF)]
        route, exps, ranked = flag("route"), flag("exps"), flag("ranked")
        CODES = CH * (1 + 2 * T)
        coded, told = sig("coded", HALF * CODES), sig("told", HALF, HALF)
        inverse = flag("inverse")
        def tile_sig(name, per=1):
            return sig(name, per * U, per * U)

        gi_set, si_set, go = tile_sig("gi_set"), tile_sig("si_set"), tile_sig("go")
        gathered = [(s, 16, 0) for s in c[f"{tag}_gathered"]]
        scattered = [(s, 16, 0) for s in c[f"{tag}_scattered"]]
        g_turned, g_copied, w1_set = tile_sig("g_turned"), tile_sig("g_copied"), tile_sig("w1_set")
        hidden, acted = tile_sig("hidden", 2), tile_sig("acted", FC)
        y, y_set = tile_sig("y"), tile_sig("y_set")
        y_loaded = [sig(f"y_loaded{h}", 16 * CH, 16 * CH) for h in range(HALF)]
        mixed1, mixed2 = sig("mixed1", HT, HT), sig("mixed2", HT, HT)
        SORTED = (6 if first else 2) + 5 + 1 + 5 + 2
        LOADS = 16 * (2 * 4 + 3 + (1 if first else 0))

        def ahead(i, u, k):
            return i + (u + k) // U, (u + k) % U

        def expert_of(eng, i, u):
            return eng.value_load(owner_i[0:1, bass.ds(i * U + u, 1)], min_val=0, max_val=E - 1)

        ctx.callback(clear, nc, [sem(s) for s in signals] + flags)
        block = ctx.enter_context(nc.Block())

        @block.sync
        def _(sp):
            sp.dma_start(wr[:, :], ins[f"{tag}_wr"]).then_inc(loads, 16)
            if first:
                sp.dma_start(br[:, :], ins["L0_br"].partition_broadcast(P)).then_inc(loads, 16)
            sp.dma_start(b2[:, :, :].rearrange("p e d -> p (e d)"),
                         ins[f"{tag}_b2"].rearrange("e d -> (e d)").partition_broadcast(P)).then_inc(loads, 16)
            sp.dma_start(W1[:, :, F:F + FC], ins[f"{tag}_b1"]).then_inc(loads, 16)
            for n in range(4):
                es = slice(n * E // 4, (n + 1) * E // 4)
                sp.dma_start(W1[:, es, 0:F], ins[f"{tag}_w1"][:, es, :]).then_inc(loads, 16)
                sp.dma_start(W2[:, es, :, :], ins[f"{tag}_w2"][:, es, :, :]).then_inc(loads, 16)
            sp.wait_ge(loads, LOADS)
            rows = xn_d.rearrange("(n p) d -> p n d", p=P)
            with sp.Fori(0, PAIRS_OF_BATCHES) as i:
                for h in range(HALF):
                    sp.wait_ge(*turn(out, i, (h + 1) * T))
                    sp.dma_start(rows[:, bass.ds((i * HALF + h) * T, T), :], XN[h][:, :, :]
                                 ).then_inc(sem(xn_stored[h]), 16)
            for u in range(U):
                sp.wait_ge(*turn(scattered[u], TURNS, 0))
            results = y_d[0:CH * TOK].rearrange("(k n p) d -> p k n d", k=CH, p=P)
            with sp.Fori(0, PAIRS_OF_BATCHES) as i:
                for h in range(HALF):
                    sp.wait_ge(*turn(mixed2, i, (h + 1) * T - HT))
                    for k in range(CH):
                        sp.dma_start(got[:, h, k, :, :], results[:, k, bass.ds((i * HALF + h) * T, T), :]
                                     ).then_inc(sem(y_loaded[h]), 16)

        @block.gpsimd
        def _(pool):
            prime(pool, signals)
            exact = dict(allow_small_or_imprecise_dtypes=True)
            pool.iota(desc[:, :, :], pattern=[[0, NG], [-1, E]], base=E, channel_multiplier=0, **exact).then_inc(made, 1)
            pool.iota(steps[:, :, :], pattern=[[0, E], [P, NG]], base=0, channel_multiplier=0, **exact).then_inc(made, 1)
            pool.iota(base[:, 0, :, :], pattern=[[NG, CH], [1, NG]], base=-CH * NG, channel_multiplier=0, **exact
                      ).then_inc(made, 1)
            pool.iota(base[:, 1, :, :], pattern=[[0, CH], [0, NG]], base=0, channel_multiplier=1, **exact
                      ).then_inc(made, 1)
            pool.iota(numbers[:, :], pattern=[[1, P]], base=0, channel_multiplier=0, **exact).then_inc(made, 1)
            pool.iota(spare[:, :], pattern=[[P, NT]], base=CH * TOK, channel_multiplier=1, **exact).then_inc(made, 1)
            pool.memset(ones[:, :], 1.0).then_inc(made, 1)
            pool.memset(tri[:, :], 1.0).then_inc(made, 1)
            pool.memset(zeros[:, :], 0.0).then_inc(made, 1)
            pool.memset(consts[:, 0, :], EPS).then_inc(made, 1)
            pool.memset(consts[:, 1, :], -0.5).then_inc(made, 1)
            pool.wait_ge(made, 11)
            pool.affine_select(out=tri[:, :], in_=tri[:, :], compare_op=ALU.is_gt, fill=0.0,
                               base=0, pattern=[[1, P]], channel_multiplier=-1).then_inc(made, 1)
            pool.wait_ge(*turn(kept, B, 0))
            pool.tensor_tensor(root[:, 0, :], mva[:, :, 1], consts[:, 0, :], ALU.add).then_inc(rooted, 1)
            pool.wait_ge(rooted, 1)
            pool.tensor_tensor(root[:, 1, :], root[:, 0, :], consts[:, 1, :], ALU.pow).then_inc(rooted, 1)

            def gather(i, u):
                pool.wait_ge(*turn(gi_set, i, u + 1))
                pool.wait_ge(*turn(g_turned, i, u + 1 - U))
                pool.sem_inc(sem(go), 1)
                pool.indirect_dma_start(xg[:, u, :], None, xn_d, bass.IndirectOffsetOnAxis(gi[:, u:u + 1], 0)
                                        ).then_inc(sem(gathered[u]), 16)

            def scatter(i, u):
                pool.wait_ge(*turn(si_set, i, u + 1))
                pool.wait_ge(*turn(y_set, i, u + 1))
                pool.sem_inc(sem(go), 1)
                pool.indirect_dma_start(y_d, bass.IndirectOffsetOnAxis(si[:, u:u + 1], 0), ys[:, u, :], None
                                        ).then_inc(sem(scattered[u]), 16)

            for h in range(HALF):
                pool.wait_ge(*turn(xn_stored[h], PAIRS_OF_BATCHES, 0))
            for u in range(U):
                gather(0, u)
            with pool.Fori(0, TURNS - 1) as i:
                for u in range(U):
                    gather(i + 1, u)
                    scatter(i, u)
            for u in range(U):
                scatter(TURNS - 1, u)

        @block.scalar
        def _(act):
            with act.Fori(0, PAIRS_OF_BATCHES) as i:
                for h in range(HALF):
                    act.wait_ge(*turn(turned, i, h + 1))
                    act.activation(XT[:, :], PS[h][:, :], ACT.Copy).then_inc(sem(copied), 1)
                    act.wait_ge(*turn(logits, i, h + 1))
                    act.sem_inc(sem(ready), 1)
                    act.activation(key[:, bass.ds((i * HALF + h) * T, T), :],
                                   PS[2 + h][:, 0:T * E].rearrange("p (t e) -> p t e", e=E), ACT.Copy
                                   ).then_inc(sem(collected), 1)
            act.wait_ge(route, 3 if first else 2)
            act.activation(ex[:, :, :], work[:, :, :], ACT.Exp).then_inc(exps, 1)
            with act.Fori(0, TURNS) as i:
                for u in range(U):
                    act.wait_ge(*turn(y, i, u - 1))
                    for f in range(FC):
                        if f % 2 == 0:
                            act.wait_ge(*turn(hidden, i, 2 * u + f // 2 + 1))
                        act.activation(hT[:, u % 2, f, :], PS[2 + 2 * (u % 2) + f // 2][:, (f % 2) * P:(f % 2 + 1) * P],
                                       func, bias=W1s[:, u % 2, F + f:F + f + 1]).then_inc(sem(acted), 1)

        @block.vector
        def _(dve):
            with dve.Fori(0, B) as i:
                for t in range(T):
                    dve.bn_stats(c["stat"][:, t, :], X[:, bass.ds(i * T + t, 1), :].rearrange("p a d -> p (a d)")
                                 ).then_inc(sem(stats), 1)
                dve.wait_ge(*turn(stats, i, T))
                dve.memset(c["pad"][:, :], 0.0)
                for t in range(T):
                    dve.bn_aggr(c["mv"][:, t, :], c["stat"][:, t, :]).then_inc(sem(mean), 1)
                dve.wait_ge(*turn(mean, i, T))
                dve.tensor_scalar(mva[:, bass.ds(i * T, T), :], c["mv"][:, :, :], 1.0, None, ALU.mult
                                  ).then_inc(sem(kept), 1)
            dve.wait_ge(*turn(kept, B, 0))
            dve.wait_ge(rooted, 2)
            with dve.Fori(0, PAIRS_OF_BATCHES) as i:
                for h in range(HALF):
                    dve.wait_ge(*turn(xn_stored[h], i, 0))
                    dve.wait_ge(*turn(turned, i, h + 1 - HALF))
                    for t in range(T):
                        n = (i * HALF + h) * T + t
                        dve.tensor_scalar(XN[h][:, t, :], X[:, bass.ds(n, 1), :].rearrange("p a d -> p (a d)"),
                                          mva[:, bass.ds(n, 1), 0], root[:, 1, bass.ds(n, 1)],
                                          ALU.subtract, ALU.mult).then_inc(sem(out), 1)
            dve.wait_ge(*turn(collected, PAIRS_OF_BATCHES, 0))
            dve.wait_ge(loads, LOADS)
            dve.wait_ge(made, 12)
            done = [0]

            def step(ins_):
                done[0] += 1
                ins_.then_inc(route, 1)
                dve.wait_ge(route, done[0])

            def best(src, most, dst):
                step(dve.tensor_reduce(red[:, most, :], src, AX_X, ALU.max))
                step(dve.tensor_tensor(eq[:, :, :], src, widen(red[:, most, :], E), ALU.is_equal))
                step(dve.tensor_tensor(eq[:, :, :], eq[:, :, :], desc[:, :, :], ALU.mult))
                step(dve.tensor_reduce(red[:, 3, :], eq[:, :, :], AX_X, ALU.max))
                step(dve.tensor_tensor(dst, desc[:, :, :], widen(red[:, 3, :], E), ALU.is_equal))

            def total(dst, src):
                step(dve.tensor_reduce(dst, src, AX_X, ALU.add))

            if first:
                step(dve.tensor_tensor(key[:, :, :], key[:, :, :], over(br[:, :], 1, NG), ALU.add))
            step(dve.tensor_reduce(red[:, 0, :], key[:, :, :], AX_X, ALU.max))
            step(dve.tensor_tensor(work[:, :, :], key[:, :, :], widen(red[:, 0, :], E), ALU.subtract))
            dve.wait_ge(exps, 1)
            if first:
                total(red[:, 1, :], ex[:, :, :])
                step(dve.reciprocal(red[:, 2, :], red[:, 1, :]))
                step(dve.tensor_tensor(key[:, :, :], ex[:, :, :], widen(red[:, 2, :], E), ALU.mult))
            best(key[:, :, :], 0, choice[:, 0, :, :])
            step(dve.scalar_tensor_tensor(work[:, :, :], choice[:, 0, :, :], -3.0e38, key[:, :, :], ALU.mult, ALU.add))
            best(work[:, :, :], 1, choice[:, 1, :, :])
            step(dve.tensor_tensor(both[:, :, :], choice[:, 0, :, :], choice[:, 1, :, :], ALU.add))
            with nc.allow_low_precision("counts up to the number of tiles are exact"):
                total(load[:, :], both[:, :, :].rearrange("p n e -> p e n"))
            assert done[0] == SORTED, done
            prob = key if first else ex
            for k in range(CH):
                step(dve.tensor_tensor(eq[:, :, :], choice[:, k, :, :], prob[:, :, :], ALU.mult))
                total(gate[:, k, :], eq[:, :, :])
            if not first:
                step(dve.tensor_tensor(red[:, 1, :], gate[:, 0, :], gate[:, 1, :], ALU.add))
                step(dve.reciprocal(red[:, 2, :], red[:, 1, :]))
                step(dve.tensor_tensor(gate[:, :, :], gate[:, :, :], over(red[:, 2, :], 1, CH), ALU.mult))
            dve.wait_ge(ranked, 1)
            step(dve.tensor_copy(count[:, :], PS[7][:, 0:E]))
            step(dve.tensor_tensor(full[:, :, :], widen(count[:, :], NG), steps[:, :, :], ALU.is_gt))
            total(tiles[:, 0, :], full[:, :, :])
            src, s = 0, 1
            while s < E:
                dst = 2 if src == 1 else 1
                step(dve.tensor_copy(tiles[:, dst, 0:s], tiles[:, src, 0:s]))
                step(dve.tensor_tensor(tiles[:, dst, s:E], tiles[:, src, s:E], tiles[:, src, 0:E - s], ALU.add))
                src, s = dst, 2 * s
            step(dve.tensor_tensor(start[:, :], tiles[:, src, :], tiles[:, 0, :], ALU.subtract))
            step(dve.tensor_scalar(start[:, :], start[:, :], float(P), None, ALU.mult))
            dve.wait_ge(ranked, 2)
            step(dve.tensor_tensor(work[:, :, :], PS[6][:, 0:NG * E].rearrange("p (n e) -> p n e", e=E),
                                   over(start[:, :], 1, NG), ALU.add))
            for k in range(CH):
                step(dve.tensor_tensor(eq[:, :, :], choice[:, k, :, :], work[:, :, :], ALU.mult))
                total(place[:, k, :], eq[:, :, :])
            step(dve.tensor_copy(place_i[:, 0, :, :], place[:, :, :]))
            step(dve.tensor_scalar(place_i[:, 1, :, :], place_i[:, 0, :, :], P.bit_length() - 1, None,
                                   ALU.logical_shift_right))
            step(dve.tensor_scalar(place_i[:, 2, :, :], place_i[:, 0, :, :], P - 1, None, ALU.bitwise_and))
            step(dve.tensor_copy(tile_of[:, :, :], place_i[:, 1, :, :]))
            step(dve.tensor_copy(row[:, :, :], place_i[:, 2, :, :]))
            step(dve.tensor_tensor(code[:, 0, :, :], base[:, 0, :, :], tile_of[:, :, :], ALU.subtract))
            step(dve.tensor_tensor(code[:, 1, :, :], base[:, 1, :, :], row[:, :, :], ALU.subtract))
            step(dve.tensor_tensor(past[:, :, :], widen(numbers[:, 0:NT], E), over(tiles[:, src, :], 1, NT), ALU.is_ge))
            total(owner[:, 0, :], past[:, :, :])
            step(dve.tensor_scalar(owner[:, 1, :], owner[:, 0, :], float(E - 1), None, ALU.min))
            step(dve.tensor_copy(owner_i[:, :], owner[:, 1, :]))
            with dve.Fori(0, PAIRS_OF_BATCHES) as i:
                for h in range(HALF):
                    at = (i * HALF + h) * T
                    dve.wait_ge(*turn(told, i, h + 1 - HALF))
                    for k in range(CH):
                        dve.tensor_tensor(is_row[:, h, k, :, :], over(numbers[:, :], 1, T),
                                          widen(row[:, k, bass.ds(at, T)], P), ALU.is_equal).then_inc(sem(coded), 1)
                        for t in range(T):
                            for z in range(2):
                                dve.tensor_scalar(is_tile[:, h, k, t, z * NT:(z + 1) * NT], numbers[:, 0:NT],
                                                  tile_of[:, k, bass.ds(at + t, 1)], code[:, z, k, bass.ds(at + t, 1)],
                                                  ALU.is_equal, ALU.mult).then_inc(sem(coded), 1)
            dve.wait_ge(inverse, 1)
            step(dve.scalar_tensor_tensor(dest[:, 0, :], PS[5][:, 0:NT], float(P), spare[:, :], ALU.mult, ALU.add))
            step(dve.tensor_tensor(dest[:, 1, :], PS[5][:, NT:2 * NT], dest[:, 0, :], ALU.add))
            step(dve.tensor_copy(dest_i[:, 0, :], dest[:, 1, :]))
            step(dve.tensor_scalar(dest_i[:, 1, :], dest_i[:, 0, :], TOK - 1, None, ALU.bitwise_and))
            step(dve.tensor_copy(source[:, :], dest_i[:, 1, :]))

            def set_source(i, u, opening=False):
                if not opening:
                    dve.wait_ge(*turn(gathered[u], i, 0))
                dve.tensor_scalar(gi[:, u:u + 1], source[:, bass.ds(i * U + u, 1)], 1.0, None, ALU.mult
                                  ).then_inc(sem(gi_set), 1)

            def set_dest(i, u, opening):
                if not opening:
                    dve.wait_ge(*turn(scattered[u], i, 0))
                dve.tensor_scalar(si[:, u:u + 1], dest[:, 1, bass.ds(i * U + u, 1)], 1.0, None, ALU.mult
                                  ).then_inc(sem(si_set), 1)

            def set_weights(i, u):
                e = expert_of(dve, i, u)
                dve.wait_ge(*turn(acted, i, FC * (u - 1)))
                dve.tensor_scalar(W1s[:, u % 2, :], W1[:, bass.ds(e, 1), :].rearrange("p a f -> p (a f)"), 1.0, None,
                                  ALU.mult).then_inc(sem(w1_set), 1)

            def set_tokens(i, u):
                dve.wait_ge(*turn(g_turned, i, u + 1))
                dve.wait_ge(*turn(hidden, i, 2 * (u - 1)))
                dve.tensor_copy(xT[:, u % 2, :], PS[u % 2][:, 0:P]).then_inc(sem(g_copied), 1)

            def set_result(i, u):
                e = expert_of(dve, i, u)
                dve.wait_ge(*turn(y, i, u + 1))
                dve.tensor_tensor(ys[:, u, :], PS[6 + u % 2][:, 0:D], b2[:, bass.ds(e, 1), :].rearrange("p a d -> p (a d)"),
                                  ALU.add).then_inc(sem(y_set), 1)

            for u in range(U):
                set_source(0, u, True)
            for u in range(2):
                set_weights(0, u)
                set_tokens(0, u)

            def tile(i, u, opening=False, last=False):
                if not last:
                    set_source(i + 1, u)
                if not last or u + 2 < U:
                    set_tokens(*ahead(i, u, 2))
                    set_weights(*ahead(i, u, 2))
                set_dest(i, u, opening)
                set_result(i, u)

            for u in range(U):
                tile(0, u, opening=True)
            with dve.Fori(1, TURNS - 1) as i:
                for u in range(U):
                    tile(i, u)
            for u in range(U):
                tile(TURNS - 1, u, last=True)
            with dve.Fori(0, PAIRS_OF_BATCHES) as i:
                for h in range(HALF):
                    dve.wait_ge(*turn(y_loaded[h], i, 16 * CH))
                    for k, mixed in enumerate((mixed1, mixed2)):
                        if k:
                            dve.wait_ge(*turn(mixed1, i, (h + 1) * T))
                        for t in range(T):
                            n = (i * HALF + h) * T + t
                            xt = X[:, bass.ds(n, 1), :].rearrange("p a d -> p (a d)")
                            dve.scalar_tensor_tensor(xt, got[:, h, k, t, :], gate[:, k, bass.ds(n, 1)], xt,
                                                     ALU.mult, ALU.add).then_inc(sem(mixed), 1)
            dve.wait_ge(*turn(mixed2, PAIRS_OF_BATCHES, 0))

        @block.tensor
        def _(pe):
            pe.wait_ge(loads, LOADS)
            with pe.Fori(0, PAIRS_OF_BATCHES) as i:
                for h in range(HALF):
                    pe.wait_ge(*turn(out, i, (h + 1) * T))
                    for t in range(T):
                        last = pe.transpose(PS[h][:, t * P:(t + 1) * P], XN[h][:, t, :], ident[:, :])
                    last.then_inc(sem(turned), 1)
                    pe.wait_ge(*turn(copied, i, h + 1))
                    pe.wait_ge(*turn(collected, i, h + 1 - HALF))
                    for t in range(T):
                        last = pe.matmul(PS[2 + h][:, t * E:(t + 1) * E], XT[:, t * P:(t + 1) * P], wr[:, :],
                                         start=True, stop=True)
                    last.then_inc(sem(logits), 1)
            pe.wait_ge(made, 12)
            pe.wait_ge(route, SORTED)
            pe.matmul(PS[7][:, 0:E], ones[:, :], load[:, :], start=True, stop=True).then_inc(ranked, 1)
            flat = both[:, :, :].rearrange("p n e -> p (n e)")
            pe.matmul(PS[6][:, 0:NG * E], tri[:, :], flat, start=True, stop=False)
            for n in range(1, NG):
                last = pe.matmul(PS[6][:, n * E:NG * E], ones[:, :], flat[:, 0:(NG - n) * E],
                                 start=False, stop=(n == NG - 1))
            last.then_inc(ranked, 1)
            pe.matmul(PS[5][:, 0:2 * NT], ones[:, :], zeros[:, :], start=True, stop=False)
            with pe.Fori(0, PAIRS_OF_BATCHES) as i:
                for h in range(HALF):
                    pe.wait_ge(*turn(coded, i, (h + 1) * CODES))
                    for k in range(CH):
                        for t in range(T):
                            last = pe.matmul(PS[5][:, 0:2 * NT], is_row[:, h, k, t, :], is_tile[:, h, k, t, :],
                                             start=False, stop=False)
                    last.then_inc(sem(told), 1)
            pe.matmul(PS[5][:, 0:2 * NT], ones[:, :], zeros[:, :], start=False, stop=True).then_inc(inverse, 1)

            def turn_tokens(i, u):
                pe.wait_ge(*turn(gathered[u], i, 16))
                pe.wait_ge(*turn(g_copied, i, u - 1))
                pe.transpose(PS[u % 2][:, 0:P], xg[:, u, :], ident[:, :]).then_inc(sem(g_turned), 1)

            def first_product(i, u):
                pe.wait_ge(*turn(g_copied, i, u + 1))
                pe.wait_ge(*turn(w1_set, i, u + 1))
                pe.wait_ge(*turn(acted, i, FC * (u - 1)))
                for f in range(FC):
                    last = pe.matmul(PS[2 + 2 * (u % 2) + f // 2][:, (f % 2) * P:(f % 2 + 1) * P],
                                     W1s[:, u % 2, f * P:(f + 1) * P], xT[:, u % 2, :], start=True, stop=True)
                    if f % 2:
                        last.then_inc(sem(hidden), 1)

            def second_product(i, u):
                e = expert_of(pe, i, u)
                pe.wait_ge(*turn(acted, i, FC * (u + 1)))
                pe.wait_ge(*turn(y_set, i, u - 1))
                for f in range(FC):
                    last = pe.matmul(PS[6 + u % 2][:, 0:D], hT[:, u % 2, f, :],
                                     W2[:, bass.ds(e, 1), f, :].rearrange("p a d -> p (a d)"),
                                     start=(f == 0), stop=(f == FC - 1))
                last.then_inc(sem(y), 1)

            def tile(i, u, last):
                if not last or u + 1 < U:
                    first_product(*ahead(i, u, 1))
                if not last or u + 2 < U:
                    turn_tokens(*ahead(i, u, 2))
                second_product(i, u)

            pe.wait_ge(*turn(gi_set, 0, 1))
            turn_tokens(0, 0)
            turn_tokens(0, 1)
            first_product(0, 0)
            with pe.Fori(0, TURNS - 1) as i:
                for u in range(U):
                    tile(i, u, False)
            for u in range(U):
                tile(TURNS - 1, u, True)




_HEAD_ROWS_A = [2, 3, 1, 0, 2, 0]
_HEAD_ROWS_B = [3, 1, 2, 3, 0, 1]
_LINE_A = [0, 0, 0, 1, 1, 2]
_LINE_B = [1, 2, 3, 2, 3, 3]


def rotary():
    f = np.float32
    freq = f(1.0) / f(10000.0) ** (np.arange(0, HD, 2, dtype=f) / f(HD))
    angle = np.arange(S, dtype=f)[:, None] * freq[None, :]
    cos = np.tile(np.repeat(np.cos(angle), 2, axis=1), (1, H)).T
    sin = np.tile(np.repeat(np.sin(angle), 2, axis=1) * np.tile(f([-1, 1]), HD // 2), (1, H)).T
    scale = f(1.0) / np.sqrt(f(HD))
    turned = np.arange(D).reshape(H, HD).T.reshape(-1)
    return np.ascontiguousarray(np.stack([cos * scale, sin * scale, cos, sin])[:, turned].astype(f))


def lay_out(v):
    turned = np.arange(D).reshape(H, HD).T.reshape(-1)
    swap = turned ^ 1
    col = lambda a: np.asarray(a).reshape(-1, 1)
    g = {}
    g["x"] = np.asarray(v["L0_attn_x"]).reshape(B * S, D)
    g["Wv"], g["Wo"] = v["L0_attn_Wv"], v["L0_attn_Wo"]
    for n in "qk":
        g["W" + n] = np.asarray(v["L0_attn_W" + n])[:, turned]
        g[f"W{n}s"] = np.asarray(v["L0_attn_W" + n])[:, swap]
    bq, bk = np.asarray(v["L0_attn_bq"]), np.asarray(v["L0_attn_bk"])
    g["acols"] = np.concatenate([col(bq[turned]), col(bq[swap]), col(bk[turned]), col(bk[swap]), col(v["L0_attn_g1"]),
                                 col(v["L0_attn_beta1"]), col(v["L0_attn_g2"]), col(v["L0_attn_beta2"])], axis=1)
    g["bv"], g["bo"], g["ab2"] = v["L0_attn_bv"], v["L0_attn_bo"], v["L0_attn_b2"]
    g["aW1"], g["aW2"] = v["L0_attn_W1"], v["L0_attn_W2"]
    g["ab1"] = np.asarray(v["L0_attn_b1"]).reshape(FC, P).T
    g["rope"] = rotary()
    g["L0_w1"] = np.asarray(v["L0_ffn_W1"]).transpose(1, 0, 2)
    g["L0_w2"] = np.asarray(v["L0_ffn_W2"]).reshape(E0, FC, P, D).transpose(2, 0, 1, 3)
    g["L0_b1"] = np.asarray(v["L0_ffn_b1"]).reshape(E0, FC, P).transpose(2, 0, 1)
    g["L0_b2"], g["L0_wr"], g["L0_br"] = v["L0_ffn_b2"], v["L0_ffn_Wr"], v["L0_ffn_br"]
    g["L1_w1"] = np.asarray(v["L1_ffn_w1"]).transpose(2, 0, 1)
    g["L1_w2"] = np.asarray(v["L1_ffn_w2"]).transpose(0, 2, 1).reshape(E1, FC, P, D).transpose(2, 0, 1, 3)
    g["L1_b1"] = np.asarray(v["L1_ffn_b1"]).reshape(E1, FC, P).transpose(2, 0, 1)
    g["L1_b2"], g["L1_wr"] = v["L1_ffn_b2"], np.asarray(v["L1_ffn_router_w"]).T
    heads = np.arange(H)[None, :] * 4
    pick = lambda w, rows: np.asarray(w)[(heads + np.array(rows)[:, None]).reshape(-1), :].T
    order = np.concatenate([turned, D + turned, np.arange(2 * D, 3 * D)])
    g["c_qkv"] = np.asarray(v["L1_attn_w_qkv"])[order].T
    g["c_wo"] = np.asarray(v["L1_attn_w_out"]).T
    g["c_read"] = np.concatenate([pick(v["L1_attn_w1_read"], _LINE_A), pick(v["L1_attn_w2_read"], _LINE_B),
                                  pick(v["L1_attn_w1_read"], _LINE_B), pick(v["L1_attn_w2_read"], _LINE_A)], axis=1)
    g["c_write1"] = np.concatenate([pick(v["L1_attn_w1_write"], _HEAD_ROWS_A),
                                    pick(v["L1_attn_w1_write"], _HEAD_ROWS_B)], axis=1)
    g["c_write2"] = np.concatenate([pick(v["L1_attn_w2_write"], _HEAD_ROWS_B),
                                    pick(v["L1_attn_w2_write"], _HEAD_ROWS_A)], axis=1)
    bqkv = np.asarray(v["L1_attn_b_qkv"])
    g["c_cols"] = np.stack([bqkv[0:D][turned], bqkv[D:2 * D][turned]], axis=1)
    g["c_bv"], g["c_bo"] = bqkv[2 * D:3 * D], v["L1_attn_b_out"]
    g["c_decay"], g["c_bias"] = v["L1_attn_decay_logits"], v["L1_attn_bias_scale"]
    return {k: np.ascontiguousarray(a) for k, a in g.items()}


def kernel(**inputs):
    import numpy as _np
    import concourse.bacc as _bacc
    from concourse import mybir as _mybir
    from concourse.bass_utils import run_bass_kernel_spmd as _run

    nc = _bacc.Bacc("TRN2", target_bir_lowering=False, num_devices=1)
    laid = lay_out(inputs)
    ins = {n: nc.dram_tensor(f"in_{n}", a.shape, _mybir.dt.from_np(a.dtype), kind="ExternalInput").ap()
           for n, a in laid.items()}
    out = nc.dram_tensor("out_x", (B * S, D), F32, kind="ExternalOutput").ap()
    build(nc, ins, out)
    r = _run(nc, [{f"in_{n}": a for n, a in laid.items()}], core_ids=[0])
    return _np.asarray(r.results[0]["out_x"]).reshape(B, S, D)
```

```python
from contextlib import ExitStack

import numpy as np

import concourse.bass as bass
from concourse import mybir

F32 = mybir.dt.float32
BF16 = mybir.dt.bfloat16
I32 = mybir.dt.int32
ALU = mybir.AluOpType
ACT = mybir.ActivationFunctionType
AX_X = mybir.AxisListType.X

P = 128
D = 128
B, S = 8, 512
T = S // P
H = 16
HD = D // H
QUAD = 4
F = 512
FC = F // P
E0, E1 = 16, 8
EPS = 1e-5
PARTS = 3
PAIRS = PARTS * PARTS
STACK = PAIRS * HD
KR0 = 96


def sem(signal):
    return signal[0]


def per_turn(signal):
    return signal[1]


def turn(signal, i, n):
    return signal[0], i * signal[1] + (n + signal[2])


def over(ap, axis, n):
    shape = list(ap.shape)
    return ap.unsqueeze(axis).to_broadcast(shape[:axis] + [n] + shape[axis:])


def prime(pool, signals):
    for s in signals:
        pool.sem_inc(sem(s), s[2])


def clear(nc, semaphores):
    with nc.Block() as block:
        @block.gpsimd
        def _(pool):
            for s in semaphores:
                pool.sem_clear(s)


def widen(ap, n):
    k = len(ap.shape)
    return ap.unsqueeze(k).to_broadcast(list(ap.shape) + [n])


def build(nc, ins, out, phases="ABCD"):
    ctx = ExitStack()
    with ctx:
        def sb(name, shape, dt=F32):
            return ctx.enter_context(nc.sbuf_tensor(name, shape, dt))

        def dram(name, shape, dt):
            return nc.dram_tensor(name, shape, dt).ap()

        X = sb("X", [P, B * T, D])
        ident = sb("ident", [P, P])
        half = sb("half", [P, T])
        eps = sb("eps", [P, T])
        pad = sb("pad", [P, 1])
        XN = sb("XN", [P, T, D])
        YN = sb("YN", [P, T, D])
        YT = sb("YT", [P, S])
        stat = sb("stat", [P, T, 6])
        mv = sb("mv", [P, T, 2])
        ve = sb("ve", [P, T])
        rstd = sb("rstd", [P, T])
        common = dict(X=X, ident=ident, half=half, eps=eps, pad=pad, XN=XN, YN=YN, YT=YT, stat=stat, mv=mv, ve=ve, rstd=rstd)

        for tag in ("L0", "L1"):
            for name in ("gathered", "scattered"):
                common[f"{tag}_{name}"] = [ctx.enter_context(nc.semaphore(f"{tag}_{name}{u}")) for u in range(4)]
        for name in ("loaded", "made", "stored"):
            common[name] = ctx.enter_context(nc.semaphore(name))
        load_inputs(nc, ins, common)
        if "A" in phases:
            layer0_attention(nc, ins, common)
        if "B" in phases:
            experts(nc, ins, common, "L0", E0)
        if "C" in phases:
            layer1_attention(nc, ins, common)
        if "D" in phases:
            experts(nc, ins, common, "L1", E1)

        stored = common["stored"]
        with nc.Block() as block:
            @block.sync
            def _(sp):
                sp.dma_start(out.rearrange("(n p) d -> p n d", p=P), X[:, :, :]).then_inc(stored, 16)
                sp.wait_ge(stored, 16)


def load_inputs(nc, ins, c):
    loaded, made = c["loaded"], c["made"]
    with nc.Block() as block:
        @block.sync
        def _(sp):
            sp.dma_start(c["X"][:, :, :], ins["x"].rearrange("(n p) d -> p n d", p=P)).then_inc(loaded, 16)
            sp.wait_ge(loaded, 16)

        @block.gpsimd
        def _(pool):
            pool.memset(c["ident"][:, :], 0.0).then_inc(made, 1)
            pool.memset(c["half"][:, :], -0.5)
            pool.memset(c["eps"][:, :], EPS)
            pool.wait_ge(made, 1)
            pool.affine_select(out=c["ident"][:, :], in_=c["ident"][:, :], compare_op=ALU.not_equal, fill=1.0,
                               base=0, pattern=[[-1, P]], channel_multiplier=1)


def spread(rows):
    return rows[:, :].unsqueeze(1).to_broadcast([rows.shape[0], H, S])


def norm_signals(sig, per):
    return {"stats": sig("norm_stats", T * per), "mean": sig("norm_mean", T * per),
            "eps_added": sig("norm_eps_added", per), "rstd": sig("norm_rstd", per), "out": sig("norm_out", T * per)}


def norm_measure(dve, c, norm, i, j, src):
    if j > 0:
        dve.wait_ge(*turn(norm["out"], i, j * T))
    for t in range(T):
        dve.bn_stats(c["stat"][:, t, :], src(t)).then_inc(sem(norm["stats"]), 1)
    dve.wait_ge(*turn(norm["stats"], i, (j + 1) * T))
    dve.memset(c["pad"][:, :], 0.0)
    for t in range(T):
        dve.bn_aggr(c["mv"][:, t, :], c["stat"][:, t, :]).then_inc(sem(norm["mean"]), 1)


def norm_root(pool, c, norm, i, j):
    pool.wait_ge(*turn(norm["mean"], i, (j + 1) * T))
    pool.tensor_tensor(c["ve"][:, :], c["mv"][:, :, 1], c["eps"][:, :], ALU.add).then_inc(sem(norm["eps_added"]), 1)
    pool.wait_ge(*turn(norm["eps_added"], i, j + 1))
    pool.tensor_tensor(c["rstd"][:, :], c["ve"][:, :], c["half"][:, :], ALU.pow).then_inc(sem(norm["rstd"]), 1)


def norm_scale(dve, c, norm, i, j, dst, src):
    dve.wait_ge(*turn(norm["rstd"], i, j + 1))
    for t in range(T):
        dve.tensor_scalar(dst(t), src(t), c["mv"][:, t, 0:1], c["rstd"][:, t:t + 1],
                          ALU.subtract, ALU.mult).then_inc(sem(norm["out"]), 1)


def norm_wait(eng, norm, i, j):
    eng.wait_ge(*turn(norm["out"], i, (j + 1) * T))


def stack_left(sp, stack, row, width, parts_d, signal, head=0):
    for a in range(PARTS):
        rows = PARTS * width
        src = heads_of(parts_d[a].rearrange("(d h) s -> d (h s)", d=width), stack, head)
        sp.dma_start(stack[row + a * rows:row + (a + 1) * rows],
                     src.unsqueeze(0).to_broadcast([PARTS] + list(src.shape))).then_inc(signal, 16)


def heads_of(src, stack, head):
    _, n, columns = stack.shape
    return src[:, head * columns:(head + n) * columns]


def stack_right(sp, stack, row, width, parts_d, signal, head=0):
    src = heads_of(parts_d.rearrange("b (d h) s -> (b d) (h s)", d=width), stack, head)
    sp.dma_start(stack[row:row + PAIRS * width],
                 src.unsqueeze(0).to_broadcast([PARTS] + list(src.shape))).then_inc(signal, 16)


def layer0_attention(nc, ins, c):
    with ExitStack() as ctx:
        def sb(name, shape, dt=F32):
            return ctx.enter_context(nc.sbuf_tensor(name, shape, dt))

        signals, flags = [], []

        def sig(name, per=1, start=1):
            signals.append((ctx.enter_context(nc.semaphore(f"a_{name}")), per, start))
            return signals[-1]

        def flag(name):
            flags.append(ctx.enter_context(nc.semaphore(f"a_{name}")))
            return flags[-1]

        X, XN, YN, YT, ident = c["X"], c["XN"], c["YN"], c["YT"], c["ident"]
        W = sb("a_W", [P, 6, D])
        W1 = sb("a_W1", [P, F])
        W2 = sb("a_W2", [P, FC, D])
        cols = sb("a_cols", [P, 8])
        b1c = sb("a_b1c", [P, FC])
        bv = sb("a_bv", [P, 2, D])
        bo = sb("a_bo", [P, T, D])
        b2 = sb("a_b2", [P, T, D])
        rope = sb("a_rope", [P, 4, S])
        rot = sb("a_rot", [P, 2, 2, S])
        part = sb("a_part", [P, 2, PARTS, S], BF16)
        QS = sb("a_QS", [P, H, S], BF16)
        KS = sb("a_KS", [P, H, S], BF16)
        zero = sb("a_zero", [2, S], BF16)
        one = sb("a_one", [2, S], BF16)
        V = sb("a_V", [P, T, H, 32])
        M = sb("a_M", [P, T, H])
        mh = sb("a_mh", [QUAD, 2, S], BF16)
        ml = sb("a_ml", [QUAD, 2, S], BF16)
        PT = sb("a_PT", [P, 8, 2, S])
        pvs = sb("a_pvs", [P, S])
        rec = sb("a_rec", [P, T, QUAD])
        AT = sb("a_AT", [P, T, D])
        ATT = sb("a_ATT", [P, S])
        XB = sb("a_XB", [P, T, D])
        XA = sb("a_XA", [P, T, D])
        XC = sb("a_XC", [P, T, D])
        ZN = sb("a_ZN", [P, T, D])
        ZT = sb("a_ZT", [P, S])
        hT = sb("a_hT", [P, FC, S])
        tail_c = {name: sb(f"a_t{name}", list(c[name].shape)) for name in ("stat", "mv", "ve", "rstd", "pad")}
        tail_c["eps"], tail_c["half"] = c["eps"], c["half"]
        parts_d = nc.dram_tensor("a_parts", [2, PARTS, P, S], BF16).ap()
        FB = [ctx.enter_context(nc.psum_tensor(f"a_F{n}", [P, S], F32)) for n in range(2)]
        ST = [ctx.enter_context(nc.psum_tensor(f"a_ST{n}", [P, 2, S], F32)) for n in range(2)]
        PV = ctx.enter_context(nc.psum_tensor("a_PV", [P, S], F32))
        TB = ctx.enter_context(nc.psum_tensor("a_TB", [P, S], F32))

        NQ = H // QUAD
        UQ = 2 * QUAD
        UNITS = NQ * UQ
        weights, const, vmade = flag("weights"), flag("const"), flag("vmade")
        norm, tail_norm = norm_signals(sig, 2), norm_signals(lambda name, per: sig("t" + name, per), 1)
        turned, yT = sig("turned"), sig("yT")
        projected, roped = sig("projected", 4), sig("roped", 4)
        valued, vdone = sig("valued", 3), sig("vdone", 3)
        filled, maxed = sig("filled", H * T), sig("maxed", H * T)
        at_turned, attT = sig("at_turned"), sig("attT")
        wo, resid = sig("wo"), sig("resid")
        z_turned, zT = sig("z_turned"), sig("zT")
        hidden, relu_a, relu_v = sig("hidden", FC), sig("relu_a", FC // 2), sig("relu_v", FC // 2)
        ffn, summed_up = sig("ffn"), sig("summed_up", 1)
        summed, cast, rest = sig("summed", 2), sig("cast", 4), sig("rest", 4)
        q_stored, k_stored = sig("q_stored", 16), sig("k_stored", 16)
        stacked = [sig(f"stacked{n}", 16 * (PARTS + 2)) for n in range(NQ // 2)]
        mturned, mhigh, mlow = sig("mturned", NQ), sig("mhigh", NQ), sig("mlow", NQ)
        mstacked = sig("mstacked", 32 * NQ, 33)
        scored, exped = sig("scored", UNITS), sig("exped", UNITS, 2)
        pv, pvcopied, pvturned = sig("pv", 2 * NQ, 2), sig("pvcopied", NQ), sig("pvturned", NQ)
        inv, attn = sig("inv", NQ), sig("attn", NQ, 2)
        passed = sig("passed", NQ // 2 + 2)
        biased, biased2, added = sig("biased"), sig("biased2"), sig("added")

        V_FILLS = [(0, 2), (2, 1), (3, 1)]
        readers = {"turned": (yT, lambda n: 1), "projected": (roped, lambda n: n + 1),
                   "valued": (vdone, lambda n: n + 1), "logits": (maxed, lambda n: n + 1),
                   "at": (attT, lambda n: 1), "wo": (resid, lambda n: 1), "z": (zT, lambda n: 1),
                   "hidden": (None, None), "ffn": (summed_up, lambda n: 1)}
        TURNED_AT, ROTATED_AT, SPLIT_AT, Z_AT, HIDDEN_AT, FFN_AT = 6, (8, 9, 10, 11), (10, 11, 12, 13), 17, (18, 20, 22, 24), 27
        PLAN = ([(0, ("at", -1, 0)), (2, ("wo", -1, 0)), (TURNED_AT, ("turned", 1, 0))]
                + [(u, ("projected", 1, n)) for n, u in enumerate(ROTATED_AT)] + [(Z_AT, ("z", -1, 0))]
                + [(u, ("hidden", -1, n)) for n, u in enumerate(HIDDEN_AT)] + [(FFN_AT, ("ffn", -1, 0))])
        EXTRA = {u: [use for at, use in PLAN if at == u] for u in range(UNITS)}

        def next_logits(u, prep):
            g = u // UQ
            if g == NQ - 1 and not prep:
                return []
            return [((g + 1) // NQ, (QUAD * T + n) % (H * T)) for n in (2 * u, 2 * u + 1)]

        def beside(u, prep):
            return [] if u and u % UQ == 0 else next_logits(u, prep)

        def early(u, prep):
            return next_logits(u + 1, prep) if u % UQ == UQ - 1 and u + 1 < UNITS else []

        def extras(u, tail, prep):
            return [use for use in EXTRA.get(u, []) if (tail if use[1] < 0 else prep)]

        def table(uses, before):
            before = [(kind, batch - 1, n) for kind, batch, n in before[-2:]]
            assert len(uses) % 2 == 0
            return {use: (n % 2, (before + uses)[n]) for n, use in enumerate(uses)}

        def uses_of(tail, prep):
            uses = []
            for u in range(UNITS):
                uses += [("logits", batch, n) for batch, n in beside(u, prep)]
                uses += extras(u, tail, prep)
                uses += [("logits", batch, n) for batch, n in early(u, prep)]
            return uses + ([("valued", 1, n) for n in range(3)] if prep else [])

        OPENING = ([("turned", 1, 0)] + [("projected", 1, n) for n in range(4)] + [("logits", 1, n) for n in range(16)]
                   + [("valued", 1, n) for n in range(3)])
        CLOSING = [use for u in range(UNITS) for use in extras(u, True, False)]
        opening = table(OPENING, [("turned", 1, 0)] * 2)
        first_turn = table(uses_of(False, True), OPENING)
        middle = table(uses_of(True, True), uses_of(False, True))
        last_turn = table(uses_of(True, False), uses_of(True, True))
        closing = table(CLOSING, uses_of(True, False))

        def turns(eng, run):
            run(0, False, True, first_turn)
            with eng.Fori(1, B - 1) as i:
                run(i, True, True, middle)
            run(B - 1, True, False, last_turn)

        def bank(tab, use):
            return FB[tab[use][0]]

        block_weights = 16 * 22
        ctx.callback(clear, nc, [sem(s) for s in signals] + flags)
        block = ctx.enter_context(nc.Block())

        @block.sync
        def _(sp):
            for n, name in enumerate(["Wq", "Wqs", "Wk", "Wks", "Wv", "Wo"]):
                sp.dma_start(W[:, n, :], ins[name]).then_inc(weights, 16)
            sp.dma_start(W1[:, :], ins["aW1"]).then_inc(weights, 16)
            sp.dma_start(W2[:, :, :], ins["aW2"].rearrange("(c p) d -> p c d", p=P)).then_inc(weights, 16)
            sp.dma_start(cols[:, :], ins["acols"]).then_inc(weights, 16)
            sp.dma_start(b1c[:, :], ins["ab1"]).then_inc(weights, 16)
            sp.dma_start(rope[:, :, :], ins["rope"].rearrange("c p s -> p c s")).then_inc(weights, 16)
            for t in range(T):
                if t < 2:
                    sp.dma_start(bv[:, t, :], ins["bv"].partition_broadcast(P)).then_inc(weights, 16)
                sp.dma_start(bo[:, t, :], ins["bo"].partition_broadcast(P)).then_inc(weights, 16)
                sp.dma_start(b2[:, t, :], ins["ab2"].partition_broadcast(P)).then_inc(weights, 16)
            sp.wait_ge(const, 4)
            sp.dma_start(KS[STACK:STACK + 2, :, :], spread(one)).then_inc(weights, 16)
            sp.wait_ge(weights, block_weights)

            def store_parts(i):
                for n in range(NQ // 2):
                    sp.wait_ge(*turn(stacked[n], i, 0))
                    sp.sem_inc(sem(passed), 1)
                for z, stored in enumerate((q_stored, k_stored)):
                    sp.wait_ge(*turn(rest, i, 2 * z + 2))
                    sp.dma_start(parts_d[z].rearrange("a p s -> p a s"), part[:, z, :, :]).then_inc(sem(stored), 16)
                for stored in (q_stored, k_stored):
                    sp.wait_ge(*turn(stored, i, 16))
                    sp.sem_inc(sem(passed), 1)

            def stack(i, n):
                first = 2 * QUAD * n
                hs, s = slice(first, first + 2 * QUAD), sem(stacked[n])
                sp.wait_ge(*turn(scored, i - 1, 2 * UQ * (n + 1)) if not isinstance(i, int) or i > 0 else (const, 4))
                sp.dma_start(QS[STACK:STACK + 2, hs, :], zero[:, :].unsqueeze(1).to_broadcast([2, 2 * QUAD, S])
                             ).then_inc(s, 16)
                stack_left(sp, QS[:, hs, :], 0, HD, parts_d[0], s, first)
                stack_right(sp, KS[:, hs, :], 0, HD, parts_d[1], s, first)

            def stack_max(i, g):
                for n, (m, part_made) in enumerate(((mh, mhigh), (ml, mlow))):
                    sp.wait_ge(*turn(part_made, i, g + 1))
                    sp.dma_start(QS[STACK + n:STACK + n + 1, QUAD * g:QUAD * g + QUAD, :], m[:, g % 2, :]
                                 ).then_inc(sem(mstacked), 16)

            store_parts(0)
            for n in range(NQ // 2):
                stack(0, n)
            stack_max(0, 0)

            def run(i, tail, prep, tab):
                stack_max(i, 1)
                if prep:
                    store_parts(i + 1)
                stack_max(i, 2)
                if prep:
                    stack(i + 1, 0)
                stack_max(i, 3)
                if prep:
                    stack_max(i + 1, 0)
                    stack(i + 1, 1)

            turns(sp, run)
            sp.wait_ge(*turn(mstacked, B, 0 - 32))

        @block.gpsimd
        def _(pool):
            prime(pool, signals)
            pool.memset(zero[:, :], 0.0).then_inc(const, 1)
            pool.memset(one[:, :], 1.0).then_inc(const, 1)
            pool.wait_ge(weights, block_weights)

            def split(i):
                for z in range(2):
                    pool.wait_ge(*turn(roped, i, 2 * z + 2))
                    pool.tensor_tensor(rot[:, z, 0, :], rot[:, z, 0, :], rot[:, z, 1, :], ALU.add
                                       ).then_inc(sem(summed), 1)
                    pool.wait_ge(*turn(cast, i, 2 * z + 1))
                    pool.tensor_tensor(rot[:, z, 1, :], rot[:, z, 0, :], part[:, z, 0, :], ALU.subtract
                                       ).then_inc(sem(rest), 1)
                    pool.wait_ge(*turn(cast, i, 2 * z + 2))
                    pool.tensor_tensor(part[:, z, 2, :], rot[:, z, 1, :], part[:, z, 1, :], ALU.subtract
                                       ).then_inc(sem(rest), 1)

            def bias_tokens(i):
                norm_wait(pool, norm, i, 0)
                pool.wait_ge(*turn(resid, i, 0))
                pool.tensor_tensor(XB[:, :, :], XN[:, :, :], bo[:, :, :], ALU.add).then_inc(sem(biased), 1)

            def bias_more(i):
                pool.wait_ge(*turn(resid, i, 1))
                pool.wait_ge(*turn(summed_up, i, 0))
                pool.tensor_tensor(XC[:, :, :], XA[:, :, :], b2[:, :, :], ALU.add).then_inc(sem(biased2), 1)

            norm_root(pool, c, norm, 0, 0)
            norm_root(pool, c, norm, 0, 1)
            split(0)

            def run(i, tail, prep, tab):
                if prep:
                    norm_root(pool, c, norm, i + 1, 0)
                bias_tokens(i)
                if tail:
                    norm_root(pool, tail_c, tail_norm, i - 1, 0)
                if prep:
                    norm_root(pool, c, norm, i + 1, 1)
                if tail:
                    bias_more(i - 1)
                if prep:
                    split(i + 1)

            turns(pool, run)
            norm_root(pool, tail_c, tail_norm, B - 1, 0)
            bias_more(B - 1)

        @block.scalar
        def _(act):
            act.wait_ge(weights, block_weights)

            def features(i, tab):
                act.wait_ge(*turn(turned, i, 1))
                act.wait_ge(*turn(vdone, i, 0))
                act.activation(YT[:, :], bank(tab, ("turned", 1, 0))[:, :], ACT.Identity, scale=cols[:, 4:5],
                               bias=cols[:, 5:6]).then_inc(sem(yT), 1)

            def split(i, z, n):
                if n == 0:
                    act.wait_ge(*turn(summed, i, z + 1))
                    act.wait_ge(*turn((q_stored, k_stored)[z], i, 0))
                    act.activation(part[:, z, 0, :], rot[:, z, 0, :], ACT.Copy).then_inc(sem(cast), 1)
                else:
                    act.wait_ge(*turn(rest, i, 2 * z + 1))
                    act.activation(part[:, z, 1, :], rot[:, z, 1, :], ACT.Copy).then_inc(sem(cast), 1)

            def minus_max(i, g):
                act.wait_ge(*turn(mturned, i, g + 1))
                act.wait_ge(*turn(mstacked, i, 32 * (g - 1)))
                act.activation(mh[:, g % 2, :], TB[0:QUAD, :], ACT.Copy, scale=-1.0).then_inc(sem(mhigh), 1)

            def tail_at(i, tab):
                act.wait_ge(*turn(at_turned, i, 1))
                act.activation(ATT[:, :], bank(tab, ("at", -1, 0))[:, :], ACT.Copy).then_inc(sem(attT), 1)

            def tail_z(i, tab):
                act.wait_ge(*turn(z_turned, i, 1))
                act.activation(ZT[:, :], bank(tab, ("z", -1, 0))[:, :], ACT.Identity, scale=cols[:, 6:7],
                               bias=cols[:, 7:8]).then_inc(sem(zT), 1)

            def tail_relu(i, tab, f):
                act.wait_ge(*turn(hidden, i, f + 1))
                act.wait_ge(*turn(ffn, i, 0))
                act.activation(hT[:, f, :], bank(tab, ("hidden", -1, f))[:, :], ACT.Relu, bias=b1c[:, f:f + 1]
                               ).then_inc(sem(relu_a), 1)

            def tail_step(u, i, tab):
                if u == 0:
                    tail_at(i, tab)
                if u == Z_AT:
                    tail_z(i, tab)
                for f in range(0, FC, 2):
                    if u == HIDDEN_AT[f]:
                        tail_relu(i, tab, f)

            def prep_step(u, i, tab):
                if u == TURNED_AT:
                    features(i, tab)
                for n in range(4):
                    if u == SPLIT_AT[n]:
                        split(i, n // 2, n % 2)

            for u in range(UNITS):
                prep_step(u, 0, opening)
            minus_max(0, 0)

            def run(i, tail, prep, tab):
                for u in range(UNITS):
                    act.wait_ge(*turn(scored, i, u + 1))
                    act.wait_ge(*turn(pv, i, u // QUAD - 1))
                    act.activation(PT[:, u % 8, :, :], ST[u % 2][:, :, :], ACT.Exp).then_inc(sem(exped), 1)
                    if tail:
                        tail_step(u, i - 1, tab)
                    if prep:
                        prep_step(u, i + 1, tab)
                    if u % UQ == UQ - 1 and (prep or u < UNITS - UQ):
                        minus_max(i + (u + 1) // UNITS, (u // UQ + 1) % NQ)

            turns(act, run)
            for u in range(UNITS):
                tail_step(u, B - 1, closing)

        @block.vector
        def _(dve):
            dve.memset(QS[64:96, :, :], 0.0).then_inc(const, 1)
            dve.memset(KS[64:96, :, :], 0.0).then_inc(const, 1)
            dve.memset(V[:, :, :, :], 0.0).then_inc(vmade, 1)
            dve.wait_ge(vmade, 1)
            dve.memset(V[:, :, :, HD:HD + 1], 1.0).then_inc(vmade, 1)
            dve.wait_ge(weights, block_weights)
            dve.wait_ge(vmade, 2)

            def x_tile(i, t):
                return X[:, bass.ds(i * T + t, 1), :].rearrange("p a d -> p (a d)")

            def rotate(i, n, tab):
                dve.wait_ge(*turn(projected, i, n + 1))
                dve.wait_ge(*turn(rest, i, 0))
                dve.scalar_tensor_tensor(rot[:, n // 2, n % 2, :], bank(tab, ("projected", 1, n))[:, :], cols[:, n:n + 1],
                                         rope[:, n, :], ALU.add, ALU.mult).then_inc(sem(roped), 1)

            def prep_step(u, i, tab):
                if u == 0:
                    norm_measure(dve, c, norm, i, 0, lambda t: x_tile(i, t))
                if u == 3:
                    dve.wait_ge(*turn(biased, i, 0))
                    norm_scale(dve, c, norm, i, 0, lambda t: XN[:, t, :], lambda t: x_tile(i, t))
                    norm_wait(dve, norm, i, 0)
                    norm_measure(dve, c, norm, i, 1, lambda t: XN[:, t, :])
                if u == 4:
                    norm_scale(dve, c, norm, i, 1, lambda t: YN[:, t, :], lambda t: XN[:, t, :])
                for n in range(4):
                    if u == ROTATED_AT[n]:
                        rotate(i, n, tab)

            def values(i, tab):
                for n, (t, count) in enumerate(V_FILLS):
                    dve.wait_ge(*turn(valued, i, n + 1))
                    dve.wait_ge(*turn(pv, i, 0))
                    dve.tensor_tensor(V[:, t:t + count, :, 0:HD],
                                      bank(tab, ("valued", 1, n))[:, 0:count * D].rearrange("p (t h d) -> p t h d",
                                                                                            t=count, d=HD),
                                      bv[:, 0:count, :].rearrange("p t (h d) -> p t h d", d=HD), ALU.add
                                      ).then_inc(sem(vdone), 1)

            def tail_step(u, i, tab):
                if u == 2:
                    dve.wait_ge(*turn(wo, i, 1))
                    dve.wait_ge(*turn(biased, i, 1))
                    dve.wait_ge(*turn(biased2, i, 0))
                    dve.tensor_tensor(XA[:, :, :], bank(tab, ("wo", -1, 0))[:, :].rearrange("p (t d) -> p t d", d=D),
                                      XB[:, :, :], ALU.add).then_inc(sem(resid), 1)
                    dve.wait_ge(*turn(resid, i, 1))
                    norm_measure(dve, tail_c, tail_norm, i, 0, lambda t: XA[:, t, :])
                if u == Z_AT - 1:
                    norm_scale(dve, tail_c, tail_norm, i, 0, lambda t: ZN[:, t, :], lambda t: XA[:, t, :])
                for f in range(1, FC, 2):
                    if u != HIDDEN_AT[f]:
                        continue
                    dve.wait_ge(*turn(hidden, i, f + 1))
                    dve.wait_ge(*turn(ffn, i, 0))
                    dve.tensor_scalar(hT[:, f, :], bank(tab, ("hidden", -1, f))[:, :], b1c[:, f:f + 1], 0.0,
                                      ALU.add, ALU.max).then_inc(sem(relu_v), 1)
                if u == FFN_AT:
                    dve.wait_ge(*turn(ffn, i, 1))
                    dve.wait_ge(*turn(biased2, i, 1))
                    dve.tensor_tensor(XC[:, :, :], bank(tab, ("ffn", -1, 0))[:, :].rearrange("p (t d) -> p t d", d=D),
                                      XC[:, :, :], ALU.add).then_inc(sem(summed_up), 1)
                    dve.wait_ge(*turn(summed_up, i, 1))
                    xb = X[:, bass.ds(i * T, T), :]
                    dve.tensor_tensor(xb, xb, XC[:, :, :], ALU.add).then_inc(sem(added), 1)

            def maximum(i, n, tab, batch):
                h, t = n // T, n % T
                dve.wait_ge(*turn(filled, i, n + 1))
                dve.tensor_reduce(M[:, t, h:h + 1], bank(tab, ("logits", batch, n))[:, :], AX_X, ALU.max
                                  ).then_inc(sem(maxed), 1)

            def minus_max(i, g):
                dve.wait_ge(*turn(mhigh, i, g + 1))
                dve.scalar_tensor_tensor(ml[:, g % 2, :], TB[0:QUAD, :], -1.0, mh[:, g % 2, :], ALU.mult,
                                         ALU.subtract).then_inc(sem(mlow), 1)

            for u in range(UNITS):
                prep_step(u, 0, opening)
            for n in range(QUAD * T):
                maximum(0, n, opening, 1)
            values(0, opening)
            minus_max(0, 0)

            def run(i, tail, prep, tab):
                for u in range(UNITS):
                    g = u // UQ
                    for batch, n in beside(u, prep):
                        maximum(i + batch, n, tab, batch)
                    if tail:
                        tail_step(u, i - 1, tab)
                    if prep:
                        prep_step(u, i + 1, tab)
                    if u % UQ < UQ - 1:
                        continue
                    for batch, n in early(u, prep)[0:1]:
                        maximum(i + batch, n, tab, batch)
                    if g < NQ - 1 or prep:
                        minus_max(i + (g + 1) // NQ, (g + 1) % NQ)
                    for batch, n in early(u, prep)[1:2]:
                        maximum(i + batch, n, tab, batch)
                    dve.wait_ge(*turn(pv, i, 2 * g + 2))
                    dve.wait_ge(*turn(pvturned, i, g))
                    dve.tensor_copy(pvs[:, :], PV[:, :]).then_inc(sem(pvcopied), 1)
                    dve.wait_ge(*turn(pvturned, i, g + 1))
                    heads = TB[:, :].rearrange("p (t j e) -> p t j e", t=T, e=32)
                    dve.wait_ge(*turn(attn, i, g))
                    dve.reciprocal(rec[:, :, :], heads[:, :, :, HD]).then_inc(sem(inv), 1)
                    dve.wait_ge(*turn(inv, i, g + 1))
                    dve.wait_ge(*turn(at_turned, i, 0))
                    dve.tensor_tensor(AT[:, :, 32 * g:32 * g + 32].rearrange("p t (j e) -> p t j e", e=HD),
                                      heads[:, :, :, 0:HD], widen(rec[:, :, :], HD), ALU.mult).then_inc(sem(attn), 1)
                if prep:
                    values(i + 1, tab)

            turns(dve, run)
            for u in range(UNITS):
                tail_step(u, B - 1, closing)
            dve.wait_ge(*turn(added, B, 0))

        @block.tensor
        def _(pe):
            pe.wait_ge(weights, block_weights)
            pe.wait_ge(vmade, 2)

            def front(tab, use, i):
                kind, batch, n = tab[use][1]
                if kind == "hidden":
                    done = turn(relu_v if n % 2 else relu_a, i + batch, n // 2 + 1)
                else:
                    done = turn(readers[kind][0], i + batch, readers[kind][1](n))
                if tab is not opening or list(tab).index(use) >= 2:
                    pe.wait_ge(*done)
                return bank(tab, use)

            def prep_step(use, i, tab):
                kind, _, n = use
                if kind == "turned":
                    norm_wait(pe, norm, i + 1, 1)
                    f = front(tab, use, i)
                    for t in range(T):
                        last = pe.transpose(f[:, t * P:(t + 1) * P], YN[:, t, :], ident[:, :])
                    last.then_inc(sem(turned), 1)
                elif kind == "projected":
                    if n == 0:
                        pe.wait_ge(*turn(yT, i + 1, 1))
                    f = front(tab, use, i)
                    pe.matmul(f[:, :], W[:, n, :], YT[:, :], start=True, stop=True).then_inc(sem(projected), 1)

            def prep_values(i, tab):
                for n, (t0, count) in enumerate(V_FILLS):
                    f = front(tab, ("valued", 1, n), i)
                    for t in range(t0, t0 + count):
                        last = pe.matmul(f[:, (t - t0) * D:(t - t0 + 1) * D], YT[:, t * P:(t + 1) * P], W[:, 4, :],
                                         start=True, stop=True)
                    last.then_inc(sem(valued), 1)

            def tail_step(use, i, tab):
                kind, _, n = use
                b = i - 1
                if kind == "at":
                    pe.wait_ge(*turn(attn, b, NQ))
                    f = front(tab, use, i)
                    for t in range(T):
                        last = pe.transpose(f[:, t * P:(t + 1) * P], AT[:, t, :], ident[:, :])
                    last.then_inc(sem(at_turned), 1)
                elif kind == "wo":
                    pe.wait_ge(*turn(attT, b, 1))
                    f = front(tab, use, i)
                    for t in range(T):
                        last = pe.matmul(f[:, t * D:(t + 1) * D], ATT[:, t * P:(t + 1) * P], W[:, 5, :],
                                         start=True, stop=True)
                    last.then_inc(sem(wo), 1)
                elif kind == "z":
                    norm_wait(pe, tail_norm, b, 0)
                    f = front(tab, use, i)
                    for t in range(T):
                        last = pe.transpose(f[:, t * P:(t + 1) * P], ZN[:, t, :], ident[:, :])
                    last.then_inc(sem(z_turned), 1)
                elif kind == "hidden":
                    pe.wait_ge(*turn(zT, b, 1))
                    f = front(tab, use, i)
                    pe.matmul(f[:, :], W1[:, n * P:(n + 1) * P], ZT[:, :], start=True, stop=True).then_inc(sem(hidden), 1)
                else:
                    pe.wait_ge(*turn(relu_a, b, FC // 2))
                    pe.wait_ge(*turn(relu_v, b, FC // 2))
                    f = front(tab, use, i)
                    for t in range(T):
                        for k in range(FC):
                            last = pe.matmul(f[:, t * D:(t + 1) * D], hT[:, k, t * P:(t + 1) * P], W2[:, k, :],
                                             start=(k == 0), stop=(k == FC - 1))
                    last.then_inc(sem(ffn), 1)

            def logits(i, tab, batch, n):
                h, t = n // T, n % T
                if n % (2 * QUAD * T) == 0:
                    pe.wait_ge(*turn(stacked[h // QUAD // 2], i + batch, 16 * (PARTS + 2)))
                f = front(tab, ("logits", batch, n), i)
                pe.matmul(f[:, :], QS[0:KR0, h, t * P:(t + 1) * P], KS[0:KR0, h, :],
                          start=True, stop=True).then_inc(sem(filled), 1)

            def turn_max(i, g):
                pe.wait_ge(*turn(maxed, i, QUAD * T * (g + 1)))
                pe.wait_ge(*turn(attn, i, g - 1))
                for t in range(T):
                    last = pe.transpose(TB[0:QUAD, t * P:(t + 1) * P], M[:, t, QUAD * g:QUAD * g + QUAD], ident[:, :])
                last.then_inc(sem(mturned), 1)

            def values(i, w, tiles=(0, 1)):
                pe.wait_ge(*turn(exped, i, QUAD * w + QUAD))
                if w == 0:
                    pe.wait_ge(*turn(vdone, i, 3))
                if w % 2 == 0:
                    pe.wait_ge(*turn(pvcopied, i, w // 2))
                for kk in tiles:
                    for j in range(QUAD):
                        kt = 2 * (w % 2) + kk
                        last = pe.matmul(PV[32 * j:32 * j + 32, :], V[:, kt, QUAD * (w // 2) + j, :],
                                         PT[:, (QUAD * w + j) % 8, kk, :], start=(kt == 0), stop=(kt == T - 1))
                if 1 in tiles:
                    last.then_inc(sem(pv), 1)

            def turn_values(i, g, more):
                pe.wait_ge(*turn(pvcopied, i, g + 1))
                pe.wait_ge(*turn(attn, i, g))
                pe.wait_ge(*turn(mlow, i, g + 2 if more else NQ))
                for t in range(T):
                    last = pe.transpose(TB[:, t * P:(t + 1) * P], pvs[:, t * P:(t + 1) * P], ident[:, :])
                last.then_inc(sem(pvturned), 1)

            def scores(i, u):
                w, j = u // QUAD, u % QUAD
                h = QUAD * (w // 2) + j
                if u % UQ == 0:
                    pe.wait_ge(*turn(mstacked, i, 32 * (w // 2 + 1)))
                pe.wait_ge(*turn(exped, i, u - 1))
                for kk in range(2):
                    kt = 2 * (w % 2) + kk
                    last = pe.matmul(ST[u % 2][:, kk, :], KS[0:KR0, h, kt * P:(kt + 1) * P], QS[0:KR0, h, :],
                                     start=True, stop=True)
                last.then_inc(sem(scored), 1)

            for use in OPENING[0:5]:
                prep_step(use, -1, opening)
            for n in range(QUAD * T):
                logits(-1, opening, 1, n)
            turn_max(0, 0)
            prep_values(-1, opening)

            def run(i, tail, prep, tab):
                for u in range(UNITS):
                    g = u // UQ
                    if u % UQ:
                        scores(i, u)
                    for batch, n in beside(u, prep):
                        logits(i, tab, batch, n)
                    if u % UQ == 0:
                        scores(i, u)
                    for use in extras(u, tail, prep):
                        (tail_step if use[1] < 0 else prep_step)(use, i, tab)
                    if u % UQ in (QUAD, QUAD + 1):
                        values(i, 2 * g, (u % UQ - QUAD,))
                    if u % UQ == UQ - 1:
                        more = prep or g < NQ - 1
                        if more:
                            turn_max(i + (g + 1) // NQ, (g + 1) % NQ)
                        for batch, n in early(u, prep):
                            logits(i, tab, batch, n)
                        values(i, 2 * g + 1)
                        turn_values(i, g, more)
                if prep:
                    prep_values(i, tab)

            turns(pe, run)
            for use in CLOSING:
                tail_step(use, B, closing)


PAST = 6
LINES = H * PAST
QC = S + S // 2 + P
IR = STACK
KR1 = 128
MR = KR1 - 2
NEG = -1.0e30


def layer1_attention(nc, ins, c):
    with ExitStack() as ctx:
        def sb(name, shape, dt=F32):
            return ctx.enter_context(nc.sbuf_tensor(f"c_{name}", shape, dt))

        signals, flags = [], []

        def sig(name, per=1, start=1):
            signals.append((ctx.enter_context(nc.semaphore(f"c_{name}")), per, start))
            return signals[-1]

        def flag(name):
            flags.append(ctx.enter_context(nc.semaphore(f"c_{name}")))
            return flags[-1]

        X, XN, ident = c["X"], c["XN"], c["ident"]
        WQ = sb("WQ", [P, 3 * D])
        WO = sb("WO", [P, D])
        WR = sb("WR", [P, 4 * LINES])
        WW = sb("WW", [P, 2, 2 * LINES])
        cols = sb("cols", [P, 2])
        bv = sb("bv", [P, D])
        bo = sb("bo", [P, D])
        XT = sb("XT", [P, S + 1])
        dec = sb("dec", [P, 4, H])
        bias = sb("bias", [P, H])
        ramp = sb("ramp", [P, P + 4])
        table_of_decays = sb("table", [P, H, P])
        expo = sb("expo", [P, 4, H])
        DQ = sb("DQ", [P, 4, H])
        mask = sb("mask", [P, P], BF16)
        identb = sb("identb", [P, P], BF16)
        only = sb("only", [P, P], BF16)
        zero = sb("zero", [2, QC], BF16)
        one = sb("one", [2, S], BF16)
        part = sb("part", [P, 2, PARTS, S], BF16)
        length = sb("length", [P, 2, T * H])
        guess = sb("guess", [P, 2, T * H])
        power = sb("power", [P, 2, T * H])
        three_halves = sb("three_halves", [P, 2, T * H])
        halved = sb("halved", [P, 2, T * H], I32)
        qk = sb("qk", [P, 2, S])
        rem = sb("rem", [P, 2, S])
        QS = sb("QS", [P, H, QC], BF16)
        KS = sb("KS", [P, H, S], BF16)
        QI = sb("QI", [PAIRS * PAST, H, S], BF16)
        KI = sb("KI", [PAIRS * PAST, H, S], BF16)
        V = sb("V", [P, T, H, 32])
        inc = sb("inc", [P, S])
        SD = sb("SD", [P, 2, QUAD, T, P])
        MD = sb("MD", [P, T, H])
        M = sb("M", [P, T, H])
        mh = sb("mh", [QUAD, 2, QC], BF16)
        ml = sb("ml", [QUAD, 2, QC], BF16)
        PT = sb("PT", [P, QUAD + 1, 2, S])
        LP = sb("LP", [P, T, 4 * LINES])
        prod = sb("prod", [P, 2, T, LINES])
        line = sb("line", [P, 2, T, LINES])
        flat = LP[:, :, :].rearrange("p t n -> p (t n)")
        LQ = flat[:, 0:6 * LINES].rearrange("p (t n) -> p t n", n=LINES)
        LK = flat[:, 6 * LINES:(6 + T) * LINES].rearrange("p (t n) -> p t n", n=LINES)
        pvs = sb("pvs", [P, S])
        rec = sb("rec", [P, T, QUAD])
        AT = sb("AT", [P, T, D])
        ATT, XB = c["YT"], c["YN"]
        q_d = nc.dram_tensor("c_q", [PARTS, P, QC], BF16).ap()
        k_d = nc.dram_tensor("c_k", [PARTS, P, S], BF16).ap()
        r_d = nc.dram_tensor("c_r", [PARTS, LINES, S], BF16).ap()
        w_d = nc.dram_tensor("c_w", [PARTS, LINES, S], BF16).ap()
        rd_d = nc.dram_tensor("c_rd", [PARTS, LINES, QC], BF16).ap()
        wd_d = nc.dram_tensor("c_wd", [PARTS, LINES, S], BF16).ap()
        FB = [ctx.enter_context(nc.psum_tensor(f"c_F{n}", [P, S], F32)) for n in range(4)]
        ST = ctx.enter_context(nc.psum_tensor("c_ST", [P, 2, S], F32))
        PV = ctx.enter_context(nc.psum_tensor("c_PV", [P, S], F32))
        TB = ctx.enter_context(nc.psum_tensor("c_TB", [P, S], F32))

        NQ = H // QUAD
        NEWTON = 3
        UQ = QUAD + 1
        UNITS = UQ * NQ
        STACKS = 1 + 3 * PARTS + 3
        SPANS = [(0, 0, S), (S, 2 * P, S), (S + 2 * P, 3 * P, S)]

        weights, made, table_made = flag("weights"), flag("made"), flag("table_made")
        made2 = flag("made2")
        norm = norm_signals(sig, 1)
        turned, xT = sig("turned"), sig("xT")
        made_qk, projected = sig("made_qk", 2), sig("projected", 2)
        cast, rest = sig("cast", 4), sig("rest", 4)
        valued, vdone = sig("valued", 2), sig("vdone", 2)
        pointed, points = sig("pointed", 8), sig("points", 8)
        product, crossed, squared = sig("product", 4), sig("crossed", 2), sig("squared", 2)
        summed, root, unit = sig("summed", 4), sig("root", 4), sig("unit", 2)
        newton = sig("newton", 4 * NEWTON)
        decayed = sig("decayed", 4)
        lined = sig("lined", 5)
        lcast, lrest, lthird = sig("lcast", 10), sig("lrest", 5), sig("lthird", 5)
        stored = [sig("stored0", 16 * 6), sig("stored1", 16 * 3)]
        stacked = [sig(f"stacked{n}", 16 * STACKS) for n in range(NQ // 2)]
        passed = sig("passed", NQ // 2 + 4)
        logit, maxed = sig("logit", 4 * H), sig("maxed", 4 * H)
        inc_decayed, diag = sig("inc_decayed", H), sig("diag", H)
        mjoined, mturned = sig("mjoined", NQ), sig("mturned", NQ)
        mhigh, mlow = sig("mhigh", 3 * NQ), sig("mlow", 3 * NQ)
        mstacked = sig("mstacked", 16 * 2 * NQ, 16 * 2 + 1)
        scored, exped = sig("scored", UQ * NQ, UQ + 1), sig("exped", UQ * NQ)
        pv, pvcopied, pvturned, inv = sig("pv", NQ), sig("pvcopied", NQ), sig("pvturned", NQ), sig("inv", NQ)
        attn = sig("attn", NQ, 2)
        at_turned, attT, wo, biased, added = sig("at_turned"), sig("attT"), sig("wo"), sig("biased"), sig("added")
        NW = 10 + 1 + 1 + 1

        readers = {"turned": (xT, lambda n: 1), "qk": (projected, lambda n: n + 1), "v": (vdone, lambda n: n + 1),
                   "points": (points, lambda n: n + 1), "line": (lrest, lambda n: n + 1),
                   "inc": (inc_decayed, lambda n: n + 1), "diag": (diag, lambda n: n + 1),
                   "past31": (maxed, lambda n: 4 * n + 2), "past2": (maxed, lambda n: 4 * n + 3),
                   "at": (attT, lambda n: 1), "wo": (added, lambda n: 1)}
        banks = {"turned": 0, "qk": 1, "v": 2, "points": 0, "line": 1, "inc": 0, "diag": 1, "past31": 2, "past2": 3,
                 "at": 2, "wo": 3}
        TAIL_AT, WO_AT, TURNED_AT, QK_AT, POINTS_AT = 1, 2, 1, (2, 2), (3, 3, 3, 3, 4, 4, 5, 5)
        CASTS = (2, 3)
        SUMS = (5, 6)
        DECAY_AT = 8
        LINE_AT = (9, 10, 10, 11, 11)
        PLAN = ([(TAIL_AT, ("at", -1, 0)), (WO_AT, ("wo", -1, 0)), (TURNED_AT, ("turned", 1, 0))]
                + [(u, ("qk", 1, n)) for n, u in enumerate(QK_AT)] + [(u, ("points", 1, n)) for n, u in enumerate(POINTS_AT)]
                + [(u, ("line", 1, n)) for n, u in enumerate(LINE_AT)])
        EXTRA = {u: [use for at, use in PLAN if at == u] for u in range(UNITS)}
        HEAD = ("inc", "diag", "past31", "past2")

        def extras(u, tail, prep):
            return [use for use in EXTRA.get(u, []) if (tail if use[1] < 0 else prep)]

        def next_head(u, prep):
            g, j = u // UQ, u % UQ
            if j == QUAD or (g == NQ - 1 and not prep):
                return None
            return (1 if g == NQ - 1 else 0), ((g + 1) % NQ) * QUAD + j

        def table(uses, before):
            last, tab = {}, {}
            for kind, batch, n in before:
                last[banks_of(kind, n)] = (kind, batch - 1, n)
            for use in uses:
                b = banks_of(use[0], use[2])
                tab[use] = (b, last.get(b))
                last[b] = use
            return tab

        def banks_of(kind, n):
            return banks[kind] if kind in HEAD else (banks[kind] + n) % 4

        def uses_of(tail, prep):
            uses = []
            for u in range(UNITS):
                if next_head(u, prep):
                    batch, h = next_head(u, prep)
                    uses += [(kind, batch, h) for kind in HEAD]
                uses += extras(u, tail, prep)
            return uses + ([("v", 1, n) for n in range(2)] if prep else [])

        OPENING = ([use for u in range(UNITS) for use in extras(u, False, True)]
                   + [(kind, 1, h) for h in range(QUAD) for kind in HEAD] + [("v", 1, n) for n in range(2)])
        CLOSING = [use for u in range(UNITS) for use in extras(u, True, False)]
        opening = table(OPENING, [])
        first_turn = table(uses_of(False, True), OPENING)
        middle = table(uses_of(True, True), uses_of(False, True))
        last_turn = table(uses_of(True, False), uses_of(True, True))
        closing = table(CLOSING, uses_of(True, False))

        def turns(eng, run):
            run(0, False, True, first_turn)
            with eng.Fori(1, B - 1) as i:
                run(i, True, True, middle)
            run(B - 1, True, False, last_turn)

        def bank(tab, use):
            return FB[tab[use][0]]

        PIECES = [(r_d, 0, S), (w_d, 0, S), (wd_d, 0, S), (rd_d, P, S), (rd_d, P + S, 2 * P)]
        ctx.callback(clear, nc, [sem(s) for s in signals] + flags)
        block = ctx.enter_context(nc.Block())

        @block.sync
        def _(sp):
            sp.dma_start(WQ[:, :], ins["c_qkv"]).then_inc(weights, 16)
            sp.dma_start(WO[:, :], ins["c_wo"]).then_inc(weights, 16)
            sp.dma_start(WR[:, :], ins["c_read"]).then_inc(weights, 16)
            sp.dma_start(WW[:, 0, :], ins["c_write1"]).then_inc(weights, 16)
            sp.dma_start(WW[:, 1, :], ins["c_write2"]).then_inc(weights, 16)
            sp.dma_start(cols[:, :], ins["c_cols"]).then_inc(weights, 16)
            sp.dma_start(dec[:, 0, :], ins["c_decay"].partition_broadcast(P)).then_inc(weights, 16)
            sp.dma_start(bias[:, :], ins["c_bias"].partition_broadcast(P)).then_inc(weights, 16)
            sp.dma_start(bv[:, :], ins["c_bv"].partition_broadcast(P)).then_inc(weights, 16)
            sp.dma_start(bo[:, :], ins["c_bo"].partition_broadcast(P)).then_inc(weights, 16)
            sp.wait_ge(made, 7)
            sp.dma_start(KS[MR:KR1, :, :], spread(one)).then_inc(weights, 16)
            sp.wait_ge(made2, 6)
            sp.dma_start(only[MR:KR1, :], one[:, 0:P]).then_inc(weights, 16)
            sp.dma_start(rd_d[:, :, 0:P].rearrange("a p s -> p a s"), QS[0:LINES, 0:PARTS, 0:P]).then_inc(weights, 16)
            sp.wait_ge(weights, 16 * NW)

            def hold():
                sp.sem_inc(sem(passed), 1)

            def store_qk(i):
                for n in range(NQ // 2):
                    sp.wait_ge(*turn(stacked[n], i, 0))
                    hold()
                for z, parts_d in enumerate((q_d, k_d)):
                    sp.wait_ge(*turn(rest, i, 2 * z + 2))
                    for at, q0, q1 in SPANS[0:1 if z else 3]:
                        sp.dma_start(parts_d[:, :, at:at + q1 - q0].rearrange("a p s -> p a s"), part[:, z, :, q0:q1]
                                     ).then_inc(sem(stored[z]), 16)

            def stored_wait(i, z):
                sp.wait_ge(*turn(stored[z], i, 16 * (1 if z else 3)))
                hold()

            def store_lines(i):
                for n, (dst, at, width) in enumerate(PIECES):
                    sp.wait_ge(*turn(lthird, i, n + 1))
                    sp.dma_start(dst[:, :, at:at + width].rearrange("a p s -> p a s"),
                                 part[0:LINES, n % 2, :, 0:width]).then_inc(sem(stored[n % 2]), 16)
                for z in range(2):
                    sp.wait_ge(*turn(stored[z], i, per_turn(stored[z])))
                    hold()

            def stack_qk(i, n):
                at, s = 2 * QUAD * n, sem(stacked[n])
                hs = slice(at, at + 2 * QUAD)
                sp.wait_ge(*turn(scored, i - 1, 2 * UQ * (n + 1)) if not isinstance(i, int) or i > 0 else (made, 7))
                sp.dma_start(QS[MR:KR1, hs, :], zero[:, :].unsqueeze(1).to_broadcast([2, 2 * QUAD, QC])).then_inc(s, 16)
                stack_left(sp, QS[:, hs, :], 0, HD, q_d, s, at)
                stack_right(sp, KS[:, hs, :], 0, HD, k_d, s, at)

            def stack_lines(n):
                at, s = 2 * QUAD * n, sem(stacked[n])
                hs = slice(at, at + 2 * QUAD)
                stack_left(sp, QI[:, hs, :], 0, PAST, r_d, s, at)
                stack_right(sp, KI[:, hs, :], 0, PAST, w_d, s, at)
                stack_right(sp, KS[:, hs, :], IR, PAST, wd_d, s, at)
                stack_left(sp, QS[:, hs, :], IR, PAST, rd_d, s, at)

            def stack_max(i, g):
                for n, (m, part_made) in enumerate(((mh, mhigh), (ml, mlow))):
                    sp.wait_ge(*turn(part_made, i, 3 * g + 3))
                    sp.dma_start(QS[MR + n:MR + n + 1, QUAD * g:QUAD * g + QUAD, :], m[:, g % 2, :]
                                 ).then_inc(sem(mstacked), 16)

            store_qk(0)
            stored_wait(0, 0)
            stored_wait(0, 1)
            for n in range(NQ // 2):
                stack_qk(0, n)
            store_lines(0)
            for n in range(NQ // 2):
                stack_lines(n)
            stack_max(0, 0)

            def run(i, tail, prep, tab):
                stack_max(i, 1)
                if prep:
                    store_qk(i + 1)
                stack_max(i, 2)
                if prep:
                    stored_wait(i + 1, 0)
                    stored_wait(i + 1, 1)
                    stack_qk(i + 1, 0)
                    store_lines(i + 1)
                    stack_lines(0)
                stack_max(i, 3)
                if prep:
                    stack_max(i + 1, 0)
                    stack_qk(i + 1, 1)
                    stack_lines(1)

            turns(sp, run)
            sp.wait_ge(*turn(mstacked, B, -16 * 2))

        @block.gpsimd
        def _(pool):
            prime(pool, signals)
            pool.memset(identb[:, :], 0.0).then_inc(made, 1)
            pool.memset(mask[:, :], 0.0).then_inc(made, 1)
            pool.iota(ramp[:, 0:P], pattern=[[-1, P]], base=0, channel_multiplier=1,
                      allow_small_or_imprecise_dtypes=True).then_inc(made, 1)
            pool.iota(ramp[:, P:P + 3], pattern=[[P, 3]], base=0, channel_multiplier=1,
                      allow_small_or_imprecise_dtypes=True).then_inc(made, 1)
            pool.iota(ramp[:, P + 3:P + 4], pattern=[[1, 1]], base=P, channel_multiplier=-1,
                      allow_small_or_imprecise_dtypes=True).then_inc(made, 1)
            pool.memset(zero[:, :], 0.0).then_inc(made, 1)
            pool.memset(one[:, :], 1.0).then_inc(made, 1)
            pool.wait_ge(made, 7)
            pool.affine_select(out=identb[:, :], in_=identb[:, :], compare_op=ALU.not_equal, fill=1.0,
                               base=0, pattern=[[-1, P]], channel_multiplier=1).then_inc(made, 1)
            pool.affine_select(out=mask[:, :], in_=mask[:, :], compare_op=ALU.is_ge, fill=NEG,
                               base=0, pattern=[[-1, P]], channel_multiplier=1).then_inc(made, 1)
            pool.wait_ge(table_made, 6 + H)
            pool.affine_select(out=table_of_decays[:, :, :], in_=table_of_decays[:, :, :], compare_op=ALU.is_gt, fill=0.0,
                               base=0, pattern=[[0, H], [-1, P]], channel_multiplier=1).then_inc(made, 1)
            pool.wait_ge(weights, 16 * NW)

            def prep(i):
                norm_root(pool, c, norm, i, 0)
                for z in range(2):
                    pool.wait_ge(*turn(cast, i, 2 * z + 1))
                    pool.wait_ge(*turn(lcast, i, 0))
                    pool.tensor_tensor(rem[:, z, :], qk[:, z, :], part[:, z, 0, :], ALU.subtract).then_inc(sem(rest), 1)
                    pool.wait_ge(*turn(cast, i, 2 * z + 2))
                    pool.tensor_tensor(part[:, z, 2, :], rem[:, z, :], part[:, z, 1, :], ALU.subtract
                                       ).then_inc(sem(rest), 1)
                for z in range(2):
                    pool.wait_ge(*turn(points, i, 4 * z + 4))
                    if z:
                        pool.wait_ge(*turn(summed, i, 2))
                    ab, cd = ((0, 1), (2, 3)) if z == 0 else ((0, 2), (1, 3))
                    for n, (a, b) in enumerate((ab, cd)):
                        pool.tensor_tensor(prod[:, n, :, :], LP[:, :, a * LINES:(a + 1) * LINES],
                                           LP[:, :, b * LINES:(b + 1) * LINES], ALU.mult).then_inc(sem(product), 1)
                    pool.wait_ge(*turn(product, i, 2 * z + 2))
                    pool.wait_ge(*turn(lined, i, 0))
                    pool.tensor_tensor(line[:, z, :, :], prod[:, 0, :, :], prod[:, 1, :, :], ALU.subtract
                                       ).then_inc(sem(crossed), 1)
                    pool.wait_ge(*turn(crossed, i, z + 1))
                    pool.tensor_tensor(prod[:, 0, :, :], line[:, z, :, :], line[:, z, :, :], ALU.mult
                                       ).then_inc(sem(squared), 1)
                pool.wait_ge(*turn(root, i, 3))
                y, p = guess[:, :, :], power[:, :, :]
                for n in range(NEWTON):
                    for k, (dst, a, b, op) in enumerate([(p, y, y, ALU.mult), (p, p, length[:, :, :], ALU.mult),
                                                         (p, p, three_halves[:, :, :], ALU.add), (y, y, p, ALU.mult)]):
                        pool.tensor_tensor(dst, a, b, op).then_inc(sem(newton), 1)
                        pool.wait_ge(*turn(newton, i, 4 * n + k + 1))
                for n, (_, _, width) in enumerate(PIECES):
                    pool.wait_ge(*turn(lcast, i, 2 * n + 2))
                    pool.tensor_tensor(part[0:LINES, n % 2, 2, 0:width], rem[0:LINES, n % 2, 0:width],
                                       part[0:LINES, n % 2, 1, 0:width], ALU.subtract).then_inc(sem(lthird), 1)

            with pool.Fori(0, B) as i:
                prep(i)

        @block.scalar
        def _(act):
            act.wait_ge(weights, 16 * NW)
            act.wait_ge(table_made, 1)
            act.activation(dec[:, 2, :], dec[:, 1, :], ACT.Exp, scale=-1.0).then_inc(table_made, 1)
            act.wait_ge(table_made, 2)
            act.activation(dec[:, 2, :], dec[:, 2, :], ACT.Ln, bias=1.0).then_inc(table_made, 1)
            act.wait_ge(table_made, 6)
            for h in range(H):
                act.activation(table_of_decays[:, h, :], ramp[:, 0:P], ACT.Exp, scale=dec[:, 3, h:h + 1]).then_inc(table_made, 1)
            act.activation(DQ[:, :, :], expo[:, :, :], ACT.Exp).then_inc(table_made, 1)

            def prep_step(u, i, tab):
                if u == TURNED_AT:
                    act.wait_ge(*turn(turned, i, 1))
                    act.wait_ge(*turn(valued, i, 0))
                    act.activation(XT[:, 1:S + 1], bank(tab, ("turned", 1, 0))[:, :], ACT.Copy).then_inc(sem(xT), 1)
                if u in CASTS:
                    z = CASTS.index(u)
                    act.wait_ge(*turn(projected, i, z + 1))
                    act.wait_ge(*turn(stored[z], i, 0))
                    act.activation(part[:, z, 0, :], qk[:, z, :], ACT.Copy).then_inc(sem(cast), 1)
                    act.wait_ge(*turn(rest, i, 2 * z + 1))
                    act.activation(part[:, z, 1, :], rem[:, z, :], ACT.Copy).then_inc(sem(cast), 1)
                for kind, batch, n in EXTRA.get(u, []):
                    if kind == "points":
                        act.wait_ge(*turn(pointed, i, n + 1))
                        act.wait_ge(*turn(lined, i, 0) if n < T else turn(product, i, 2))
                        act.activation(LP[:, n % T, :], bank(tab, ("points", 1, n))[:, 0:4 * LINES], ACT.Copy
                                       ).then_inc(sem(points), 1)
                for n, (_, _, width) in enumerate(PIECES):
                    if u == LINE_AT[n]:
                        act.wait_ge(*turn(lined, i, n + 1))
                        before = 16 * (3 + n // 2) if n % 2 == 0 else 16 * (1 + n // 2)
                        act.wait_ge(*turn(stored[n % 2], i, before))
                        act.activation(part[0:LINES, n % 2, 0, 0:width], bank(tab, ("line", 1, n))[0:LINES, 0:width],
                                       ACT.Copy).then_inc(sem(lcast), 1)
                        act.wait_ge(*turn(lrest, i, n + 1))
                        act.activation(part[0:LINES, n % 2, 1, 0:width], rem[0:LINES, n % 2, 0:width], ACT.Copy
                                       ).then_inc(sem(lcast), 1)

            def tail_step(u, i, tab):
                if u == TAIL_AT:
                    act.wait_ge(*turn(at_turned, i, 1))
                    act.activation(ATT[:, :], bank(tab, ("at", -1, 0))[:, :], ACT.Copy).then_inc(sem(attT), 1)

            def minus_max(i, g):
                act.wait_ge(*turn(mturned, i, g + 1))
                act.wait_ge(*turn(mstacked, i, 32 * (g - 1)))
                for at, q0, q1 in SPANS:
                    act.activation(mh[:, g % 2, at:at + q1 - q0], TB[0:QUAD, q0:q1], ACT.Copy, scale=-1.0
                                   ).then_inc(sem(mhigh), 1)

            for u in range(UNITS):
                prep_step(u, 0, opening)
            minus_max(0, 0)

            def run(i, tail, prep, tab):
                for u in range(UNITS):
                    g = u // UQ
                    act.wait_ge(*turn(scored, i, u + 1))
                    act.wait_ge(*turn(pv, i, g))
                    act.activation(PT[:, u % UQ, :, :], ST[:, :, :], ACT.Exp).then_inc(sem(exped), 1)
                    if tail:
                        tail_step(u, i - 1, tab)
                    if prep:
                        prep_step(u, i + 1, tab)
                    if u % UQ == QUAD and (prep or g < NQ - 1):
                        minus_max(i + (g + 1) // NQ, (g + 1) % NQ)

            turns(act, run)
            tail_step(TAIL_AT, B - 1, closing)

        @block.vector
        def _(dve):
            dve.memset(V[:, :, :, :], 0.0).then_inc(made2, 1)
            dve.memset(QS[:, :, 0:P], 0.0).then_inc(made2, 1)
            dve.memset(XT[:, 0:1], 0.0).then_inc(made2, 1)
            dve.memset(only[:, :], 0.0).then_inc(made2, 1)
            dve.memset(three_halves[:, :, :], 1.5).then_inc(made2, 1)
            dve.wait_ge(made2, 5)
            dve.memset(V[:, :, :, HD:HD + 1], 1.0).then_inc(made2, 1)
            dve.wait_ge(made2, 6)
            dve.wait_ge(weights, 16 * NW)
            dve.tensor_scalar(dec[:, 1, :], dec[:, 0, :], -44.0, None, ALU.max).then_inc(table_made, 1)
            dve.wait_ge(table_made, 3)
            dve.tensor_scalar(dec[:, 3, :], dec[:, 2, :], -1.0, None, ALU.mult).then_inc(table_made, 1)
            dve.tensor_scalar(ramp[:, 0:P], ramp[:, 0:P], 0.0, None, ALU.max).then_inc(table_made, 1)
            dve.wait_ge(table_made, 5)
            dve.tensor_tensor(expo[:, :, :], dec[:, 3, :].unsqueeze(1).to_broadcast([P, 4, H]),
                              widen(ramp[:, P:P + 4], H), ALU.mult).then_inc(table_made, 1)
            dve.wait_ge(table_made, 7 + H)
            dve.wait_ge(made, 10)

            def prep_step(u, i, tab):
                def x_tile(t):
                    return X[:, bass.ds(i * T + t, 1), :].rearrange("p a d -> p (a d)")

                if u == 0:
                    norm_measure(dve, c, norm, i, 0, x_tile)
                if u == TURNED_AT:
                    dve.wait_ge(*turn(turned, i, 0))
                    norm_scale(dve, c, norm, i, 0, lambda t: XN[:, t, :], x_tile)
                for z in range(2):
                    if u == QK_AT[z]:
                        dve.wait_ge(*turn(made_qk, i, z + 1))
                        dve.wait_ge(*turn(rest, i, 0))
                        dve.tensor_scalar(qk[:, z, :], bank(tab, ("qk", 1, z))[:, :], cols[:, z:z + 1],
                                          1.0 if z else float(HD) ** -0.5, ALU.add, ALU.mult).then_inc(sem(projected), 1)
                if u in SUMS:
                    z = SUMS.index(u)
                    dve.wait_ge(*turn(squared, i, z + 1))
                    dve.tensor_reduce(length[:, z, :].rearrange("p (t h) -> p t h", t=T),
                                      prod[:, 0, :, :].rearrange("p t (e h) -> p t h e", e=PAST),
                                      AX_X, ALU.add).then_inc(sem(summed), 1)
                    dve.wait_ge(*turn(summed, i, 2 * z + 1))
                    dve.tensor_scalar(length[:, z, :], length[:, z, :], 1e-24, None, ALU.max).then_inc(sem(summed), 1)
                if u == SUMS[1]:
                    dve.wait_ge(*turn(summed, i, 4))
                    dve.tensor_scalar(halved[:, :, :], length[:, :, :].bitcast(I32), 1, None, ALU.logical_shift_right
                                      ).then_inc(sem(root), 1)
                    dve.tensor_scalar(length[:, :, :], length[:, :, :], -0.5, None, ALU.mult).then_inc(sem(root), 1)
                    dve.wait_ge(*turn(root, i, 1))
                    dve.tensor_scalar(guess[:, :, :].bitcast(I32), halved[:, :, :], -1.0, float(0x5f3759df),
                                      ALU.mult, ALU.add).then_inc(sem(root), 1)
                if u == DECAY_AT:
                    dve.wait_ge(*turn(newton, i, 4 * NEWTON))
                    rn = guess[:, :, :].rearrange("p z (t h) -> p z t h", t=T)
                    dve.tensor_tensor(rn[:, 0], rn[:, 0], over(bias[:, :], 1, T), ALU.mult).then_inc(sem(root), 1)
                    dve.wait_ge(*turn(root, i, 4))
                    for z in range(2):
                        v = line[:, z, :, :].rearrange("p t (e h) -> p t e h", e=PAST)
                        dve.tensor_tensor(v, v, over(rn[:, z], 2, PAST), ALU.mult).then_inc(sem(unit), 1)
                    dve.wait_ge(*turn(unit, i, 2))
                    v = line[:, 0, :, :].rearrange("p t (e h) -> p t e h", e=PAST)
                    first = 0
                    for kt in range(T - 1):
                        n = T - 1 - kt
                        dve.tensor_tensor(LQ[:, first:first + n, :].rearrange("p t (e h) -> p t e h", e=PAST),
                                          v[:, kt + 1:T], over(DQ[:, 0:n, :], 2, PAST), ALU.mult).then_inc(sem(decayed), 1)
                        first += n
                    dve.tensor_tensor(LK[:, :, :].rearrange("p t (e h) -> p t e h", e=PAST),
                                      line[:, 1, :, :].rearrange("p t (e h) -> p t e h", e=PAST),
                                      over(over(DQ[:, 3, :], 1, PAST), 1, T), ALU.mult).then_inc(sem(decayed), 1)
                for n, (_, _, width) in enumerate(PIECES):
                    if u == LINE_AT[n]:
                        dve.wait_ge(*turn(lcast, i, 2 * n + 1))
                        dve.wait_ge(*turn(lthird, i, n - 1) if n >= 2 else turn(rest, i, 2 * n + 2))
                        dve.tensor_tensor(rem[0:LINES, n % 2, 0:width], bank(tab, ("line", 1, n))[0:LINES, 0:width],
                                          part[0:LINES, n % 2, 0, 0:width], ALU.subtract).then_inc(sem(lrest), 1)

            def values(i, tab):
                for n in range(2):
                    dve.wait_ge(*turn(valued, i, n + 1))
                    dve.wait_ge(*turn(pv, i, 0))
                    dve.tensor_tensor(V[:, 2 * n:2 * n + 2, :, 0:HD],
                                      bank(tab, ("v", 1, n))[:, 0:2 * D].rearrange("p (t h d) -> p t h d", t=2, d=HD),
                                      over(bv[:, :].rearrange("p (h d) -> p h d", d=HD), 1, 2), ALU.add
                                      ).then_inc(sem(vdone), 1)

            def tail_step(u, i, tab):
                xb = X[:, bass.ds(i * T, T), :]
                if u == 0:
                    dve.wait_ge(*turn(added, i, 0))
                    dve.tensor_tensor(XB[:, :, :], xb, over(bo[:, :], 1, T), ALU.add).then_inc(sem(biased), 1)
                if u == WO_AT:
                    dve.wait_ge(*turn(wo, i, 1))
                    dve.wait_ge(*turn(biased, i, 1))
                    dve.tensor_tensor(xb, bank(tab, ("wo", -1, 0))[:, :].rearrange("p (t d) -> p t d", d=D),
                                      XB[:, :, :], ALU.add).then_inc(sem(added), 1)

            def maxima(i, h, tab, batch):
                g = h // QUAD
                dve.wait_ge(*turn(logit, i, 4 * h + 1))
                dve.wait_ge(*turn(diag, i, h))
                dve.tensor_tensor(inc[:, :].rearrange("p (t k) -> p t k", k=P),
                                  bank(tab, ("inc", batch, h))[:, :].rearrange("p (t k) -> p t k", k=P),
                                  over(table_h(h), 1, T), ALU.mult).then_inc(sem(inc_decayed), 1)
                f = bank(tab, ("past31", batch, h))
                dve.wait_ge(*turn(logit, i, 4 * h + 3))
                dve.tensor_reduce(M[:, 3, h:h + 1], f[:, 0:3 * P], AX_X, ALU.max).then_inc(sem(maxed), 1)
                dve.tensor_reduce(M[:, 1, h:h + 1], f[:, 3 * P:4 * P], AX_X, ALU.max).then_inc(sem(maxed), 1)
                dve.wait_ge(*turn(logit, i, 4 * h + 4))
                dve.tensor_reduce(M[:, 2, h:h + 1], bank(tab, ("past2", batch, h))[:, 0:2 * P], AX_X, ALU.max
                                  ).then_inc(sem(maxed), 1)
                dve.wait_ge(*turn(inc_decayed, i, h + 1))
                dve.wait_ge(*turn(scored, i, UQ * (g - 1)))
                sd = SD[:, g % 2, h % QUAD, :, :]
                dve.tensor_tensor(sd, bank(tab, ("diag", batch, h))[:, :].rearrange("p (t k) -> p t k", k=P),
                                  inc[:, :].rearrange("p (t k) -> p t k", k=P), ALU.add).then_inc(sem(diag), 1)
                dve.wait_ge(*turn(diag, i, h + 1))
                dve.tensor_reduce(MD[:, :, h], sd, AX_X, ALU.max).then_inc(sem(maxed), 1)

            def table_h(h):
                return table_of_decays[:, h, :]

            def join(i, g):
                hs = slice(QUAD * g, QUAD * g + QUAD)
                dve.wait_ge(*turn(maxed, i, 4 * QUAD * (g + 1)))
                dve.tensor_tensor(MD[:, 1:T, hs], MD[:, 1:T, hs], M[:, 1:T, hs], ALU.max).then_inc(sem(mjoined), 1)
                dve.wait_ge(*turn(mhigh, i, 3 * g + 3))
                for at, q0, q1 in SPANS:
                    dve.scalar_tensor_tensor(ml[:, g % 2, at:at + q1 - q0], TB[0:QUAD, q0:q1], -1.0,
                                             mh[:, g % 2, at:at + q1 - q0], ALU.mult, ALU.subtract
                                             ).then_inc(sem(mlow), 1)

            for u in range(UNITS):
                prep_step(u, 0, opening)
            for h in range(QUAD):
                maxima(0, h, opening, 1)
            join(0, 0)
            values(0, opening)

            def run(i, tail, prep, tab):
                for u in range(UNITS):
                    g = u // UQ
                    if next_head(u, prep):
                        batch, h = next_head(u, prep)
                        maxima(i + batch, h, tab, batch)
                    if tail:
                        tail_step(u, i - 1, tab)
                    if prep:
                        prep_step(u, i + 1, tab)
                    if u % UQ < QUAD:
                        continue
                    if prep or g < NQ - 1:
                        join(i + (g + 1) // NQ, (g + 1) % NQ)
                    dve.wait_ge(*turn(pv, i, g + 1))
                    dve.wait_ge(*turn(pvturned, i, g))
                    dve.tensor_copy(pvs[:, :], PV[:, :]).then_inc(sem(pvcopied), 1)
                    dve.wait_ge(*turn(pvturned, i, g + 1))
                    heads = TB[:, :].rearrange("p (t j e) -> p t j e", t=T, e=32)
                    dve.reciprocal(rec[:, :, :], heads[:, :, :, HD]).then_inc(sem(inv), 1)
                    dve.wait_ge(*turn(inv, i, g + 1))
                    dve.wait_ge(*turn(at_turned, i, 0))
                    dve.tensor_tensor(AT[:, :, 32 * g:32 * g + 32].rearrange("p t (j e) -> p t j e", e=HD),
                                      heads[:, :, :, 0:HD], widen(rec[:, :, :], HD), ALU.mult).then_inc(sem(attn), 1)
                if prep:
                    values(i + 1, tab)

            turns(dve, run)
            for u in (0, WO_AT):
                tail_step(u, B - 1, closing)
            dve.wait_ge(*turn(added, B, 0))

        @block.tensor
        def _(pe):
            pe.wait_ge(weights, 16 * NW)
            pe.wait_ge(made, 10)
            pe.wait_ge(made2, 6)

            def front(tab, use, i):
                if tab[use][1]:
                    kind, batch, n = tab[use][1]
                    pe.wait_ge(*turn(readers[kind][0], i + batch, readers[kind][1](n)))
                return bank(tab, use)

            def prep_step(use, i, tab):
                kind, _, n = use
                b = i + 1
                if kind == "turned":
                    norm_wait(pe, norm, b, 0)
                    f = front(tab, use, i)
                    for t in range(T):
                        last = pe.transpose(f[:, t * P:(t + 1) * P], XN[:, t, :], ident[:, :])
                    last.then_inc(sem(turned), 1)
                elif kind == "qk":
                    if n == 0:
                        pe.wait_ge(*turn(xT, b, 1))
                    pe.matmul(front(tab, use, i)[:, :], WQ[:, n * D:(n + 1) * D], XT[:, 1:S + 1], start=True, stop=True
                              ).then_inc(sem(made_qk), 1)
                elif kind == "points":
                    t, f = n % T, front(tab, use, i)
                    if n < T:
                        pe.matmul(f[:, 0:4 * LINES], XT[:, 1 + t * P:1 + (t + 1) * P], WR[:, :], start=True, stop=True
                                  ).then_inc(sem(pointed), 1)
                    else:
                        pe.matmul(f[:, 0:2 * LINES], XT[:, t * P:(t + 1) * P], WW[:, 0, :], start=True, stop=True)
                        pe.matmul(f[:, 2 * LINES:4 * LINES], XT[:, 1 + t * P:1 + (t + 1) * P], WW[:, 1, :],
                                  start=True, stop=True).then_inc(sem(pointed), 1)
                else:
                    src, tiles = [(line[:, 0], range(T)), (line[:, 1], range(T)), (LK, range(T)), (LQ, range(T)),
                                  (LQ, range(T, 6))][n]
                    if n < 2:
                        pe.wait_ge(*turn(unit, b, 2))
                    else:
                        pe.wait_ge(*turn(decayed, b, 4))
                    f = front(tab, use, i)
                    for k, t in enumerate(tiles):
                        last = pe.transpose(f[0:LINES, k * P:(k + 1) * P], src[:, t, :], ident[:, :])
                    last.then_inc(sem(lined), 1)

            def prep_values(i, tab):
                for n in range(2):
                    f = front(tab, ("v", 1, n), i)
                    for t in range(2 * n, 2 * n + 2):
                        last = pe.matmul(f[:, (t % 2) * D:(t % 2 + 1) * D], XT[:, 1 + t * P:1 + (t + 1) * P],
                                         WQ[:, 2 * D:3 * D], start=True, stop=True)
                    last.then_inc(sem(valued), 1)

            def tail_step(use, i, tab):
                if use[0] == "at":
                    pe.wait_ge(*turn(attn, i - 1, NQ))
                    f = front(tab, use, i)
                    for t in range(T):
                        last = pe.transpose(f[:, t * P:(t + 1) * P], AT[:, t, :], ident[:, :])
                    last.then_inc(sem(at_turned), 1)
                else:
                    pe.wait_ge(*turn(attT, i - 1, 1))
                    f = front(tab, use, i)
                    for t in range(T):
                        last = pe.matmul(f[:, t * D:(t + 1) * D], ATT[:, t * P:(t + 1) * P], WO[:, :],
                                         start=True, stop=True)
                    last.then_inc(sem(wo), 1)

            def logits(i, tab, batch, h):
                if h % (2 * QUAD) == 0:
                    pe.wait_ge(*turn(stacked[h // QUAD // 2], i + batch, 16 * STACKS))
                f = front(tab, ("inc", batch, h), i)
                for t in range(T):
                    ts = slice(t * P, (t + 1) * P)
                    last = pe.matmul(f[:, ts], QI[:, h, ts], KI[:, h, ts], start=True, stop=True)
                last.then_inc(sem(logit), 1)
                f = front(tab, ("diag", batch, h), i)
                for t in range(T):
                    ts = slice(t * P, (t + 1) * P)
                    pe.matmul(f[:, ts], QS[0:STACK, h, ts], KS[0:STACK, h, ts], start=True, stop=False)
                    last = pe.matmul(f[:, ts], identb[:, :], mask[:, :], start=False, stop=True)
                last.then_inc(sem(logit), 1)
                f = front(tab, ("past31", batch, h), i)
                for kt in range(3):
                    at = [3 * P, S + P, S + 2 * P][kt]
                    pe.matmul(f[:, kt * P:(kt + 1) * P], QS[0:KR1, h, at:at + P], KS[0:KR1, h, kt * P:(kt + 1) * P],
                              start=True, stop=True)
                pe.matmul(f[:, 3 * P:4 * P], QS[0:KR1, h, P:2 * P], KS[0:KR1, h, 0:P], start=True, stop=True
                          ).then_inc(sem(logit), 1)
                f = front(tab, ("past2", batch, h), i)
                pe.matmul(f[:, 0:P], QS[0:KR1, h, 2 * P:3 * P], KS[0:KR1, h, 0:P], start=True, stop=True)
                pe.matmul(f[:, P:2 * P], QS[0:KR1, h, S:S + P], KS[0:KR1, h, P:2 * P], start=True, stop=True
                          ).then_inc(sem(logit), 1)

            def turn_max(i, g):
                pe.wait_ge(*turn(mjoined, i, g + 1))
                pe.wait_ge(*turn(attn, i, g - 1))
                for t in range(T):
                    last = pe.transpose(TB[0:QUAD, t * P:(t + 1) * P], MD[:, t, QUAD * g:QUAD * g + QUAD],
                                        ident[:, :])
                last.then_inc(sem(mturned), 1)

            def diagonal(out, g, j, t):
                pe.matmul(out, only[:, :], QS[0:KR1, QUAD * g + j, t * P:(t + 1) * P], start=True, stop=False)
                return pe.matmul(out, SD[:, g % 2, j, t, :], ident[:, :], start=False, stop=True)

            def scores(i, g, j):
                h = QUAD * g + j
                if j == 0:
                    pe.wait_ge(*turn(mstacked, i, 32 * (g + 1)))
                u = UQ * g + j
                pe.wait_ge(*turn(exped, i, u))
                if j < QUAD:
                    diagonal(ST[:, 0, 0:P], g, j, 0)
                    pe.matmul(ST[:, 0, P:S], KS[0:KR1, h, 0:P], QS[0:KR1, h, P:S], start=True, stop=True)
                    diagonal(ST[:, 1, 0:P], g, j, 1)
                    pe.matmul(ST[:, 1, P:3 * P], KS[0:KR1, h, P:2 * P], QS[0:KR1, h, S:S + 2 * P],
                              start=True, stop=True)
                    diagonal(ST[:, 1, 3 * P:4 * P], g, j, 3).then_inc(sem(scored), 1)
                else:
                    for k in range(QUAD):
                        h = QUAD * g + k
                        at = (k % 2) * 2 * P
                        diagonal(ST[:, k // 2, at:at + P], g, k, 2)
                        last = pe.matmul(ST[:, k // 2, at + P:at + 2 * P], KS[0:KR1, h, 2 * P:3 * P],
                                         QS[0:KR1, h, S + 2 * P:QC], start=True, stop=True)
                    last.then_inc(sem(scored), 1)

            def values(i, g):
                pe.wait_ge(*turn(exped, i, UQ * (g + 1)))
                if g == 0:
                    pe.wait_ge(*turn(vdone, i, 2))
                pe.wait_ge(*turn(pvcopied, i, g))
                def buf(j):
                    return PT[:, j, :, :]
                for kt in range(T):
                    for j in range(QUAD):
                        if kt == 0:
                            src = buf(j)[:, 0, :]
                        elif kt == 1:
                            src = buf(j)[:, 1, 0:3 * P]
                        elif kt == 2:
                            src = buf(QUAD)[:, j // 2, (j % 2) * 2 * P:(j % 2 + 1) * 2 * P]
                        else:
                            src = buf(j)[:, 1, 3 * P:4 * P]
                        last = pe.matmul(PV[32 * j:32 * j + 32, kt * P:S], V[:, kt, QUAD * g + j, :], src,
                                         start=(kt == 0), stop=(kt == T - 1), skip_group_check=True)
                last.then_inc(sem(pv), 1)

            def turn_values(i, g, more):
                pe.wait_ge(*turn(pvcopied, i, g + 1))
                pe.wait_ge(*turn(mlow, i, 3 * (g + 2 if more else NQ)))
                pe.wait_ge(*turn(attn, i, g))
                for t in range(T):
                    last = pe.transpose(TB[:, t * P:(t + 1) * P], pvs[:, t * P:(t + 1) * P], ident[:, :])
                last.then_inc(sem(pvturned), 1)

            for use in OPENING:
                if use[0] in ("turned", "qk", "points", "line"):
                    prep_step(use, -1, opening)
            for h in range(QUAD):
                logits(-1, opening, 1, h)
            turn_max(0, 0)
            prep_values(-1, opening)

            def run(i, tail, prep, tab):
                for u in range(UNITS):
                    g, j = u // UQ, u % UQ
                    if j:
                        scores(i, g, j)
                    if next_head(u, prep):
                        logits(i, tab, *next_head(u, prep))
                    if j == 0:
                        scores(i, g, j)
                    for use in extras(u, tail, prep):
                        (tail_step if use[1] < 0 else prep_step)(use, i, tab)
                    if j == QUAD:
                        more = prep or g < NQ - 1
                        if more:
                            turn_max(i + (g + 1) // NQ, (g + 1) % NQ)
                        values(i, g)
                        turn_values(i, g, more)
                if prep:
                    prep_values(i, tab)

            turns(pe, run)
            for use in CLOSING:
                tail_step(use, B, closing)


def experts(nc, ins, c, tag, E):
    first = tag == "L0"
    func = ACT.Relu if first else ACT.Gelu
    with ExitStack() as ctx:
        def sb(name, shape, dt=F32):
            return ctx.enter_context(nc.sbuf_tensor(f"{tag}_{name}", shape, dt))

        signals, flags = [], []

        def sig(name, per=1, start=1):
            signals.append((ctx.enter_context(nc.semaphore(f"{tag}_{name}")), per, start))
            return signals[-1]

        def flag(name):
            flags.append(ctx.enter_context(nc.semaphore(f"{tag}_{name}")))
            return flags[-1]

        NG = B * T
        TOK = NG * P
        CH = 2
        NT = CH * NG + E
        U = len(c[f"{tag}_gathered"])
        TURNS = NT // U
        HALF = 2
        PAIRS_OF_BATCHES = B // HALF
        HT = HALF * T
        assert NT % U == 0 and NT <= P

        X, XN, ident = c["X"], [c["XN"], c["YN"]], c["ident"]
        XT = [c["YT"], sb("XT", [P, S])]
        W1 = sb("W1", [P, E, F + FC])
        W2 = sb("W2", [P, E, FC, D])
        b2 = sb("b2", [P, E, D])
        wr = sb("wr", [P, E])
        br = sb("br", [P, E])
        mva = sb("mva", [P, NG, 2])
        root = sb("root", [P, 2, NG])
        consts = sb("consts", [P, 2, NG])
        desc = sb("desc", [P, NG, E])
        key = sb("key", [P, NG, E])
        ex = sb("ex", [P, NG, E])
        work = sb("work", [P, NG, E])
        eq = sb("eq", [P, NG, E])
        choice = sb("choice", [P, CH, NG, E])
        both = sb("both", [P, NG, E], BF16)
        load = sb("load", [P, E], BF16)
        red = sb("red", [P, 4, NG])
        gate = sb("gate", [P, CH, NG])
        tri = sb("tri", [P, P], BF16)
        ones = sb("ones", [P, P], BF16)
        zeros = sb("zeros", [P, 2 * NT], BF16)
        steps = sb("steps", [P, E, NG])
        full = sb("full", [P, E, NG])
        count = sb("count", [P, E])
        tiles = sb("tiles", [P, 3, E])
        start = sb("start", [P, E])
        place = sb("place", [P, CH, NG])
        place_i = sb("place_i", [P, 3, CH, NG], I32)
        row = sb("row", [P, CH, NG])
        tile_of = sb("tile_of", [P, CH, NG])
        base = sb("base", [P, 2, CH, NG])
        code = sb("code", [P, 2, CH, NG])
        numbers = sb("numbers", [P, P])
        is_row = sb("is_row", [P, HALF, CH, T, P], BF16)
        is_tile = sb("is_tile", [P, HALF, CH, T, 2 * NT], BF16)
        past = sb("past", [P, NT, E])
        owner = sb("owner", [P, 2, NT])
        owner_i = sb("owner_i", [P, NT], I32)
        spare = sb("spare", [P, NT])
        dest = sb("dest", [P, 2, NT])
        dest_i = sb("dest_i", [P, 2, NT], I32)
        source = sb("source", [P, NT])
        gi = sb("gi", [P, U], I32)
        si = sb("si", [P, U], I32)
        xg = sb("xg", [P, U, D])
        xT = sb("xT", [P, 2, P])
        W1s = sb("W1s", [P, 2, F + FC])
        hT = sb("hT", [P, 2, FC, P])
        ys = sb("ys", [P, U, D])
        MIX = 4
        got = sb("got", [P, MIX, CH, T, D])
        xn_d = nc.dram_tensor(f"{tag}_xn", [TOK, D], F32).ap()
        y_d = nc.dram_tensor(f"{tag}_y", [CH * TOK + NT * P, D], F32).ap()
        PS = [ctx.enter_context(nc.psum_tensor(f"{tag}_P{n}", [P, S], F32)) for n in range(8)]

        loads, wr_loaded, made = flag("loads"), flag("wr_loaded"), flag("made")
        stats, mean, kept = sig("stats", T), sig("mean", T), sig("kept")
        rooted = flag("rooted")
        out = sig("out", HT)
        turned, copied = sig("turned", HALF, HALF), sig("copied", HALF, HALF)
        logits, ready, collected = sig("logits", HALF, HALF), sig("ready", HALF), sig("collected", HALF, HALF)
        xn_stored = [sig(f"xn_stored{h}", 16) for h in range(HALF)]
        route, exps, ranked = flag("route"), flag("exps"), flag("ranked")
        CODES = CH * (1 + 2 * T)
        coded, told = sig("coded", HALF * CODES), sig("told", HALF, HALF)
        inverse = flag("inverse")
        def tile_sig(name, per=1):
            return sig(name, per * U, per * U)

        gi_set, si_set, go = tile_sig("gi_set"), tile_sig("si_set"), tile_sig("go")
        gathered = [(s, 16, 0) for s in c[f"{tag}_gathered"]]
        scattered = [(s, 16, 0) for s in c[f"{tag}_scattered"]]
        g_turned, g_copied, w1_set = tile_sig("g_turned"), tile_sig("g_copied"), tile_sig("w1_set")
        hidden, acted = tile_sig("hidden", 2), tile_sig("acted", FC)
        y, y_set = tile_sig("y"), tile_sig("y_set")
        y_loaded = [sig(f"y_loaded{h}", 16 * CH, 16 * CH) for h in range(MIX)]
        mixed1, mixed2 = sig("mixed1", MIX * T, MIX * T), sig("mixed2", MIX * T, MIX * T)
        SORTED = (6 if first else 2) + 5 + 1 + 5 + 2
        LOADS = 16 * (2 * 4 + 2 + (1 if first else 0))

        def ahead(i, u, k):
            return i + (u + k) // U, (u + k) % U

        def expert_of(eng, i, u):
            return eng.value_load(owner_i[0:1, bass.ds(i * U + u, 1)], min_val=0, max_val=E - 1)

        ctx.callback(clear, nc, [sem(s) for s in signals] + flags)
        block = ctx.enter_context(nc.Block())

        @block.sync
        def _(sp):
            sp.dma_start(wr[:, :], ins[f"{tag}_wr"]).then_inc(wr_loaded, 16)
            if first:
                sp.dma_start(br[:, :], ins["L0_br"].partition_broadcast(P)).then_inc(loads, 16)
            sp.dma_start(b2[:, :, :].rearrange("p e d -> p (e d)"),
                         ins[f"{tag}_b2"].rearrange("e d -> (e d)").partition_broadcast(P)).then_inc(loads, 16)
            sp.dma_start(W1[:, :, F:F + FC], ins[f"{tag}_b1"]).then_inc(loads, 16)
            for n in range(4):
                es = slice(n * E // 4, (n + 1) * E // 4)
                sp.dma_start(W1[:, es, 0:F], ins[f"{tag}_w1"][:, es, :]).then_inc(loads, 16)
                sp.dma_start(W2[:, es, :, :], ins[f"{tag}_w2"][:, es, :, :]).then_inc(loads, 16)
            rows = xn_d.rearrange("(n p) d -> p n d", p=P)
            with sp.Fori(0, PAIRS_OF_BATCHES) as i:
                for h in range(HALF):
                    sp.wait_ge(*turn(out, i, (h + 1) * T))
                    sp.dma_start(rows[:, bass.ds((i * HALF + h) * T, T), :], XN[h][:, :, :]
                                 ).then_inc(sem(xn_stored[h]), 16)
            for u in range(U):
                sp.wait_ge(*turn(scattered[u], TURNS, 0))
            results = y_d[0:CH * TOK].rearrange("(k n p) d -> p k n d", k=CH, p=P)
            with sp.Fori(0, B // MIX) as i:
                for h in range(MIX):
                    sp.wait_ge(*turn(mixed2, i, (h + 1) * T - MIX * T))
                    for k in range(CH):
                        sp.dma_start(got[:, h, k, :, :], results[:, k, bass.ds((i * MIX + h) * T, T), :]
                                     ).then_inc(sem(y_loaded[h]), 16)

        @block.gpsimd
        def _(pool):
            prime(pool, signals)
            exact = dict(allow_small_or_imprecise_dtypes=True)
            pool.iota(desc[:, :, :], pattern=[[0, NG], [-1, E]], base=E, channel_multiplier=0, **exact).then_inc(made, 1)
            pool.iota(steps[:, :, :], pattern=[[0, E], [P, NG]], base=0, channel_multiplier=0, **exact).then_inc(made, 1)
            pool.iota(base[:, 0, :, :], pattern=[[NG, CH], [1, NG]], base=-CH * NG, channel_multiplier=0, **exact
                      ).then_inc(made, 1)
            pool.iota(base[:, 1, :, :], pattern=[[0, CH], [0, NG]], base=0, channel_multiplier=1, **exact
                      ).then_inc(made, 1)
            pool.iota(numbers[:, :], pattern=[[1, P]], base=0, channel_multiplier=0, **exact).then_inc(made, 1)
            pool.iota(spare[:, :], pattern=[[P, NT]], base=CH * TOK, channel_multiplier=1, **exact).then_inc(made, 1)
            pool.memset(ones[:, :], 1.0).then_inc(made, 1)
            pool.memset(tri[:, :], 1.0).then_inc(made, 1)
            pool.memset(zeros[:, :], 0.0).then_inc(made, 1)
            pool.memset(consts[:, 0, :], EPS).then_inc(made, 1)
            pool.memset(consts[:, 1, :], -0.5).then_inc(made, 1)
            pool.wait_ge(made, 11)
            pool.affine_select(out=tri[:, :], in_=tri[:, :], compare_op=ALU.is_gt, fill=0.0,
                               base=0, pattern=[[1, P]], channel_multiplier=-1).then_inc(made, 1)
            pool.wait_ge(*turn(kept, B, 0))
            pool.tensor_tensor(root[:, 0, :], mva[:, :, 1], consts[:, 0, :], ALU.add).then_inc(rooted, 1)
            pool.wait_ge(rooted, 1)
            pool.tensor_tensor(root[:, 1, :], root[:, 0, :], consts[:, 1, :], ALU.pow).then_inc(rooted, 1)

            def gather(i, u):
                pool.wait_ge(*turn(gi_set, i, u + 1))
                pool.wait_ge(*turn(g_turned, i, u + 1 - U))
                pool.sem_inc(sem(go), 1)
                pool.indirect_dma_start(xg[:, u, :], None, xn_d, bass.IndirectOffsetOnAxis(gi[:, u:u + 1], 0)
                                        ).then_inc(sem(gathered[u]), 16)

            def scatter(i, u):
                pool.wait_ge(*turn(si_set, i, u + 1))
                pool.wait_ge(*turn(y_set, i, u + 1))
                pool.sem_inc(sem(go), 1)
                pool.indirect_dma_start(y_d, bass.IndirectOffsetOnAxis(si[:, u:u + 1], 0), ys[:, u, :], None
                                        ).then_inc(sem(scattered[u]), 16)

            for h in range(HALF):
                pool.wait_ge(*turn(xn_stored[h], PAIRS_OF_BATCHES, 0))
            for u in range(U):
                gather(0, u)
            with pool.Fori(0, TURNS - 1) as i:
                for u in range(U):
                    gather(i + 1, u)
                    scatter(i, u)
            for u in range(U):
                scatter(TURNS - 1, u)

        @block.scalar
        def _(act):

            def copy_tokens(i, h):
                act.wait_ge(*turn(turned, i, h + 1))
                act.wait_ge(*turn(logits, i, h + 1 - HALF))
                act.activation(XT[h][:, :], PS[h][:, :], ACT.Copy).then_inc(sem(copied), 1)

            def copy_logits(i, h):
                act.wait_ge(*turn(logits, i, h + 1))
                act.sem_inc(sem(ready), 1)
                act.activation(key[:, bass.ds((i * HALF + h) * T, T), :],
                               PS[2 + h][:, 0:T * E].rearrange("p (t e) -> p t e", e=E), ACT.Copy
                               ).then_inc(sem(collected), 1)

            copy_tokens(0, 0)
            with act.Fori(0, PAIRS_OF_BATCHES - 1) as i:
                copy_tokens(i, 1)
                copy_logits(i, 0)
                copy_tokens(i + 1, 0)
                copy_logits(i, 1)
            copy_tokens(PAIRS_OF_BATCHES - 1, 1)
            copy_logits(PAIRS_OF_BATCHES - 1, 0)
            copy_logits(PAIRS_OF_BATCHES - 1, 1)
            act.wait_ge(route, 3 if first else 2)
            act.activation(ex[:, :, :], work[:, :, :], ACT.Exp).then_inc(exps, 1)
            with act.Fori(0, TURNS) as i:
                for u in range(U):
                    act.wait_ge(*turn(y, i, u - 1))
                    for f in range(FC):
                        if f % 2 == 0:
                            act.wait_ge(*turn(hidden, i, 2 * u + f // 2 + 1))
                        act.activation(hT[:, u % 2, f, :], PS[2 + 2 * (u % 2) + f // 2][:, (f % 2) * P:(f % 2 + 1) * P],
                                       func, bias=W1s[:, u % 2, F + f:F + f + 1]).then_inc(sem(acted), 1)

        @block.vector
        def _(dve):
            with dve.Fori(0, B) as i:
                for t in range(T):
                    dve.bn_stats(c["stat"][:, t, :], X[:, bass.ds(i * T + t, 1), :].rearrange("p a d -> p (a d)")
                                 ).then_inc(sem(stats), 1)
                dve.wait_ge(*turn(stats, i, T))
                dve.memset(c["pad"][:, :], 0.0)
                for t in range(T):
                    dve.bn_aggr(c["mv"][:, t, :], c["stat"][:, t, :]).then_inc(sem(mean), 1)
                dve.wait_ge(*turn(mean, i, T))
                dve.tensor_scalar(mva[:, bass.ds(i * T, T), :], c["mv"][:, :, :], 1.0, None, ALU.mult
                                  ).then_inc(sem(kept), 1)
            dve.wait_ge(*turn(kept, B, 0))
            dve.wait_ge(rooted, 2)
            with dve.Fori(0, PAIRS_OF_BATCHES) as i:
                for h in range(HALF):
                    dve.wait_ge(*turn(xn_stored[h], i, 0))
                    dve.wait_ge(*turn(turned, i, h + 1 - HALF))
                    for t in range(T):
                        n = (i * HALF + h) * T + t
                        dve.tensor_scalar(XN[h][:, t, :], X[:, bass.ds(n, 1), :].rearrange("p a d -> p (a d)"),
                                          mva[:, bass.ds(n, 1), 0], root[:, 1, bass.ds(n, 1)],
                                          ALU.subtract, ALU.mult).then_inc(sem(out), 1)
            dve.wait_ge(*turn(collected, PAIRS_OF_BATCHES, 0))
            dve.wait_ge(loads, LOADS)
            dve.wait_ge(made, 12)
            done = [0]

            def step(ins_):
                done[0] += 1
                ins_.then_inc(route, 1)
                dve.wait_ge(route, done[0])

            def best(src, most, dst):
                step(dve.tensor_reduce(red[:, most, :], src, AX_X, ALU.max))
                step(dve.tensor_tensor(eq[:, :, :], src, widen(red[:, most, :], E), ALU.is_equal))
                step(dve.tensor_tensor(eq[:, :, :], eq[:, :, :], desc[:, :, :], ALU.mult))
                step(dve.tensor_reduce(red[:, 3, :], eq[:, :, :], AX_X, ALU.max))
                step(dve.tensor_tensor(dst, desc[:, :, :], widen(red[:, 3, :], E), ALU.is_equal))

            def total(dst, src):
                step(dve.tensor_reduce(dst, src, AX_X, ALU.add))

            if first:
                step(dve.tensor_tensor(key[:, :, :], key[:, :, :], over(br[:, :], 1, NG), ALU.add))
            step(dve.tensor_reduce(red[:, 0, :], key[:, :, :], AX_X, ALU.max))
            step(dve.tensor_tensor(work[:, :, :], key[:, :, :], widen(red[:, 0, :], E), ALU.subtract))
            dve.wait_ge(exps, 1)
            if first:
                total(red[:, 1, :], ex[:, :, :])
                step(dve.reciprocal(red[:, 2, :], red[:, 1, :]))
                step(dve.tensor_tensor(key[:, :, :], ex[:, :, :], widen(red[:, 2, :], E), ALU.mult))
            best(key[:, :, :], 0, choice[:, 0, :, :])
            step(dve.scalar_tensor_tensor(work[:, :, :], choice[:, 0, :, :], -3.0e38, key[:, :, :], ALU.mult, ALU.add))
            best(work[:, :, :], 1, choice[:, 1, :, :])
            step(dve.tensor_tensor(both[:, :, :], choice[:, 0, :, :], choice[:, 1, :, :], ALU.add))
            with nc.allow_low_precision("counts up to the number of tiles are exact"):
                total(load[:, :], both[:, :, :].rearrange("p n e -> p e n"))
            assert done[0] == SORTED, done
            prob = key if first else ex
            for k in range(CH):
                step(dve.tensor_tensor(eq[:, :, :], choice[:, k, :, :], prob[:, :, :], ALU.mult))
                total(gate[:, k, :], eq[:, :, :])
            if not first:
                step(dve.tensor_tensor(red[:, 1, :], gate[:, 0, :], gate[:, 1, :], ALU.add))
                step(dve.reciprocal(red[:, 2, :], red[:, 1, :]))
                step(dve.tensor_tensor(gate[:, :, :], gate[:, :, :], over(red[:, 2, :], 1, CH), ALU.mult))
            dve.wait_ge(ranked, 1)
            step(dve.tensor_copy(count[:, :], PS[7][:, 0:E]))
            step(dve.tensor_tensor(full[:, :, :], widen(count[:, :], NG), steps[:, :, :], ALU.is_gt))
            total(tiles[:, 0, :], full[:, :, :])
            src, s = 0, 1
            while s < E:
                dst = 2 if src == 1 else 1
                step(dve.tensor_copy(tiles[:, dst, 0:s], tiles[:, src, 0:s]))
                step(dve.tensor_tensor(tiles[:, dst, s:E], tiles[:, src, s:E], tiles[:, src, 0:E - s], ALU.add))
                src, s = dst, 2 * s
            step(dve.tensor_tensor(start[:, :], tiles[:, src, :], tiles[:, 0, :], ALU.subtract))
            step(dve.tensor_scalar(start[:, :], start[:, :], float(P), None, ALU.mult))
            dve.wait_ge(ranked, 2)
            step(dve.tensor_tensor(work[:, :, :], PS[6][:, 0:NG * E].rearrange("p (n e) -> p n e", e=E),
                                   over(start[:, :], 1, NG), ALU.add))
            for k in range(CH):
                step(dve.tensor_tensor(eq[:, :, :], choice[:, k, :, :], work[:, :, :], ALU.mult))
                total(place[:, k, :], eq[:, :, :])
            step(dve.tensor_copy(place_i[:, 0, :, :], place[:, :, :]))
            step(dve.tensor_scalar(place_i[:, 1, :, :], place_i[:, 0, :, :], P.bit_length() - 1, None,
                                   ALU.logical_shift_right))
            step(dve.tensor_scalar(place_i[:, 2, :, :], place_i[:, 0, :, :], P - 1, None, ALU.bitwise_and))
            step(dve.tensor_copy(tile_of[:, :, :], place_i[:, 1, :, :]))
            step(dve.tensor_copy(row[:, :, :], place_i[:, 2, :, :]))
            step(dve.tensor_tensor(code[:, 0, :, :], base[:, 0, :, :], tile_of[:, :, :], ALU.subtract))
            step(dve.tensor_tensor(code[:, 1, :, :], base[:, 1, :, :], row[:, :, :], ALU.subtract))
            step(dve.tensor_tensor(past[:, :, :], widen(numbers[:, 0:NT], E), over(tiles[:, src, :], 1, NT), ALU.is_ge))
            total(owner[:, 0, :], past[:, :, :])
            step(dve.tensor_scalar(owner[:, 1, :], owner[:, 0, :], float(E - 1), None, ALU.min))
            step(dve.tensor_copy(owner_i[:, :], owner[:, 1, :]))
            with dve.Fori(0, PAIRS_OF_BATCHES) as i:
                for h in range(HALF):
                    at = (i * HALF + h) * T
                    dve.wait_ge(*turn(told, i, h + 1 - HALF))
                    for k in range(CH):
                        dve.tensor_tensor(is_row[:, h, k, :, :], over(numbers[:, :], 1, T),
                                          widen(row[:, k, bass.ds(at, T)], P), ALU.is_equal).then_inc(sem(coded), 1)
                        for t in range(T):
                            for z in range(2):
                                dve.tensor_scalar(is_tile[:, h, k, t, z * NT:(z + 1) * NT], numbers[:, 0:NT],
                                                  tile_of[:, k, bass.ds(at + t, 1)], code[:, z, k, bass.ds(at + t, 1)],
                                                  ALU.is_equal, ALU.mult).then_inc(sem(coded), 1)
            dve.wait_ge(inverse, 1)
            step(dve.scalar_tensor_tensor(dest[:, 0, :], PS[5][:, 0:NT], float(P), spare[:, :], ALU.mult, ALU.add))
            step(dve.tensor_tensor(dest[:, 1, :], PS[5][:, NT:2 * NT], dest[:, 0, :], ALU.add))
            step(dve.tensor_copy(dest_i[:, 0, :], dest[:, 1, :]))
            step(dve.tensor_scalar(dest_i[:, 1, :], dest_i[:, 0, :], TOK - 1, None, ALU.bitwise_and))
            step(dve.tensor_copy(source[:, :], dest_i[:, 1, :]))

            def set_source(i, u, opening=False):
                if not opening:
                    dve.wait_ge(*turn(gathered[u], i, 0))
                dve.tensor_scalar(gi[:, u:u + 1], source[:, bass.ds(i * U + u, 1)], 1.0, None, ALU.mult
                                  ).then_inc(sem(gi_set), 1)

            def set_dest(i, u, opening):
                if not opening:
                    dve.wait_ge(*turn(scattered[u], i, 0))
                dve.tensor_scalar(si[:, u:u + 1], dest[:, 1, bass.ds(i * U + u, 1)], 1.0, None, ALU.mult
                                  ).then_inc(sem(si_set), 1)

            def set_weights(i, u, e):
                dve.wait_ge(*turn(acted, i, FC * (u - 1)))
                dve.tensor_scalar(W1s[:, u % 2, :], W1[:, bass.ds(e, 1), :].rearrange("p a f -> p (a f)"), 1.0, None,
                                  ALU.mult).then_inc(sem(w1_set), 1)

            def set_tokens(i, u):
                dve.wait_ge(*turn(g_turned, i, u + 1))
                dve.wait_ge(*turn(hidden, i, 2 * (u - 1)))
                dve.tensor_copy(xT[:, u % 2, :], PS[u % 2][:, 0:P]).then_inc(sem(g_copied), 1)

            def set_result(i, u, e):
                dve.wait_ge(*turn(y, i, u + 1))
                dve.tensor_tensor(ys[:, u, :], PS[6 + u % 2][:, 0:D], b2[:, bass.ds(e, 1), :].rearrange("p a d -> p (a d)"),
                                  ALU.add).then_inc(sem(y_set), 1)

            for u in range(U):
                set_source(0, u, True)
            for u in range(2):
                set_weights(0, u, expert_of(dve, 0, u))
                set_tokens(0, u)

            def tile(i, u, opening=False, last=False):
                e = expert_of(dve, i, u)
                if not last:
                    set_source(i + 1, u)
                if not last or u + 2 < U:
                    e2 = expert_of(dve, *ahead(i, u, 2))
                    set_tokens(*ahead(i, u, 2))
                    set_weights(*ahead(i, u, 2), e2)
                set_dest(i, u, opening)
                set_result(i, u, e)

            for u in range(U):
                tile(0, u, opening=True)
            with dve.Fori(1, TURNS - 1) as i:
                for u in range(U):
                    tile(i, u)
            for u in range(U):
                tile(TURNS - 1, u, last=True)
            with dve.Fori(0, B // MIX) as i:
                for h in range(MIX):
                    dve.wait_ge(*turn(y_loaded[h], i, 16 * CH))
                    for k, mixed in enumerate((mixed1, mixed2)):
                        if k:
                            dve.wait_ge(*turn(mixed1, i, (h + 1) * T))
                        for t in range(T):
                            n = (i * MIX + h) * T + t
                            xt = X[:, bass.ds(n, 1), :].rearrange("p a d -> p (a d)")
                            dve.scalar_tensor_tensor(xt, got[:, h, k, t, :], gate[:, k, bass.ds(n, 1)], xt,
                                                     ALU.mult, ALU.add).then_inc(sem(mixed), 1)
            dve.wait_ge(*turn(mixed2, B // MIX, 0))

        @block.tensor
        def _(pe):
            pe.wait_ge(wr_loaded, 16)

            def turn_batch(i, h):
                pe.wait_ge(*turn(out, i, (h + 1) * T))
                pe.wait_ge(*turn(copied, i, h + 1 - HALF))
                for t in range(T):
                    last = pe.transpose(PS[h][:, t * P:(t + 1) * P], XN[h][:, t, :], ident[:, :])
                last.then_inc(sem(turned), 1)

            def batch_logits(i, h):
                pe.wait_ge(*turn(copied, i, h + 1))
                pe.wait_ge(*turn(collected, i, h + 1 - HALF))
                for t in range(T):
                    last = pe.matmul(PS[2 + h][:, t * E:(t + 1) * E], XT[h][:, t * P:(t + 1) * P], wr[:, :],
                                     start=True, stop=True)
                last.then_inc(sem(logits), 1)

            turn_batch(0, 0)
            with pe.Fori(0, PAIRS_OF_BATCHES - 1) as i:
                turn_batch(i, 1)
                batch_logits(i, 0)
                turn_batch(i + 1, 0)
                batch_logits(i, 1)
            turn_batch(PAIRS_OF_BATCHES - 1, 1)
            batch_logits(PAIRS_OF_BATCHES - 1, 0)
            batch_logits(PAIRS_OF_BATCHES - 1, 1)
            pe.wait_ge(loads, LOADS)
            pe.wait_ge(made, 12)
            pe.wait_ge(route, SORTED)
            pe.matmul(PS[7][:, 0:E], ones[:, :], load[:, :], start=True, stop=True).then_inc(ranked, 1)
            flat = both[:, :, :].rearrange("p n e -> p (n e)")
            pe.matmul(PS[6][:, 0:NG * E], tri[:, :], flat, start=True, stop=False)
            for n in range(1, NG):
                last = pe.matmul(PS[6][:, n * E:NG * E], ones[:, :], flat[:, 0:(NG - n) * E],
                                 start=False, stop=(n == NG - 1))
            last.then_inc(ranked, 1)
            pe.matmul(PS[5][:, 0:2 * NT], ones[:, :], zeros[:, :], start=True, stop=False)
            with pe.Fori(0, PAIRS_OF_BATCHES) as i:
                for h in range(HALF):
                    pe.wait_ge(*turn(coded, i, (h + 1) * CODES))
                    for k in range(CH):
                        for t in range(T):
                            last = pe.matmul(PS[5][:, 0:2 * NT], is_row[:, h, k, t, :], is_tile[:, h, k, t, :],
                                             start=False, stop=False)
                    last.then_inc(sem(told), 1)
            pe.matmul(PS[5][:, 0:2 * NT], ones[:, :], zeros[:, :], start=False, stop=True).then_inc(inverse, 1)

            def turn_tokens(i, u):
                pe.wait_ge(*turn(gathered[u], i, 16))
                pe.wait_ge(*turn(g_copied, i, u - 1))
                pe.transpose(PS[u % 2][:, 0:P], xg[:, u, :], ident[:, :]).then_inc(sem(g_turned), 1)

            def first_product(i, u):
                pe.wait_ge(*turn(g_copied, i, u + 1))
                pe.wait_ge(*turn(w1_set, i, u + 1))
                pe.wait_ge(*turn(acted, i, FC * (u - 1)))
                for f in range(FC):
                    last = pe.matmul(PS[2 + 2 * (u % 2) + f // 2][:, (f % 2) * P:(f % 2 + 1) * P],
                                     W1s[:, u % 2, f * P:(f + 1) * P], xT[:, u % 2, :], start=True, stop=True)
                    if f % 2:
                        last.then_inc(sem(hidden), 1)

            def second_product(i, u, e):
                pe.wait_ge(*turn(acted, i, FC * (u + 1)))
                pe.wait_ge(*turn(y_set, i, u - 1))
                for f in range(FC):
                    last = pe.matmul(PS[6 + u % 2][:, 0:D], hT[:, u % 2, f, :],
                                     W2[:, bass.ds(e, 1), f, :].rearrange("p a d -> p (a d)"),
                                     start=(f == 0), stop=(f == FC - 1))
                last.then_inc(sem(y), 1)

            def tile(i, u, last):
                e = expert_of(pe, i, u)
                if not last or u + 1 < U:
                    first_product(*ahead(i, u, 1))
                if not last or u + 2 < U:
                    turn_tokens(*ahead(i, u, 2))
                second_product(i, u, e)

            pe.wait_ge(*turn(gi_set, 0, 1))
            turn_tokens(0, 0)
            turn_tokens(0, 1)
            first_product(0, 0)
            with pe.Fori(0, TURNS - 1) as i:
                for u in range(U):
                    tile(i, u, False)
            for u in range(U):
                tile(TURNS - 1, u, True)




_HEAD_ROWS_A = [2, 3, 1, 0, 2, 0]
_HEAD_ROWS_B = [3, 1, 2, 3, 0, 1]
_LINE_A = [0, 0, 0, 1, 1, 2]
_LINE_B = [1, 2, 3, 2, 3, 3]


def rotary():
    f = np.float32
    freq = f(1.0) / f(10000.0) ** (np.arange(0, HD, 2, dtype=f) / f(HD))
    angle = np.arange(S, dtype=f)[:, None] * freq[None, :]
    cos = np.tile(np.repeat(np.cos(angle), 2, axis=1), (1, H)).T
    sin = np.tile(np.repeat(np.sin(angle), 2, axis=1) * np.tile(f([-1, 1]), HD // 2), (1, H)).T
    scale = f(1.0) / np.sqrt(f(HD))
    turned = np.arange(D).reshape(H, HD).T.reshape(-1)
    return np.ascontiguousarray(np.stack([cos * scale, sin * scale, cos, sin])[:, turned].astype(f))


def lay_out(v):
    turned = np.arange(D).reshape(H, HD).T.reshape(-1)
    swap = turned ^ 1
    col = lambda a: np.asarray(a).reshape(-1, 1)
    g = {}
    g["x"] = np.asarray(v["L0_attn_x"]).reshape(B * S, D)
    g["Wv"], g["Wo"] = v["L0_attn_Wv"], v["L0_attn_Wo"]
    for n in "qk":
        g["W" + n] = np.asarray(v["L0_attn_W" + n])[:, turned]
        g[f"W{n}s"] = np.asarray(v["L0_attn_W" + n])[:, swap]
    bq, bk = np.asarray(v["L0_attn_bq"]), np.asarray(v["L0_attn_bk"])
    g["acols"] = np.concatenate([col(bq[turned]), col(bq[swap]), col(bk[turned]), col(bk[swap]), col(v["L0_attn_g1"]),
                                 col(v["L0_attn_beta1"]), col(v["L0_attn_g2"]), col(v["L0_attn_beta2"])], axis=1)
    g["bv"], g["bo"], g["ab2"] = v["L0_attn_bv"], v["L0_attn_bo"], v["L0_attn_b2"]
    g["aW1"], g["aW2"] = v["L0_attn_W1"], v["L0_attn_W2"]
    g["ab1"] = np.asarray(v["L0_attn_b1"]).reshape(FC, P).T
    g["rope"] = rotary()
    g["L0_w1"] = np.asarray(v["L0_ffn_W1"]).transpose(1, 0, 2)
    g["L0_w2"] = np.asarray(v["L0_ffn_W2"]).reshape(E0, FC, P, D).transpose(2, 0, 1, 3)
    g["L0_b1"] = np.asarray(v["L0_ffn_b1"]).reshape(E0, FC, P).transpose(2, 0, 1)
    g["L0_b2"], g["L0_wr"], g["L0_br"] = v["L0_ffn_b2"], v["L0_ffn_Wr"], v["L0_ffn_br"]
    g["L1_w1"] = np.asarray(v["L1_ffn_w1"]).transpose(2, 0, 1)
    g["L1_w2"] = np.asarray(v["L1_ffn_w2"]).transpose(0, 2, 1).reshape(E1, FC, P, D).transpose(2, 0, 1, 3)
    g["L1_b1"] = np.asarray(v["L1_ffn_b1"]).reshape(E1, FC, P).transpose(2, 0, 1)
    g["L1_b2"], g["L1_wr"] = v["L1_ffn_b2"], np.asarray(v["L1_ffn_router_w"]).T
    heads = np.arange(H)[None, :] * 4
    pick = lambda w, rows: np.asarray(w)[(heads + np.array(rows)[:, None]).reshape(-1), :].T
    order = np.concatenate([turned, D + turned, np.arange(2 * D, 3 * D)])
    g["c_qkv"] = np.asarray(v["L1_attn_w_qkv"])[order].T
    g["c_wo"] = np.asarray(v["L1_attn_w_out"]).T
    g["c_read"] = np.concatenate([pick(v["L1_attn_w1_read"], _LINE_A), pick(v["L1_attn_w2_read"], _LINE_B),
                                  pick(v["L1_attn_w1_read"], _LINE_B), pick(v["L1_attn_w2_read"], _LINE_A)], axis=1)
    g["c_write1"] = np.concatenate([pick(v["L1_attn_w1_write"], _HEAD_ROWS_A),
                                    pick(v["L1_attn_w1_write"], _HEAD_ROWS_B)], axis=1)
    g["c_write2"] = np.concatenate([pick(v["L1_attn_w2_write"], _HEAD_ROWS_B),
                                    pick(v["L1_attn_w2_write"], _HEAD_ROWS_A)], axis=1)
    bqkv = np.asarray(v["L1_attn_b_qkv"])
    g["c_cols"] = np.stack([bqkv[0:D][turned], bqkv[D:2 * D][turned]], axis=1)
    g["c_bv"], g["c_bo"] = bqkv[2 * D:3 * D], v["L1_attn_b_out"]
    g["c_decay"], g["c_bias"] = v["L1_attn_decay_logits"], v["L1_attn_bias_scale"]
    return {k: np.ascontiguousarray(a) for k, a in g.items()}


def kernel(**inputs):
    import numpy as _np
    import concourse.bacc as _bacc
    from concourse import mybir as _mybir
    from concourse.bass_utils import run_bass_kernel_spmd as _run

    nc = _bacc.Bacc("TRN2", target_bir_lowering=False, num_devices=1)
    laid = lay_out(inputs)
    ins = {n: nc.dram_tensor(f"in_{n}", a.shape, _mybir.dt.from_np(a.dtype), kind="ExternalInput").ap()
           for n, a in laid.items()}
    out = nc.dram_tensor("out_x", (B * S, D), F32, kind="ExternalOutput").ap()
    build(nc, ins, out)
    r = _run(nc, [{f"in_{n}": a for n, a in laid.items()}], core_ids=[0])
    return _np.asarray(r.results[0]["out_x"]).reshape(B, S, D)
```
